# Optimizing a Trainium2 kernel written in Bass

```python
import numpy as np
import jax
import jax.numpy as jnp

def _softmax(x, axis=-1):
    return jax.nn.softmax(x, axis=axis)

def _gelu(x):
    return jax.nn.gelu(x, approximate=True)

def _silu(x):
    return jax.nn.silu(x)

def _sigmoid(x):
    return jax.nn.sigmoid(x)

def _layernorm(x, axis=-1, eps=1e-05):
    m = jnp.mean(x, axis=axis, keepdims=True)
    v = jnp.var(x, axis=axis, keepdims=True)
    return (x - m) / jnp.sqrt(v + eps)

def _scatter_add(tgt, idx, src, axis=0):
    return tgt.at[idx].add(src)

def _segment_sum(src, seg, n):
    return jax.ops.segment_sum(src, seg, n)
kernel_name = 'mk_seq_postln_d1_jaxref_r8_731139'

def setup_inputs(seed: int=0):
    np.random.seed(seed)
    _w = jnp.asarray

    def _L0_attn_setup():
        import jax, jax.numpy as jnp
        import numpy as np
        N_LAYER = 12
        N_HEAD = 16
        N_EMBD = 128
        key = jax.random.key(seed)
        k0, k1, k2 = jax.random.split(key, 3)
        B, T, C = (4, 256, N_EMBD)
        inputs_embeds = jax.random.normal(k0, (B, T, C), dtype=jnp.float32)
        Wqkv = jax.random.normal(k1, (N_LAYER, 3 * C, C), dtype=jnp.float32) * 0.0002
        bqkv = jnp.zeros((N_LAYER, 3 * C), dtype=jnp.float32)
        Wproj = jax.random.normal(k2, (N_LAYER, C, C), dtype=jnp.float32) * 0.0002
        bproj = jnp.zeros((N_LAYER, C), dtype=jnp.float32)
        return {'inputs_embeds': inputs_embeds, 'Wqkv': Wqkv, 'bqkv': bqkv, 'Wproj': Wproj, 'bproj': bproj}
    _L0_attn_in = _L0_attn_setup()

    def _L0_ffn_setup():
        import jax, jax.numpy as jnp
        import numpy as np
        B, S, D, H, F, E = (2, 128, 128, 16, 256, 8)
        HD = D // H

        def _ln(x, g, b, eps=1e-05):
            m = x.mean(-1, keepdims=True)
            v = ((x - m) ** 2).mean(-1, keepdims=True)
            return (x - m) / jnp.sqrt(v + eps) * g + b
        key = jax.random.key(seed)
        ks = jax.random.split(key, 12)
        rn = lambda k, shp, s=0.02: jax.random.normal(k, shp, jnp.float32) * s
        return {'src': jax.random.normal(ks[0], (B, S, D), jnp.float32), 'q_w': rn(ks[1], (D, D)), 'k_w': rn(ks[2], (D, D)), 'v_w': rn(ks[3], (D, D)), 'out_w': rn(ks[4], (D, D)), 'gate_w': rn(ks[5], (D, D)), 'gate_b': rn(ks[6], (D,)), 'scale_w': rn(ks[7], (H, HD)), 'n1_g': jnp.ones((D,), jnp.float32), 'n1_b': jnp.zeros((D,), jnp.float32), 'n2_g': jnp.ones((D,), jnp.float32), 'n2_b': jnp.zeros((D,), jnp.float32), 'moe_gate_w': rn(ks[8], (D, E)), 'moe_gate_b': jnp.zeros((E,), jnp.float32), 'w1': rn(ks[9], (E, D, F)), 'b1': jnp.zeros((E, F), jnp.float32), 'ln_g': jnp.ones((E, F), jnp.float32), 'ln_b': jnp.zeros((E, F), jnp.float32), 'w2': rn(ks[10], (E, F, D)), 'b2': jnp.zeros((E, D), jnp.float32), 'res_scale': jnp.ones((E,), jnp.float32)}
    _L0_ffn_in = _L0_ffn_setup()
    _d = {'L0_attn_inputs_embeds': _L0_attn_in['inputs_embeds'], 'L0_attn_Wqkv': _L0_attn_in['Wqkv'], 'L0_attn_bqkv': _L0_attn_in['bqkv'], 'L0_attn_Wproj': _L0_attn_in['Wproj'], 'L0_attn_bproj': _L0_attn_in['bproj'], 'L0_ffn_q_w': _L0_ffn_in['q_w'], 'L0_ffn_k_w': _L0_ffn_in['k_w'], 'L0_ffn_v_w': _L0_ffn_in['v_w'], 'L0_ffn_out_w': _L0_ffn_in['out_w'], 'L0_ffn_gate_w': _L0_ffn_in['gate_w'], 'L0_ffn_gate_b': _L0_ffn_in['gate_b'], 'L0_ffn_scale_w': _L0_ffn_in['scale_w'], 'L0_ffn_n1_g': _L0_ffn_in['n1_g'], 'L0_ffn_n1_b': _L0_ffn_in['n1_b'], 'L0_ffn_n2_g': _L0_ffn_in['n2_g'], 'L0_ffn_n2_b': _L0_ffn_in['n2_b'], 'L0_ffn_moe_gate_w': _L0_ffn_in['moe_gate_w'], 'L0_ffn_moe_gate_b': _L0_ffn_in['moe_gate_b'], 'L0_ffn_w1': _L0_ffn_in['w1'], 'L0_ffn_b1': _L0_ffn_in['b1'], 'L0_ffn_ln_g': _L0_ffn_in['ln_g'], 'L0_ffn_ln_b': _L0_ffn_in['ln_b'], 'L0_ffn_w2': _L0_ffn_in['w2'], 'L0_ffn_b2': _L0_ffn_in['b2'], 'L0_ffn_res_scale': _L0_ffn_in['res_scale']}
    _x0 = _d['L0_attn_inputs_embeds']
    _d['L0_attn_inputs_embeds'] = jax.random.normal(jax.random.fold_in(jax.random.key(seed), 1), (8, 256, 128), dtype=_x0.dtype)
    del _x0
    return _d

def reference(L0_attn_inputs_embeds, L0_attn_Wqkv, L0_attn_bqkv, L0_attn_Wproj, L0_attn_bproj, L0_ffn_q_w, L0_ffn_k_w, L0_ffn_v_w, L0_ffn_out_w, L0_ffn_gate_w, L0_ffn_gate_b, L0_ffn_scale_w, L0_ffn_n1_g, L0_ffn_n1_b, L0_ffn_n2_g, L0_ffn_n2_b, L0_ffn_moe_gate_w, L0_ffn_moe_gate_b, L0_ffn_w1, L0_ffn_b1, L0_ffn_ln_g, L0_ffn_ln_b, L0_ffn_w2, L0_ffn_b2, L0_ffn_res_scale):

    def _L0_attn_ref(inputs_embeds, Wqkv, bqkv, Wproj, bproj):
        import jax, jax.numpy as jnp
        import numpy as np
        N_LAYER = 12
        N_HEAD = 16
        N_EMBD = 128
        B, T, C = inputs_embeds.shape
        H = N_HEAD
        D = C // H
        scale = 1.0 / np.sqrt(D).astype(np.float32)
        x = inputs_embeds
        for i in range(N_LAYER):
            qkv = x @ Wqkv[i].T + bqkv[i]
            q, k, v = jnp.split(qkv, 3, axis=-1)
            q = q.reshape(B, T, H, D).transpose(0, 2, 1, 3)
            k = k.reshape(B, T, H, D).transpose(0, 2, 1, 3)
            v = v.reshape(B, T, H, D).transpose(0, 2, 1, 3)
            att = jnp.einsum('bhqd,bhkd->bhqk', q, k) * scale
            y = jnp.einsum('bhqk,bhkd->bhqd', att, v)
            y = y.transpose(0, 2, 1, 3).reshape(B, T, C)
            x = y @ Wproj[i].T + bproj[i] + x
        return x

    def _L0_ffn_ref(src, q_w, k_w, v_w, out_w, gate_w, gate_b, scale_w, n1_g, n1_b, n2_g, n2_b, moe_gate_w, moe_gate_b, w1, b1, ln_g, ln_b, w2, b2, res_scale):
        import jax, jax.numpy as jnp
        import numpy as np
        B, S, D, H, F, E = (2, 128, 128, 16, 256, 8)
        HD = D // H

        def _ln(x, g, b, eps=1e-05):
            m = x.mean(-1, keepdims=True)
            v = ((x - m) ** 2).mean(-1, keepdims=True)
            return (x - m) / jnp.sqrt(v + eps) * g + b
        b, s, d = src.shape
        h = scale_w.shape[0]
        hd = d // h
        q = (src @ q_w).reshape(b, s, h, hd).transpose(0, 2, 1, 3)
        k = (src @ k_w).reshape(b, s, h, hd).transpose(0, 2, 1, 3)
        v = (src @ v_w).reshape(b, s, h, hd).transpose(0, 2, 1, 3)
        scores = jnp.einsum('bhqd,bhkd->bhqk', q, k) / np.float32(np.sqrt(hd))
        scale = jax.nn.sigmoid(jnp.einsum('bhsd,hd->bhs', q, scale_w)) * 2.0
        scores = scores * scale[..., None]
        aw = jax.nn.softmax(scores, axis=-1)
        out = jnp.einsum('bhqk,bhkd->bhqd', aw, v).transpose(0, 2, 1, 3).reshape(b, s, d)
        gate = jax.nn.sigmoid(out @ gate_w + gate_b)
        attn = out * gate @ out_w
        x = _ln(src + attn, n1_g, n1_b)
        xr = x.reshape(-1, d)
        n = xr.shape[0]
        logits = xr @ moe_gate_w + moe_gate_b
        top_v, top_i = jax.lax.top_k(logits, 2)
        wts = jax.nn.softmax(top_v, axis=-1)
        chosen = jnp.max(top_i, axis=-1)

        def expert(W1, B1, G, Bt, W2, B2, rsc):
            hh = xr @ W1 + B1
            hh = jax.nn.gelu(_ln(hh, G, Bt), approximate=False)
            return (hh @ W2 + B2) * rsc + xr
        outs = jax.vmap(expert)(w1, b1, ln_g, ln_b, w2, b2, res_scale)
        sel = jnp.take_along_axis(outs.transpose(1, 0, 2), chosen[:, None, None], axis=1)[:, 0]
        moe = sel * jnp.sum(wts, axis=-1, keepdims=True)
        return _ln(x + moe.reshape(b, s, d), n2_g, n2_b)
    x = L0_attn_inputs_embeds
    x = _layernorm(x + _L0_attn_ref(x, L0_attn_Wqkv, L0_attn_bqkv, L0_attn_Wproj, L0_attn_bproj), axis=-1)
    x = _layernorm(x + _L0_ffn_ref(x, L0_ffn_q_w, L0_ffn_k_w, L0_ffn_v_w, L0_ffn_out_w, L0_ffn_gate_w, L0_ffn_gate_b, L0_ffn_scale_w, L0_ffn_n1_g, L0_ffn_n1_b, L0_ffn_n2_g, L0_ffn_n2_b, L0_ffn_moe_gate_w, L0_ffn_moe_gate_b, L0_ffn_w1, L0_ffn_b1, L0_ffn_ln_g, L0_ffn_ln_b, L0_ffn_w2, L0_ffn_b2, L0_ffn_res_scale), axis=-1)
    return x

_drawn_inputs = setup_inputs


def setup_inputs(seed=0):
    import zlib

    import numpy as np

    out = dict(_drawn_inputs(seed))
    spreads = {'L0_attn_bqkv': (0.0, 0.8),
     'L0_attn_bproj': (0.0, 0.1),
     'L0_ffn_n1_g': (1.0, 0.2),
     'L0_ffn_n1_b': (0.0, 0.1),
     'L0_ffn_n2_g': (1.0, 0.2),
     'L0_ffn_n2_b': (0.0, 0.1),
     'L0_ffn_moe_gate_b': (0.0, 0.1),
     'L0_ffn_b1': (0.0, 0.272),
     'L0_ffn_ln_g': (1.0, 0.6),
     'L0_ffn_ln_b': (0.0, 0.8),
     'L0_ffn_b2': (0.0, 0.1),
     'L0_ffn_res_scale': (1.0, 0.6)}
    factors = {'L0_attn_Wqkv': 8.0,
     'L0_attn_Wproj': 8.0,
     'L0_ffn_q_w': 8.0,
     'L0_ffn_k_w': 8.0,
     'L0_ffn_v_w': 8.0,
     'L0_ffn_out_w': 8.0,
     'L0_ffn_gate_w': 8.0,
     'L0_ffn_gate_b': 8.0,
     'L0_ffn_scale_w': 31.172}
    for name, (base, spread) in spreads.items():
        noise = np.random.default_rng([zlib.crc32(name.encode()), seed]).standard_normal(out[name].shape)
        drawn = base * np.exp(spread * noise) if base else spread * noise
        out[name] = jnp.asarray(drawn.astype(out[name].dtype))
    for name, factor in factors.items():
        out[name] = (out[name] * factor).astype(out[name].dtype)
    return out
```

```python
import numpy as np
import concourse.bass as bass
from concourse import mybir
from concourse.alu_op_type import AluOpType as ALU
from contextlib import ExitStack

fp32 = mybir.dt.float32
bf16 = mybir.dt.bfloat16
u32 = mybir.dt.uint32
ACT = mybir.ActivationFunctionType
AX = mybir.AxisListType

P = 128
B, T, C = 8, 256, 128
TT = T // P
NT = B * TT
L = 12
H = 16
HD = C // H
E, F = 8, 256
FC = F // P
GB = 4
Q4 = 4
QW = P // Q4
EPS = 1e-5
SCALE = float(np.float32(1.0) / np.sqrt(np.float32(HD)))

NSLOT = 3

CBQ, CBP, CKT, CVT, CQT, CPT, CQN = 0, 1, 2, 2 + C, 2 + 2 * C, 2 + 3 * C, 2 + 4 * C
CQB = CQN + C
WCOLS = CQB
BQ = C + B


def build(nc, x_d, lw_d, lb_d, fw, consts, out_d):
    ctx = ExitStack()
    with ctx:
        def sb(name, shape, dt=fp32):
            return ctx.enter_context(nc.sbuf_tensor(name, shape, dt))

        def sem(name):
            return ctx.enter_context(nc.semaphore(name))

        X = sb("X", [P, B, TT, C])
        XT = sb("XT", [P, B, T])
        IR = sb("IR", [P, B, C])
        BR = sb("BR", [B, 2, 2 * C])
        KV = sb("KV", [P, 2 * C])
        MEAN = sb("MEAN", [P, B])
        MEAN0 = sb("MEAN0", [P, B])
        MSUM = sb("MSUM", [P, B])
        IDN = sb("IDN", [P, P])
        MASK = sb("MASK", [P, Q4, QW])
        DIAG = sb("DIAG", [B, B])
        AVG = sb("AVG", [P, P])

        arena = sb("ARENA", [P, 10752])
        at = [0]

        def piece(n, *dims):
            v = arena[:, at[0]:at[0] + n]
            at[0] += n
            names = "abcd"[:len(dims)]
            return v.rearrange(f"p ({' '.join(names)}) -> p {' '.join(names)}", **dict(zip(names, dims)))

        G = piece(B * C, B, C)
        RT = piece(B * C, B, C)
        IA = piece(2 * B * C, 2, B, C)
        U = piece(B * C, B, C)
        GV = piece(B * C, B, C)
        MF = piece(B * C, B, C)
        BT = piece(B * BQ, B, BQ)
        V8 = piece(B * C, B, C)
        WL = piece(2 * (WCOLS + B), 2, WCOLS + B)

        at[0] = 0
        HT = piece(NT * P, NT, P)
        QF = piece(NT * P, NT, P)
        QP = piece(3 * NT * P // 2, 3 * NT * P // 2).bitcast(bf16).rearrange("p (s t) -> p s t", s=3)
        KP = piece(3 * NT * P // 2, 3 * NT * P // 2).bitcast(bf16).rearrange("p (s t) -> p s t", s=3)
        KF = HT
        ON = HT
        OTS = sb("OTS", [P, 3, Q4, T])
        VT = sb("VT", [P, NT + TT, H, HD])
        VS = sb("VS", [P, NSLOT, TT, H, QW])
        PT = sb("PT", [P, 4, 2, T])
        STK = sb("STK", [P, 2, NSLOT, H, T], bf16)
        QS, KS = STK[:, 0], STK[:, 1]
        TH = sb("TH", [P, NT, P])
        X2 = sb("X2", [P, NT, C])
        NM = sb("NM", [P, NSLOT, H, TT])
        SHF = sb("SHF", [TT * H // 2, 2, P])
        SH = sb("SH", [TT * H // 2, 2, 3, P], bf16)
        RC = sb("RC", [P, 2, H])
        QW_ = {n: sb(n, [P, C]) for n in ("qw", "kw", "vw", "ow", "gw")}
        SWB = sb("SWB", [P, P])
        SWC = sb("SWC", [P, 1])
        GBH = sb("GBH", [P, 2])
        EM = sb("EM", [P, P])
        ROWS = sb("ROWS", [P, 4, C])
        MG = sb("MG", [P, E])
        ER = sb("ER", [P, 3, E])
        NH = sb("NH", [P, NT])
        ST = sb("ST", [P, NT, 6])
        MV = sb("MV", [P, NT, 2])
        VE = sb("VE", [P, NT])
        RS = sb("RS", [P, NT])

        OT = QF
        late = STK[:].rearrange("p a b c d -> p (a b c d)").bitcast(fp32)
        HN = late[:, 0:2048].rearrange("p (u k f) -> p u k f", u=2, k=4)
        GT = late[:, 2048:4096].rearrange("p (u c t) -> p u c t", u=2, c=FC)
        ACC = late[:, 4096:6144].rearrange("p (n c) -> p n c", n=NT)
        X2T = late[:, 6144:8192]
        W1 = sb("W1", [P, E, F])
        W2 = sb("W2", [P, E, FC, C])
        LNW = sb("LNW", [P, 2, FC, E])
        B1F = TH[0:3].rearrange("p n c -> p (n c)")
        B2F = X2[0:3, 0:E].rearrange("p n c -> p (n c)")
        B1P = sb("B1P", [P, E * F], bf16)
        B2P = sb("B2P", [P, E * C], bf16)
        ONE3 = sb("ONE3", [P, P], bf16)
        ALF = sb("ALF", [3, 2])
        ST2 = sb("ST2", [P, 2, 4, 6])
        MV2 = sb("MV2", [P, 2, 4, 2])
        VE2 = sb("VE2", [P, 2, 4])
        NG2 = sb("NG2", [P, 2, 4])
        RS2 = sb("RS2", [P, 2, 4])
        NB2 = sb("NB2", [P, 2, 4])
        MK = sb("MK", [P, NT])
        RT8 = [sb(f"RT8_{n}", [P, NT, E]) for n in range(3)]
        OH = sb("OH", [P, NT, E])
        R1 = [sb(f"R1_{n}", [P, NT]) for n in range(6)]
        RSC = sb("RSC", [P, NT])
        WS = sb("WS", [P, NT])
        PS = ctx.enter_context(nc.psum_tensor("PS", [P, 8, 512], fp32))
        scr = nc.dram_tensor("parts", (2, H, 3, HD, (NT + TT) * P), bf16).ap()
        scm = nc.dram_tensor("shifts", (NSLOT, 3, H, T), bf16).ap()

        def bank(g, k):
            return PS[:, 4 * g + k, :]

        def batches(ap):
            return ap.rearrange("p (b c) -> p b c", b=GB)

        s_const = sem("const_loaded")
        s_x = sem("x_loaded")
        s_w = [sem(f"layer_weights_loaded_{u}") for u in range(2)]
        s_zero = sem("pool_constants_set")
        s_mrow = sem("mean_rows_summed")
        s_mcol = sem("mean_columns_summed")
        s_xc = sem("x_centred")
        s_gram = sem("gram_summed")
        s_xct = sem("centred_x_transposed")
        s_xt = sem("centred_xT_copied")
        s_g = sem("gram_ready")
        s_mean = sem("mean_ready")
        s_p = sem("gv_done")
        s_pc = sem("gv_copied")
        s_row = sem("mean_keys_values_done")
        s_kv = sem("mean_keys_values_copied")
        s_v8 = sem("mean_values_spread")
        s_qbd = sem("mean_queries_done")
        s_qb = sem("mean_queries_ready")
        s_k = sem("ktv_done")
        s_m = sem("ktv_masked")
        s_r = sem("rt_done")
        s_rt = sem("rt_ready")
        s_b = sem("bt_done")
        s_bt = sem("bt_copied")
        s_a = sem("a_done")
        s_ia = sem("ia_ready")
        s_ym = sem("mean_update_done")
        s_u = sem("u_done")
        s_uc = sem("u_copied")
        s_gd = sem("gram_done")
        s_out = sem("out_stored")

        s_wf = sem("ffn_weights_loaded")
        s_stk0 = sem("stack_constants_set")
        s_ir = sem("i_plus_r_ready")
        s_ms = sem("mean_sum_ready")
        s_h = sem("residual_done")
        s_htv, s_hta = sem("residual_copied_by_dve"), sem("residual_copied_by_act")
        s_tok = sem("residual_transposed")
        s_st = sem("statistics_taken")
        s_mv = sem("mean_variance_ready")
        s_ve = sem("variance_plus_eps_ready")
        s_rs = sem("rstd_ready")
        s_x1 = sem("x1_ready")
        s_x1t = sem("x1_transposed")
        s_xtc = sem("x1t_copied")
        s_q = sem("queries_done")
        s_qf = sem("queries_copied")
        s_kd = sem("keys_done")
        s_kf = sem("keys_scaled")
        s_z = sem("query_scale_done")
        s_th = sem("query_scale_tanh")
        s_v = sem("values_done")
        s_vt = sem("values_copied")
        s_qs = sem("queries_scaled")
        s_swb = sem("scale_weights_spread")
        s_q1, s_q1r, s_q2, s_q3 = (sem(f"query_{n}") for n in ("part_1", "rest_1", "part_2", "part_3"))
        s_k1, s_k1r, s_k2, s_k3 = (sem(f"key_{n}") for n in ("part_1", "rest_1", "part_2", "part_3"))
        s_scr = sem("parts_stored")
        s_stk = [sem(f"stack_loaded_{u}") for u in range(NSLOT)]
        s_mxd = sem("max_scores_done")
        s_max = sem("maxima_taken")
        s_mt = sem("maxima_transposed")
        s_sha = sem("shift_part_1")
        s_shb = sem("shift_rest_1")
        s_shc = sem("shift_part_2")
        s_shd = sem("shift_part_3")
        s_shs = [sem(f"shifts_stored_{u}") for u in range(2)]
        s_shl = [sem(f"shifts_loaded_{u}") for u in range(2)]
        s_qk = sem("scores_done")
        s_exp = sem("exponentials_ready")
        s_vs = sem("batch_values_ready")
        s_pv = sem("pv_done")
        s_ot = sem("outputs_copied")
        s_tr = sem("outputs_transposed")
        s_rc = sem("sums_inverted")
        s_on = sem("outputs_normalised")
        s_we = sem("expert_weights_loaded")
        s_eb = sem("expert_bias_parts_ready")
        s_ebp = sem("b2_parts_ready")
        s_gbh = sem("half_gate_bias_ready")
        s_ott = sem("normalised_outputs_transposed")
        s_otc = sem("transposed_outputs_copied")
        s_gt = sem("gate_done")
        s_tg = sem("gate_tanh")
        s_og = sem("gated_outputs_ready")
        s_at = sem("out_projection_done")
        s_xp = sem("attention_residual_ready")
        s_xn = sem("x2_normalised")
        s_xg = sem("x2_scaled")
        s_x2 = sem("x2_ready")
        s_x2t = sem("x2_transposed")
        s_x2c = sem("x2t_copied")
        s_lg = sem("logits_done")
        s_rch = sem("routing_steps")
        s_ed = sem("second_weight_exponential")
        s_oh = sem("routing_ready")
        s_acc = sem("expert_output_cleared")
        s_h1 = sem("hidden_done")
        s_st2 = sem("hidden_statistics_taken")
        s_mv2 = sem("hidden_mean_variance")
        s_ve2 = sem("hidden_variance_plus_eps")
        s_rs2a = sem("hidden_rstd")
        s_rs2 = sem("hidden_rstd_and_shift")
        s_nrm = sem("hidden_normalised")
        s_td = sem("hidden_transposed")
        s_gl = sem("gelu_ready")
        s_y = sem("expert_output_done")
        s_sel = sem("expert_output_selected")
        s_mk = sem("expert_mask_ready")
        s_xb = sem("x1_plus_bias_ready")
        s_f1, s_f2, s_f3, s_f4, s_f5 = (sem(f"final_{n}") for n in ("scaled", "weighted", "normalised", "gained", "summed"))
        s_fo = sem("output_rows_ready")
        block = ctx.enter_context(nc.Block())

        def alone(engine, semaphore, value):
            engine.wait_ge(semaphore, value)
            engine.nop(nofuse=True)

        XN = X[:].rearrange("p b t c -> p (b t) c")
        cols = lambda i: slice(4 * P * i, 4 * P * (i + 1))
        flat = lambda ap: ap.rearrange("p a c -> p (a c)")
        XTF = XT[:].rearrange("p b t -> p (b t)")
        SROW = 3 * QW
        KEXP, KMAX = SROW + 3, 2 * QW + HD

        @block.sync
        def _(sp):
            sp.dma_start(AVG[:], consts["avg"]).then_inc(s_const, 16)
            for i in range(4):
                sp.dma_start(X[:, 2 * i:2 * i + 2], x_d[2 * i:2 * i + 2].rearrange("b (p t) c -> p b t c", t=TT)).then_inc(s_x, 16)
            sp.dma_start(IDN[:], consts["ident"]).then_inc(s_const, 16)
            sp.dma_start(MASK[:], consts["mask"]).then_inc(s_const, 16)
            sp.dma_start(DIAG[:], consts["diag"]).then_inc(s_const, 16)
            sp.dma_start(B1F, fw["b1"].broadcast_to([3, E * F])).then_inc(s_eb, 16)
            sp.dma_start(ALF[:], consts["alf"]).then_inc(s_eb, 16)
            sp.dma_start(B2F, fw["b2"].broadcast_to([3, E * C])).then_inc(s_ebp, 16)
            for u in range(2):
                sp.dma_start(WL[:, u, 0:WCOLS], lw_d[u]).then_inc(s_w[u], 16)
                sp.dma_start(BR[:, u, :], lb_d[u:u + 1, :].broadcast_to([B, 2 * C])).then_inc(s_w[u], 16)
            with sp.Fori(0, L // 2 - 1) as i:
                for u in range(2):
                    sp.wait_ge(s_mean, 2 * i + u + 2)
                    sp.dma_start(WL[:, u, 0:WCOLS], lw_d[bass.ds(2 * i + u + 2, 1)].rearrange("l p c -> p (l c)")).then_inc(s_w[u], 16)
                    sp.dma_start(BR[:, u, :], lb_d[bass.ds(2 * i + u + 2, 1), :].broadcast_to([B, 2 * C])).then_inc(s_w[u], 16)
            for n, w in QW_.items():
                sp.dma_start(w[:], fw[n]).then_inc(s_wf, 16)
            sp.dma_start(SWC[:], fw["swc"]).then_inc(s_wf, 16)
            sp.dma_start(EM[:], consts["em"]).then_inc(s_wf, 16)
            sp.dma_start(GBH[:, 0:1], fw["gb"]).then_inc(s_we, 16)
            sp.dma_start(ROWS[:], fw["rows"].broadcast_to([P, 4 * C]).rearrange("p (r c) -> p r c", r=4)).then_inc(s_we, 16)
            sp.dma_start(ER[:], fw["er"].broadcast_to([P, 3 * E]).rearrange("p (r c) -> p r c", r=3)).then_inc(s_we, 16)
            sp.dma_start(MG[:], fw["mg"]).then_inc(s_we, 16)
            sp.dma_start(W1[:], fw["w1"]).then_inc(s_we, 16)
            sp.dma_start(W2[:], fw["w2"]).then_inc(s_we, 16)
            sp.dma_start(LNW[:], fw["lnw"]).then_inc(s_we, 16)
            for i in range(4):
                sp.wait_ge(s_q3, i + 1)
                sp.wait_ge(s_k3, i + 1)
                for n, part in enumerate((QP, KP)):
                    for s in range(3):
                        sp.dma_start(scr[n, :, s, :, cols(i)], part[:, s, cols(i)]).then_inc(s_scr, 16)
            for n, part in enumerate((QP, KP)):
                for s in range(3):
                    sp.dma_start(scr[n, :, s, :, B * T:], part[:, s, (B - 1) * T:]).then_inc(s_scr, 16)

            def load_stack(n, slot):
                tok = bass.ds(n * T, T)
                q = scr[0, :, :, :, tok].rearrange("h s d t -> s d h t")
                k = scr[1, :, :, :, tok].rearrange("h s d t -> (s d) h t")
                row = 0
                for part, times in ((0, 3), (1, 2), (2, 1)):
                    for _ in range(times):
                        sp.dma_start(QS[HD * row:HD * (row + 1), slot], q[part]).then_inc(s_stk[slot], 16)
                        row += 1
                row = 0
                for parts in (3, 2, 1):
                    sp.dma_start(KS[HD * row:HD * (row + parts), slot], k[0:HD * parts]).then_inc(s_stk[slot], 16)
                    row += parts

            def load_shift(n, slot, half):
                heads = slice(half * H // 2, (half + 1) * H // 2)
                sp.wait_ge(s_shd, 2 * n + half + 1)
                sp.dma_start(scm[slot, :, heads, :].rearrange("s h (q t) -> (h q) s t", q=TT), SH[:, half]).then_inc(s_shs[half], 16)
                sp.wait_ge(s_shs[half], 16 * (n + 1))
                sp.dma_start(QS[SROW:SROW + 3, slot, heads, :], scm[slot, :, heads, :]).then_inc(s_shl[half], 16)

            sp.wait_ge(s_scr, 16 * 30)
            sp.wait_ge(s_stk0, 3)
            for n in range(NSLOT):
                load_stack(n, n)
            for half in range(2):
                load_shift(0, 0, half)

            def sp_step(i, c, last):
                b = NSLOT * i + c
                if not last and c > 0:
                    sp.wait_ge(s_qk, 16 * b)
                    load_stack(b + 2, (c + 2) % NSLOT)
                if not last:
                    for half in range(2):
                        load_shift(b + 1, (c + 1) % NSLOT, half)

            sp_step(0, 0, False)
            with sp.Fori(0, 2) as i:
                for u in range(3):
                    sp_step(i, 1 + u, False)
            for i in range(4):
                sp.wait_ge(s_fo, i + 1)
                sp.dma_start(out_d[2 * i:2 * i + 2].rearrange("b (p t) c -> p b t c", t=TT),
                             ACC[:, 4 * i:4 * i + 4].rearrange("p (b t) c -> p b t c", t=TT)).then_inc(s_out, 16)
            sp.wait_ge(s_out, 64)

        @block.gpsimd
        def _(pool):
            nc.gpsimd.memset(B2P[:], 0.0).then_inc(s_ebp, 1)
            nc.gpsimd.memset(KV[:], 0.0).then_inc(s_zero, 1)
            nc.gpsimd.memset(V8[:], 0.0).then_inc(s_zero, 1)
            pool.wait_ge(s_const, 64)
            nc.gpsimd.tensor_copy(RT[:], IDN[:].unsqueeze(1).broadcast_to([P, B, C])).then_inc(s_zero, 1)
            nc.gpsimd.tensor_copy(IA[:, 1], IDN[:].unsqueeze(1).broadcast_to([P, B, C])).then_inc(s_zero, 1)
            with pool.Fori(0, L) as l:
                pool.wait_ge(s_kv, l + 1)
                nc.gpsimd.tensor_tensor(V8[0:B], KV[0:B, C:].unsqueeze(1).broadcast_to([B, B, C]),
                                        DIAG[:].unsqueeze(2).broadcast_to([B, B, C]), ALU.mult).then_inc(s_v8, 1)

            nc.gpsimd.memset(NH[:], -0.5).then_inc(s_stk0, 1)
            nc.gpsimd.memset(VT[:, NT:], 0.0).then_inc(s_stk0, 1)
            nc.gpsimd.memset(VS[:], 0.0).then_inc(s_zero, 1)
            pool.wait_ge(s_zero, 6)
            nc.gpsimd.memset(VS[:, :, :, :, HD:HD + 1], 1.0).then_inc(s_zero, 1)
            pool.wait_ge(s_zero, 7)
            nc.gpsimd.memset(STK[:].bitcast(u32), 0).then_inc(s_zero, 1)
            pool.wait_ge(s_zero, 8)
            nc.gpsimd.memset(KS[SROW:SROW + 3], 1.0).then_inc(s_stk0, 1)
            pool.wait_ge(s_stk0, 3)
            def rstd(i):
                t = slice(4 * i, 4 * i + 4)
                pool.wait_ge(s_mv, i + 1)
                nc.gpsimd.tensor_scalar(VE[:, t], MV[:, t, 1], EPS, None, ALU.add).then_inc(s_ve, 1)
                pool.wait_ge(s_ve, i + 1)
                nc.gpsimd.tensor_tensor(RS[:, t], VE[:, t], NH[:, t], ALU.pow).then_inc(s_rs, 1)

            for i in range(4):
                rstd(i)
            for i in range(4):
                k, c = flat(KF)[:, cols(i)], cols(i)
                pool.wait_ge(s_k1, i + 1)
                nc.gpsimd.tensor_tensor(k, k, KP[:, 0, c], ALU.subtract).then_inc(s_k1r, 1)
            for i in range(4):
                k, c = flat(KF)[:, cols(i)], cols(i)
                pool.wait_ge(s_k2, i + 1)
                nc.gpsimd.tensor_tensor(KP[:, 2, c], k, KP[:, 1, c], ALU.subtract).then_inc(s_k3, 1)

            def batch_values(b, slot):
                nc.gpsimd.tensor_copy(VS[:, slot, :, :, 0:HD], VT[:, bass.ds(b * TT, TT)]).then_inc(s_vs, 1)

            def shift_parts(n, half, first=False):
                m = 2 * n + half
                pool.wait_ge(s_shb, m + 1)
                if not first:
                    alone(pool, s_shs[half], 16 * n)
                else:
                    pool.wait_ge(s_vs, NSLOT)
                nc.gpsimd.tensor_copy(SH[:, half, 1], SHF[:, half]).then_inc(s_shc, 1)
                pool.wait_ge(s_shc, m + 1)
                nc.gpsimd.tensor_tensor(SH[:, half, 2], SHF[:, half], SH[:, half, 1], ALU.subtract).then_inc(s_shd, 1)

            pool.wait_ge(s_vt, 4)
            for b in range(NSLOT):
                batch_values(b, b)
            for half in range(2):
                shift_parts(0, half, True)

            def pool_step(i, c):
                b = NSLOT * i + c
                if c > 0:
                    pool.wait_ge(s_pv, 8 * b)
                    alone(pool, s_shd, 2 * b + 2)
                    batch_values(b + 2, (c + 2) % NSLOT)
                    pool.wait_ge(s_vs, b + 3)
                for half in range(2):
                    shift_parts(b + 1, half)

            pool_step(0, 0)
            with pool.Fori(0, 2) as i:
                for u in range(3):
                    pool_step(i, 1 + u)

            for i in range(4):
                pool.wait_ge(s_shd, 16)
                t = slice(4 * i, 4 * i + 4)
                pool.wait_ge(s_mv, i + 5)
                nc.gpsimd.tensor_scalar(VE[:, t], MV[:, t, 1], EPS, None, ALU.add).then_inc(s_ve, 1)
                pool.wait_ge(s_ve, i + 5)
                nc.gpsimd.tensor_tensor(RS[:, t], VE[:, t], NH[:, t], ALU.pow).then_inc(s_rs, 1)
            nc.gpsimd.memset(ACC, 0.0).then_inc(s_acc, 1)
            nc.gpsimd.tensor_tensor(XN, XN, ROWS[:, 3, :].unsqueeze(1).broadcast_to([P, NT, C]), ALU.add).then_inc(s_xb, 1)

            def hidden_rstd(n, u):
                alone(pool, s_mv2, n + 1)
                nc.gpsimd.tensor_scalar(NG2[:, u], MV2[:, u, :, 0], -1.0, None, ALU.mult).then_inc(s_ve2, 1)
                nc.gpsimd.tensor_scalar(VE2[:, u], MV2[:, u, :, 1], EPS, None, ALU.add).then_inc(s_ve2, 1)
                alone(pool, s_ve2, 2 * n + 2)
                nc.gpsimd.tensor_tensor(RS2[:, u], VE2[:, u], NH[:, 0:4], ALU.pow).then_inc(s_rs2a, 1)
                pool.wait_ge(s_rs2a, n + 1)
                nc.gpsimd.tensor_tensor(NB2[:, u], NG2[:, u], RS2[:, u], ALU.mult).then_inc(s_rs2, 1)

            hidden_rstd(0, 0)
            pool.wait_ge(s_oh, 1)
            with pool.Fori(0, E - 1) as x:
                for q in range(4):
                    hidden_rstd(4 * x + q + 1, (q + 1) % 2)
                    if q == 0:
                        alone(pool, s_sel, 4 * x + 2)
                        nc.gpsimd.tensor_copy(MK[:], OH[:, :, bass.ds(x + 1, 1)].rearrange("p n o -> p (n o)")).then_inc(s_mk, 1)
            for r in (2, 3):
                for i in range(4):
                    t = slice(4 * i, 4 * i + 4)
                    pool.wait_ge(s_mv, 4 * r + i + 1)
                    nc.gpsimd.tensor_scalar(VE[:, t], MV[:, t, 1], EPS, None, ALU.add).then_inc(s_ve, 1)
                    pool.wait_ge(s_ve, 4 * r + i + 1)
                    nc.gpsimd.tensor_tensor(RS[:, t], VE[:, t], NH[:, t], ALU.pow).then_inc(s_rs, 1)

        @block.tensor
        def _(pe):
            mm = nc.tensor.matmul
            pe.wait_ge(s_const, 64)
            pe.wait_ge(s_x, 64)
            for g in range(2):
                for t in range(TT):
                    last = mm(batches(bank(g, 0)), AVG[:], X[:, GB * g:GB * (g + 1), t, :], start=t == 0, stop=t == TT - 1)
                last.then_inc(s_mrow, 1)
            for b in range(B):
                for t in range(TT):
                    last = mm(bank(0, 1)[:, b:b + 1], X[:, b, t, :], AVG[:, 0:1], start=t == 0, stop=t == TT - 1)
            last.then_inc(s_mcol, 1)
            pe.wait_ge(s_xc, 4)
            for g in range(2):
                for b in range(GB):
                    xb = X[:, GB * g + b]
                    for t in range(TT):
                        last = mm(bank(g, 2)[:, b * C:(b + 1) * C], xb[:, t, :], xb[:, t, :], start=t == 0, stop=t == TT - 1)
                last.then_inc(s_gram, 1)
            for i, (g, k) in enumerate(((0, 3), (1, 3), (0, 0), (1, 0))):
                for j in range(2 * TT):
                    last = nc.tensor.transpose(bank(g, k)[:, j * P:(j + 1) * P], X[:, 2 * i + j // TT, j % TT, :], IDN[:])
                last.then_inc(s_xct, 1)
            pe.wait_ge(s_xt, 4)
            pe.wait_ge(s_zero, 5)
            with pe.Fori(0, L // 2) as i:
                for u in range(2):
                    l = 2 * i + u
                    W = WL[:, u]
                    pe.wait_ge(s_w[u], 32 * i + 32)
                    pe.wait_ge(s_mean, l + 1)
                    for g in range(2):
                        pe.wait_ge(s_g, 2 * l + g + 1)
                        for b in range(GB):
                            last = mm(bank(g, 0)[:, b * C:(b + 1) * C], G[:, GB * g + b, :], W[:, CVT:CVT + C], start=True, stop=True)
                        last.then_inc(s_p, 1)
                    mm(bank(0, 3)[0:B, 0:2 * C], MEAN[:], W[:, CKT:CKT + 2 * C], start=True, stop=True).then_inc(s_row, 1)
                    mm(bank(1, 3)[:, 0:B], W[:, CQT:CQT + C], MEAN[:], start=True, stop=True).then_inc(s_qbd, 1)
                    pe.wait_ge(s_v8, l + 1)
                    for g in range(2):
                        pe.wait_ge(s_pc, 2 * l + g + 1)
                        for q in range(Q4):
                            quad = slice(QW * q, QW * (q + 1))
                            out = bank(g, 2)[quad, 0:GB * QW].rearrange("p (b j) -> p b j", b=GB)
                            mm(out, W[:, CKT + QW * q:CKT + QW * (q + 1)], GV[:, GB * g:GB * (g + 1), quad], start=True, stop=False)
                            last = mm(out, KV[:, quad], V8[:, GB * g:GB * (g + 1), quad], start=False, stop=True)
                        last.then_inc(s_k, 1)
                    for g in range(2):
                        if g == 0:
                            pe.wait_ge(s_kv, l + 1)
                        else:
                            pe.wait_ge(s_qb, l + 1)
                        pe.wait_ge(s_rt, 2 * l + g + 1)
                        for b in range(GB):
                            n = GB * g + b
                            last = mm(bank(g, 3)[:, b * C:(b + 1) * C], IA[:, 1 - u, n, :], RT[:, n, :], start=True, stop=True)
                        last.then_inc(s_r, 1)
                    for g in range(2):
                        pe.wait_ge(s_m, 2 * l + g + 1)
                        for b in range(GB):
                            o = (b % 2) * BQ
                            last = mm(bank(g, b // 2)[:, o:o + BQ], MF[:, GB * g + b, :], W[:, CQN:CQN + BQ], start=True, stop=True)
                        last.then_inc(s_b, 1)
                    for g in range(2):
                        pe.wait_ge(s_bt, 2 * l + g + 1)
                        for b in range(GB):
                            last = mm(bank(g, 2)[:, b * C:(b + 1) * C], BT[:, GB * g + b, 0:C], W[:, CPT:CPT + C], start=True, stop=True)
                        last.then_inc(s_a, 1)
                    for g in range(2):
                        n = GB * g
                        own = BT[:].rearrange("p b c -> p (b c)")[:, n * BQ + C + n::BQ + 1][:, 0:GB]
                        mm(bank(g, 0)[:, 0:GB], W[:, CPT:CPT + C], own, start=True, stop=True).then_inc(s_ym, 1)
                    for g in range(2):
                        pe.wait_ge(s_ia, 2 * l + g + 1)
                        pe.wait_ge(s_rt, 2 * l + g + 3)
                        for b in range(GB):
                            n = GB * g + b
                            last = mm(bank(g, 3)[:, b * C:(b + 1) * C], G[:, n, :], IA[:, u, n, :], start=True, stop=True)
                        last.then_inc(s_u, 1)
                    for g in range(2):
                        pe.wait_ge(s_uc, 2 * l + g + 1)
                        for b in range(GB):
                            n = GB * g + b
                            last = mm(bank(g, 1)[:, b * C:(b + 1) * C], IA[:, u, n, :], U[:, n, :], start=True, stop=True)
                        last.then_inc(s_gd, 1)
            for g in range(2):
                for b in range(GB):
                    n = GB * g + b
                    last = mm(bank(g, 3)[:, b * C:(b + 1) * C], RT[:, n, :], IA[:, 1, n, :], start=True, stop=True)
                last.then_inc(s_r, 1)

            pe.wait_ge(s_ir, 2)
            for i in range(4):
                for b in (2 * i, 2 * i + 1):
                    last = mm(PS[:, i, (b % 2) * T:(b % 2 + 1) * T], IR[:, b, :], XT[:, b, :], start=True, stop=True)
                last.then_inc(s_h, 1)
            for i in range(4):
                pe.wait_ge((s_htv, s_hta)[i % 2], i // 2 + 1)
                for k in range(4):
                    last = nc.tensor.transpose(PS[:, 4 + i, k * P:(k + 1) * P], HT[:, 4 * i + k, :], IDN[:])
                last.then_inc(s_tok, 1)
            for i in range(4):
                pe.wait_ge(s_x1, i + 1)
                for k in range(4):
                    last = nc.tensor.transpose(PS[:, i, k * P:(k + 1) * P], XN[:, 4 * i + k, :], IDN[:])
                last.then_inc(s_x1t, 1)
            pe.wait_ge(s_wf, 16 * 7)
            for i in range(4):
                pe.wait_ge(s_xtc, i + 1)
                mm(PS[:, 4 + i, :], QW_["qw"][:], XTF[:, cols(i)], start=True, stop=True).then_inc(s_q, 1)
                mm(PS[:, i, :], QW_["kw"][:], XTF[:, cols(i)], start=True, stop=True).then_inc(s_kd, 1)
            pe.wait_ge(s_swb, 1)
            for i in range(4):
                pe.wait_ge(s_qf, i + 1)
                mm(PS[:, 4 + i, :], SWB[:], flat(QF)[:, cols(i)], start=True, stop=True).then_inc(s_z, 1)
            for i in range(4):
                pe.wait_ge(s_kf, i + 1)
                for k in range(4):
                    last = mm(PS[:, i, k * P:(k + 1) * P], XTF[:, (4 * i + k) * P:(4 * i + k + 1) * P], QW_["vw"][:], start=True, stop=True)
                last.then_inc(s_v, 1)

            def max_scores(M, j, slot, loaded):
                pe.wait_ge(s_stk[slot], 144 * loaded)
                if M is not None:
                    pe.wait_ge(s_max, M - 1)
                for k in range(4):
                    h = 4 * (j // 2) + k
                    last = mm(PS[:, 2 * (j % 2) + k // 2, (k % 2) * T:(k % 2 + 1) * T],
                              QS[0:KMAX, slot, h, (j % 2) * P:(j % 2 + 1) * P], KS[0:KMAX, slot, h, :], start=True, stop=True)
                last.then_inc(s_mxd, 1)

            def shift_rows(n, half, slot):
                pe.wait_ge(s_max, 8 * n + 4 * half + 4)
                nm = NM[:, slot, half * H // 2:(half + 1) * H // 2, :].rearrange("p h q -> p (h q)")
                nc.tensor.transpose(PS[0:H, 7, 0:P], nm, IDN[:]).then_inc(s_mt, 1)

            def pv(b, j, slot, first):
                if j == 0:
                    pe.wait_ge(s_vs, b + 1)
                pe.wait_ge(s_exp, 16 * b + 2 * j + 2)
                if j % 2 == 0 and not (first and j == 0):
                    pe.wait_ge(s_ot, 4 * b + j // 2)
                for k in range(4):
                    last = mm(PS[QW * k:QW * (k + 1), 6, 0:T], VS[:, slot, j % 2, 4 * (j // 2) + k, :],
                              PT[:, (2 * j + k // 2) % 4, k % 2, :], start=j % 2 == 0, stop=j % 2 == 1)
                last.then_inc(s_pv, 1)

            def out_tokens(b, qt, slot):
                pe.wait_ge(s_ot, 4 * b + 4)
                for g in range(Q4):
                    last = nc.tensor.transpose(PS[:, 7, g * P:(g + 1) * P], OTS[:, slot, g, qt * P:(qt + 1) * P], IDN[:])
                last.then_inc(s_tr, 1)

            for j in range(8):
                max_scores(j if j > 1 else None, j, 0, 1)
                if j == 5:
                    pe.wait_ge(s_vt, 4)
                    shift_rows(0, 0, 0)
            pe.wait_ge(s_shb, 1)
            shift_rows(0, 1, 0)
            for j in range(3):
                max_scores(8 + j, j, 1, 1)

            def pe_step(i, c, first=False, last=False):
                b, r = NSLOT * i + c, c % NSLOT
                for j in range(8):
                    if not last:
                        a = c + (1 if j < 5 else 2)
                        max_scores(8 * b + j + 11, (j + 3) % 8, a % NSLOT, i + a // NSLOT + 1)
                    if j % 4 == 0:
                        pe.wait_ge(s_shl[j // 4], 16 * b + 16)
                    for k in (0, 1):
                        if not (first and j == 0):
                            pe.wait_ge(s_exp, 16 * b + 2 * j + k - 1)
                        for hh in (0, 1):
                            h = 4 * (j // 2) + 2 * k + hh
                            o = mm(PS[:, 4 + k, hh * T:(hh + 1) * T], KS[0:KEXP, r, h, (j % 2) * P:(j % 2 + 1) * P],
                                   QS[0:KEXP, r, h, :], start=True, stop=True)
                        o.then_inc(s_qk, 1)
                    if j > 0:
                        pv(b, j - 1, r, first)
                    elif not first:
                        pv(b - 1, 7, (c - 1) % NSLOT, False)
                    if j == 2 and not last:
                        pe.wait_ge(s_shb, 2 * b + 2)
                        shift_rows(b + 1, 0, (c + 1) % NSLOT)
                    if j == 3 and not first:
                        pe.wait_ge(s_shb, 16 if last else 2 * b + 3)
                        out_tokens(b - 1, 0, (c - 1) % NSLOT)
                    if j == 5 and not first:
                        pe.wait_ge(s_on, 2 * b - 1)
                        out_tokens(b - 1, 1, (c - 1) % NSLOT)
                    if j == 6 and not last:
                        if first:
                            pe.wait_ge(s_shb, 3)
                        else:
                            pe.wait_ge(s_on, 2 * b)
                        shift_rows(b + 1, 1, (c + 1) % NSLOT)

            pe_step(0, 0, first=True)
            with pe.Fori(0, 2) as i:
                for u in range(3):
                    pe_step(i, 1 + u)
            pe_step(0, 7, last=True)
            pv(7, 7, 7 % NSLOT, False)
            for qt in range(TT):
                pe.wait_ge(s_on, 14 + qt)
                out_tokens(7, qt, 7 % NSLOT)

            pe.wait_ge(s_on, 16)
            pe.wait_ge(s_max, 67)
            for i in range(4):
                for k in range(4):
                    last = nc.tensor.transpose(PS[:, i, k * P:(k + 1) * P], ON[:, 4 * i + k, :], IDN[:])
                last.then_inc(s_ott, 1)
            for i in range(4):
                pe.wait_ge(s_otc, i + 1)
                mm(PS[:, 4 + i, :], QW_["gw"][:], flat(OT)[:, cols(i)], start=True, stop=True).then_inc(s_gt, 1)
            for i in range(4):
                pe.wait_ge(s_og, i + 1)
                for k in range(4):
                    last = mm(PS[:, i, k * P:(k + 1) * P], OT[:, 4 * i + k, :], QW_["ow"][:], start=True, stop=True)
                last.then_inc(s_at, 1)
            for i in range(4):
                pe.wait_ge(s_x2, i + 1)
                for k in range(4):
                    last = nc.tensor.transpose(PS[:, 4 + i, k * P:(k + 1) * P], X2[:, 4 * i + k, :], IDN[:])
                last.then_inc(s_x2t, 1)
            pe.wait_ge(s_we, 16 * 7)
            for i in range(4):
                pe.wait_ge(s_x2c, i + 1)
                for k in range(4):
                    n = 4 * i + k
                    last = mm(PS[:, 0, n * E:(n + 1) * E], X2T[:, n * P:(n + 1) * P], MG[:], start=True, stop=True)
            last.then_inc(s_lg, 1)

            def hidden(x, q):
                for k in range(4):
                    out = PS[:, 2 * (q % 2) + k // 2, :].rearrange("p (k f) -> p k f", k=2)
                    if k % 2 == 0:
                        mm(out, ONE3[:], B1P[:, bass.ds(x * F, F)].unsqueeze(1).broadcast_to([P, 2, F]), start=True, stop=False)
                    n = 4 * q + k
                    last = mm(out[:, k % 2, :], X2T[:, n * P:(n + 1) * P], W1[:, bass.ds(x, 1), :].rearrange("p o f -> p (o f)"),
                              start=False, stop=k % 2 == 1)
                last.then_inc(s_h1, 1)

            pe.wait_ge(s_eb, 40)
            pe.wait_ge(s_ebp, 22)
            pe.wait_ge(s_oh, 1)
            hidden(0, 0)
            with pe.Fori(0, E - 1) as x:
                for q in range(4):
                    n = 4 * x + q
                    pe.wait_ge(s_nrm, n + 1)
                    hidden(x + (q + 1) // 4, (q + 1) % 4)
                    pe.wait_ge(s_nrm, n + 2)
                    pe.wait_ge(s_gl, 2 * n + 1)
                    for c in range(FC):
                        for k in range(4):
                            last = nc.tensor.transpose(PS[:, 4 + c, k * P:(k + 1) * P], HN[:, q % 2, k, c * P:(c + 1) * P], IDN[:])
                        last.then_inc(s_td, 1)
                    for p in ([q - 1] if q in (1, 2) else [2, 3] if q == 3 else []):
                        n = 4 * x + p
                        pe.wait_ge(s_gl, 2 * n + 3)
                        pe.wait_ge(s_sel, n + 1)
                        out = PS[:, 6 + p % 2, :].rearrange("p (k c) -> p k c", k=4)
                        mm(out, ONE3[:], B2P[:, bass.ds(x * C, C)].unsqueeze(1).broadcast_to([P, 4, C]), start=True, stop=False)
                        for k in range(4):
                            for c in range(FC):
                                last = mm(out[:, k, :], GT[:, p % 2, c, k * P:(k + 1) * P],
                                          W2[:, bass.ds(x, 1), c, :].rearrange("p o c -> p (o c)"), start=False, stop=k == 3 and c == FC - 1)
                        last.then_inc(s_y, 1)

        @block.scalar
        def _(act):
            copy = lambda out, in_: nc.scalar.activation(out, in_, ACT.Copy)
            for i, (g, k) in enumerate(((0, 3), (1, 3), (0, 0), (1, 0))):
                act.wait_ge(s_xct, i + 1)
                copy(XT[:, 2 * i:2 * i + 2, :], bank(g, k).rearrange("p (b t) -> p b t", b=2)).then_inc(s_xt, 1)
            act.wait_ge(s_zero, 5)
            nc.scalar.copy(MSUM[:, 0:1], IDN[:, 0:1]).then_inc(s_rt, 1)
            nc.scalar.copy(MSUM[:, 1:2], IDN[:, 0:1]).then_inc(s_rt, 1)
            with act.Fori(0, L) as l:
                for g in range(2):
                    act.wait_ge(s_p, 2 * l + g + 1)
                    copy(GV[:, GB * g:GB * (g + 1), :], batches(bank(g, 0))).then_inc(s_pc, 1)
                for g in range(2):
                    act.wait_ge(s_r, 2 * l + g + 1)
                    copy(RT[:, GB * g:GB * (g + 1), :], batches(bank(g, 3))).then_inc(s_rt, 1)
                for g in range(2):
                    act.wait_ge(s_b, 2 * l + g + 1)
                    copy(BT[:, GB * g:GB * (g + 1), :].rearrange("p (k b) c -> p k (b c)", k=2),
                         PS[:, 4 * g:4 * g + 2, 0:2 * BQ]).then_inc(s_bt, 1)
                for g in range(2):
                    act.wait_ge(s_u, 2 * l + g + 1)
                    copy(U[:, GB * g:GB * (g + 1), :], batches(bank(g, 3))).then_inc(s_uc, 1)

            pe_bias = lambda i: MSUM[:, 2 * i:2 * i + 1]
            act.wait_ge(s_ms, 1)
            for i in (1, 3):
                act.wait_ge(s_h, i + 1)
                for b in (2 * i, 2 * i + 1):
                    o = nc.scalar.activation(flat(HT)[:, b * T:(b + 1) * T], PS[:, i, (b % 2) * T:(b % 2 + 1) * T],
                                             ACT.Identity, bias=MSUM[:, b:b + 1])
                o.then_inc(s_hta, 1)
            for i in range(4):
                act.wait_ge(s_x1t, i + 1)
                copy(XTF[:, cols(i)], PS[:, i, :]).then_inc(s_xtc, 1)
            for i in range(4):
                act.wait_ge(s_kd, i + 1)
                nc.scalar.activation(flat(KF)[:, cols(i)], PS[:, i, :], ACT.Copy, scale=SCALE).then_inc(s_kf, 1)
            for i in range(4):
                act.wait_ge(s_kf, i + 1)
                copy(KP[:, 0, cols(i)], flat(KF)[:, cols(i)]).then_inc(s_k1, 1)
                act.wait_ge(s_z, i + 1)
                nc.scalar.activation(flat(TH[:])[:, cols(i)], PS[:, 4 + i, :], ACT.Tanh, scale=0.5).then_inc(s_th, 1)
            for i in range(4):
                act.wait_ge(s_qs, i + 1)
                copy(QP[:, 0, cols(i)], flat(QF)[:, cols(i)]).then_inc(s_q1, 1)
                act.wait_ge(s_k1r, i + 1)
                copy(KP[:, 1, cols(i)], flat(KF)[:, cols(i)]).then_inc(s_k2, 1)
            for i in range(4):
                act.wait_ge(s_q1r, i + 1)
                copy(QP[:, 1, cols(i)], flat(QF)[:, cols(i)]).then_inc(s_q2, 1)

            def copy_out(b, g, slot):
                act.wait_ge(s_pv, 8 * b + 2 * g + 2)
                copy(OTS[:, slot, g, :], PS[:, 6, 0:T]).then_inc(s_ot, 1)

            def act_step(i, c, first=False):
                b, r = NSLOT * i + c, c % NSLOT
                for j in range(8):
                    for k in (0, 1):
                        act.wait_ge(s_qk, 16 * b + 2 * j + k + 1)
                        if not (first and j < 2):
                            act.wait_ge(s_pv, 8 * b + j - 1)
                        nc.scalar.activation(PT[:, (2 * j + k) % 4], PS[:, 4 + k, :].rearrange("p (h t) -> p h t", h=2),
                                             ACT.Exp).then_inc(s_exp, 1)
                    if j % 2 == 0 and j > 0:
                        copy_out(b, j // 2 - 1, r)
                    elif j == 0 and not first:
                        copy_out(b - 1, 3, (c - 1) % NSLOT)

            act_step(0, 0, first=True)
            with act.Fori(0, 2) as i:
                for u in range(3):
                    act_step(i, 1 + u)
            act_step(0, 7)
            copy_out(7, 3, 7 % NSLOT)

            for i in range(4):
                act.wait_ge(s_ott, i + 1)
                copy(flat(OT)[:, cols(i)], PS[:, i, :]).then_inc(s_otc, 1)
            act.wait_ge(s_gbh, 1)
            for i in range(4):
                act.wait_ge(s_gt, i + 1)
                nc.scalar.activation(flat(TH[:])[:, cols(i)], PS[:, 4 + i, :], ACT.Tanh, scale=0.5, bias=GBH[:, 1:2]).then_inc(s_tg, 1)
            for i in range(4):
                act.wait_ge(s_x2t, i + 1)
                copy(X2T[:, cols(i)], PS[:, 4 + i, :]).then_inc(s_x2c, 1)
            act.wait_ge(s_rch, 12)
            nc.scalar.activation(R1[5][:], R1[4][:], ACT.Exp).then_inc(s_ed, 1)
            nc.scalar.copy(RC[:, 0, 0:1], IDN[:, 0:1]).then_inc(s_nrm, 1)
            nc.scalar.copy(RC[:, 0, 1:2], IDN[:, 0:1]).then_inc(s_gl, 1)

            def normalise_hidden(n, u):
                act.wait_ge(s_rs2, n + 1)
                for k in range(4):
                    o = nc.scalar.activation(HN[:, u, k, :], PS[:, 2 * u + k // 2, (k % 2) * F:(k % 2 + 1) * F], ACT.Identity,
                                             scale=RS2[:, u, k:k + 1], bias=NB2[:, u, k:k + 1])
                o.then_inc(s_nrm, 1)

            normalise_hidden(0, 0)
            with act.Fori(0, E - 1) as x:
                for q in range(4):
                    n = 4 * x + q
                    normalise_hidden(n + 1, (q + 1) % 2)
                    for c in range(FC):
                        alone(act, s_td, 2 * n + c + 1)
                        nc.scalar.activation(GT[:, q % 2, c, :], PS[:, 4 + c, :], ACT.Gelu,
                                             scale=LNW[:, 0, c, bass.ds(x, 1)], bias=LNW[:, 1, c, bass.ds(x, 1)]).then_inc(s_gl, 1)

        @block.vector
        def _(dve):
            tt = nc.vector.tensor_tensor
            nc.vector.memset(ONE3[:], 0.0).then_inc(s_eb, 1)
            nc.vector.memset(B1P[:].bitcast(u32), 0).then_inc(s_eb, 1)
            dve.wait_ge(s_eb, 34)
            nc.vector.memset(ONE3[0:3, :], 1.0).then_inc(s_eb, 1)
            dve.wait_ge(s_ebp, 17)
            for full, parts, done, k in ((B1F, B1P, s_eb, 35), (B2F, B2P, s_ebp, 17)):
                nc.vector.tensor_copy(parts[0:3], full).then_inc(done, 1)
                dve.wait_ge(done, k + 1)
                nc.vector.scalar_tensor_tensor(full, parts[0:3], ALF[:, 0:1], full, ALU.mult, ALU.add).then_inc(done, 1)
                dve.wait_ge(done, k + 2)
                nc.vector.tensor_copy(parts[0:3], full).then_inc(done, 1)
                dve.wait_ge(done, k + 3)
                nc.vector.scalar_tensor_tensor(full, parts[0:3], ALF[:, 1:2], full, ALU.mult, ALU.add).then_inc(done, 1)
                dve.wait_ge(done, k + 4)
                nc.vector.tensor_copy(parts[0:3], full).then_inc(done, 1)
            for g in range(2):
                dve.wait_ge(s_mrow, g + 1)
                for t in range(TT):
                    xg = X[:, GB * g:GB * (g + 1), t, :]
                    if g == 0 and t == 0:
                        dve.wait_ge(s_mcol, 1)
                    tt(xg, xg, batches(bank(g, 0)), ALU.subtract).then_inc(s_xc, 1)
            nc.vector.tensor_copy(MEAN[:], bank(0, 1)[:, 0:B]).then_inc(s_mean, 1)
            nc.vector.tensor_copy(MEAN0[:], bank(0, 1)[:, 0:B]).then_inc(s_zero, 1)
            for g in range(2):
                dve.wait_ge(s_gram, g + 1)
                nc.vector.tensor_copy(G[:, GB * g:GB * (g + 1), :], batches(bank(g, 2))).then_inc(s_g, 1)
            dve.wait_ge(s_zero, 5)
            with dve.Fori(0, L // 2) as i:
                for u in range(2):
                    l = 2 * i + u
                    dve.wait_ge(s_row, l + 1)
                    tt(KV[0:B, :], bank(0, 3)[0:B, 0:2 * C], BR[:, u, :], ALU.add).then_inc(s_kv, 1)
                    dve.wait_ge(s_qbd, l + 1)
                    nc.vector.tensor_scalar(WL[:, u, CQB:CQB + B], bank(1, 3)[:, 0:B], WL[:, u, CBQ:CBQ + 1], None, ALU.add).then_inc(s_qb, 1)
                    for g in range(2):
                        dve.wait_ge(s_k, 2 * l + g + 1)
                        for b in range(GB):
                            o = tt(MF[:, GB * g + b, :].rearrange("p (q j) -> p q j", q=Q4),
                                   bank(g, 2)[:, QW * b:QW * (b + 1)].unsqueeze(1).broadcast_to([P, Q4, QW]),
                                   MASK[:], ALU.mult)
                        o.then_inc(s_m, 1)
                    for g in range(2):
                        dve.wait_ge(s_a, 2 * l + g + 1)
                        tt(IA[:, u, GB * g:GB * (g + 1), :], batches(bank(g, 2)),
                           IDN[:].unsqueeze(1).broadcast_to([P, GB, C]), ALU.add).then_inc(s_ia, 1)
                    for g in range(2):
                        dve.wait_ge(s_ym, 2 * l + g + 1)
                        m = MEAN[:, GB * g:GB * (g + 1)]
                        o = nc.vector.scalar_tensor_tensor(m, bank(g, 0)[:, 0:GB], WL[:, u, CBP:CBP + 1], m, ALU.add, ALU.add)
                    o.then_inc(s_mean, 1)
                    for g in range(2):
                        dve.wait_ge(s_gd, 2 * l + g + 1)
                        nc.vector.tensor_copy(G[:, GB * g:GB * (g + 1), :], batches(bank(g, 1))).then_inc(s_g, 1)
            for g in range(2):
                dve.wait_ge(s_r, 2 * L + g + 1)
                tt(IR[:, GB * g:GB * (g + 1), :], batches(bank(g, 3)),
                   IDN[:].unsqueeze(1).broadcast_to([P, GB, C]), ALU.add).then_inc(s_ir, 1)
            dve.wait_ge(s_mean, L + 1)
            tt(MSUM[:], MEAN[:], MEAN0[:], ALU.add).then_inc(s_ms, 1)
            dve.wait_ge(s_ms, 1)
            for i in (0, 2):
                dve.wait_ge(s_h, i + 1)
                for b in (2 * i, 2 * i + 1):
                    o = nc.vector.tensor_scalar(flat(HT)[:, b * T:(b + 1) * T], PS[:, i, (b % 2) * T:(b % 2 + 1) * T],
                                                MSUM[:, b:b + 1], None, ALU.add)
                o.then_inc(s_htv, 1)
            dve.wait_ge(s_wf, 16 * 7)
            nc.vector.tensor_scalar(SWB[:], EM[:], SWC[:, 0:1], None, ALU.mult).then_inc(s_swb, 1)

            def statistics(src, i, k0):
                for k in range(4):
                    o = nc.vector.bn_stats(ST[:, 4 * i + k, :], src(k))
                o.then_inc(s_st, 1)
                dve.wait_ge(s_st, k0 + i + 1)
                for k in range(4):
                    o = nc.vector.bn_aggr(MV[:, 4 * i + k, :], ST[:, 4 * i + k, :])
                o.then_inc(s_mv, 1)

            for i in range(4):
                dve.wait_ge(s_tok, i + 1)
                statistics(lambda k: PS[:, 4 + i, k * P:(k + 1) * P], i, 0)
            for i in range(4):
                dve.wait_ge(s_rs, i + 1)
                for k in range(4):
                    n = 4 * i + k
                    o = nc.vector.tensor_scalar(XN[:, n, :], PS[:, 4 + i, k * P:(k + 1) * P], MV[:, n, 0:1], RS[:, n:n + 1],
                                                ALU.subtract, ALU.mult)
                o.then_inc(s_x1, 1)
            for i in range(4):
                dve.wait_ge(s_q, i + 1)
                nc.vector.tensor_copy(flat(QF)[:, cols(i)], PS[:, 4 + i, :]).then_inc(s_qf, 1)
            for i in range(4):
                q = flat(QF)[:, cols(i)]
                dve.wait_ge(s_v, i + 1)
                nc.vector.tensor_copy(VT[:, 4 * i:4 * i + 4].rearrange("p n h d -> p (n h d)"), PS[:, i, :]).then_inc(s_vt, 1)
                dve.wait_ge(s_th, i + 1)
                nc.vector.scalar_tensor_tensor(q, flat(TH[:])[:, cols(i)], 1.0, q, ALU.add, ALU.mult).then_inc(s_qs, 1)
            for i in range(4):
                q = flat(QF)[:, cols(i)]
                dve.wait_ge(s_q1, i + 1)
                tt(q, q, QP[:, 0, cols(i)], ALU.subtract).then_inc(s_q1r, 1)
            for i in range(4):
                dve.wait_ge(s_q2, i + 1)
                tt(QP[:, 2, cols(i)], flat(QF)[:, cols(i)], QP[:, 1, cols(i)], ALU.subtract).then_inc(s_q3, 1)

            def take_max(M, j, slot):
                dve.wait_ge(s_mxd, M + 1)
                g = 4 * (j // 2)
                nc.vector.tensor_reduce(NM[:, slot, g:g + 4, j % 2],
                                        PS[:, 2 * (j % 2):2 * (j % 2) + 2, :].rearrange("p k (h t) -> p (k h) t", h=2),
                                        AX.X, ALU.max, negate=True).then_inc(s_max, 1)

            def shift_part(n, half, first=False):
                m = 2 * n + half
                dve.wait_ge(s_mt, m + 1)
                if not first:
                    dve.wait_ge(s_shs[half], 16 * n)
                nc.vector.tensor_copy(SH[:, half, 0], PS[0:H, 7, 0:P]).then_inc(s_sha, 1)
                dve.wait_ge(s_sha, m + 1)
                tt(SHF[:, half], PS[0:H, 7, 0:P], SH[:, half, 0], ALU.subtract).then_inc(s_shb, 1)

            def normalise(b, qt):
                dve.wait_ge(s_tr, 2 * b + qt + 1)
                o = PS[:, 7, :].rearrange("p (h d) -> p h d", d=QW)
                nc.vector.reciprocal(RC[:, qt, :], o[:, :, HD]).then_inc(s_rc, 1)
                dve.wait_ge(s_rc, 2 * b + qt + 1)
                tt(ON[:, bass.ds(2 * b + qt, 1), :].rearrange("p o (h d) -> p (o h) d", d=HD), o[:, :, 0:HD],
                   RC[:, qt, :].unsqueeze(2).broadcast_to([P, H, HD]), ALU.mult).then_inc(s_on, 1)

            for j in range(8):
                take_max(j, j, 0)
                if j == 5:
                    shift_part(0, 0, True)
            shift_part(0, 1, True)
            for j in range(3):
                take_max(8 + j, j, 1)

            def dve_step(i, c, first=False, last=False):
                b = NSLOT * i + c
                for j in range(8):
                    if not last:
                        take_max(8 * b + j + 11, (j + 3) % 8, (c + (1 if j < 5 else 2)) % NSLOT)
                    if j == 2 and not last:
                        shift_part(b + 1, 0)
                    if j == 3 and not first:
                        normalise(b - 1, 0)
                    if j == 5 and not first:
                        normalise(b - 1, 1)
                    if j == 6 and not last:
                        shift_part(b + 1, 1)

            dve_step(0, 0, first=True)
            with dve.Fori(0, 2) as i:
                for u in range(3):
                    dve_step(i, 1 + u)
            dve_step(0, 7, last=True)
            for qt in range(TT):
                normalise(7, qt)
            dve.wait_ge(s_we, 16 * 7)
            nc.vector.tensor_scalar(GBH[:, 1:2], GBH[:, 0:1], 0.5, None, ALU.mult).then_inc(s_gbh, 1)
            for i in range(4):
                dve.wait_ge(s_tg, i + 1)
                o = flat(OT)[:, cols(i)]
                nc.vector.scalar_tensor_tensor(o, flat(TH[:])[:, cols(i)], 1.0, o, ALU.add, ALU.mult).then_inc(s_og, 1)
            quad = lambda ap, i: ap[:, 4 * i:4 * i + 4, :]
            row = lambda r: ROWS[:, r, :].unsqueeze(1).broadcast_to([P, 4, C])
            for i in range(4):
                dve.wait_ge(s_at, i + 1)
                nc.vector.scalar_tensor_tensor(quad(X2, i), PS[:, i, :].rearrange("p (k c) -> p k c", k=4), 0.5, quad(XN, i),
                                               ALU.mult, ALU.add).then_inc(s_xp, 1)
                dve.wait_ge(s_xp, i + 1)
                statistics(lambda k: X2[:, 4 * i + k, :], i, 4)
            for i in range(4):
                dve.wait_ge(s_rs, 4 + i + 1)
                for k in range(4):
                    n = 4 * i + k
                    o = nc.vector.tensor_scalar(X2[:, n, :], X2[:, n, :], MV[:, n, 0:1], RS[:, n:n + 1], ALU.subtract, ALU.mult)
                o.then_inc(s_xn, 1)
                dve.wait_ge(s_xn, i + 1)
                tt(quad(X2, i), quad(X2, i), row(0), ALU.mult).then_inc(s_xg, 1)
                dve.wait_ge(s_xg, i + 1)
                tt(quad(X2, i), quad(X2, i), row(1), ALU.add).then_inc(s_x2, 1)

            chain = [0]

            def link(ins):
                chain[0] += 1
                ins.then_inc(s_rch, 1)
                dve.wait_ge(s_rch, chain[0])

            per = lambda a: a[:].unsqueeze(2).broadcast_to([P, NT, E])
            each = lambda r: ER[:, r, :].unsqueeze(1).broadcast_to([P, NT, E])
            lg, t8, l2 = (a[:] for a in RT8)
            top1, key1, top2, key2, diff, expd = R1
            red = lambda out, in_, op=ALU.max: nc.vector.tensor_reduce(out[:], in_, AX.X, op)
            dve.wait_ge(s_lg, 1)
            link(tt(lg, PS[:, 0, 0:NT * E].rearrange("p (n e) -> p n e", n=NT), each(0), ALU.add))
            link(red(top1, lg))
            link(tt(t8, lg, per(top1), ALU.is_equal))
            link(tt(t8, t8, each(2), ALU.mult))
            link(red(key1, t8))
            link(tt(t8, each(2), per(key1), ALU.is_equal))
            link(nc.vector.scalar_tensor_tensor(l2, t8, -3.0e38, lg, ALU.mult, ALU.add))
            link(red(top2, l2))
            link(tt(t8, l2, per(top2), ALU.is_equal))
            link(tt(t8, t8, each(2), ALU.mult))
            link(red(key2, t8))
            link(tt(diff[:], top2[:], top1[:], ALU.subtract))
            link(tt(key1[:], key1[:], key2[:], ALU.min))
            link(tt(OH[:], each(2), per(key1), ALU.is_equal))
            link(tt(t8, OH[:], each(1), ALU.mult))
            link(red(RSC, t8, ALU.add))
            dve.wait_ge(s_ed, 1)
            link(nc.vector.tensor_scalar(key1[:], expd[:], 1.0, None, ALU.add))
            link(nc.vector.reciprocal(key2[:], key1[:]))
            link(tt(top1[:], expd[:], key2[:], ALU.mult))
            tt(WS[:], top1[:], key2[:], ALU.add).then_inc(s_oh, 1)
            dve.wait_ge(s_acc, 1)
            nc.vector.tensor_copy(RC[:, 1, 1:2], IDN[:, 0:1]).then_inc(s_sel, 1)
            nc.vector.tensor_copy(RC[:, 1, 2:3], IDN[:, 0:1]).then_inc(s_sel, 1)

            def hidden_statistics(n, u):
                dve.wait_ge(s_h1, n + 1)
                for k in range(4):
                    o = nc.vector.bn_stats(ST2[:, u, k, :], PS[:, 2 * u + k // 2, (k % 2) * F:(k % 2 + 1) * F])
                o.then_inc(s_st2, 1)
                alone(dve, s_st2, n + 1)
                for k in range(4):
                    o = nc.vector.bn_aggr(MV2[:, u, k, :], ST2[:, u, k, :])
                o.then_inc(s_mv2, 1)

            hidden_statistics(0, 0)
            with dve.Fori(0, E - 1) as x:
                for q in range(4):
                    hidden_statistics(4 * x + q + 1, (q + 1) % 2)
                    for p in ([q - 1] if q in (1, 2) else [2, 3] if q == 3 else []):
                        dve.wait_ge(s_y, 4 * x + p + 1)
                        alone(dve, s_mk, x + 1)
                        nc.vector.copy_predicated(quad(ACC, p), MK[:, 4 * p:4 * p + 4].bitcast(u32).unsqueeze(2).broadcast_to([P, 4, C]),
                                                  PS[:, 6 + p % 2, :].rearrange("p (k c) -> p k c", k=4)).then_inc(s_sel, 1)

            dve.wait_ge(s_sel, 4 * (E - 1) + 2)
            dve.wait_ge(s_xb, 1)
            stt = nc.vector.scalar_tensor_tensor
            for i in range(4):
                for k in range(4):
                    n = 4 * i + k
                    o = stt(ACC[:, n, :], ACC[:, n, :], RSC[:, n:n + 1], X2[:, n, :], ALU.mult, ALU.add)
                o.then_inc(s_f1, 1)
                dve.wait_ge(s_f1, i + 1)
                for k in range(4):
                    n = 4 * i + k
                    o = stt(ACC[:, n, :], ACC[:, n, :], WS[:, n:n + 1], X2[:, n, :], ALU.mult, ALU.add)
                o.then_inc(s_f2, 1)
                dve.wait_ge(s_f2, i + 1)
                statistics(lambda k: ACC[:, 4 * i + k, :], i, 8)
            for i in range(4):
                dve.wait_ge(s_rs, 8 + i + 1)
                for k in range(4):
                    n = 4 * i + k
                    o = nc.vector.tensor_scalar(ACC[:, n, :], ACC[:, n, :], MV[:, n, 0:1], RS[:, n:n + 1], ALU.subtract, ALU.mult)
                o.then_inc(s_f3, 1)
                dve.wait_ge(s_f3, i + 1)
                tt(quad(ACC, i), quad(ACC, i), row(2), ALU.mult).then_inc(s_f4, 1)
                dve.wait_ge(s_f4, i + 1)
                tt(quad(ACC, i), quad(ACC, i), quad(XN, i), ALU.add).then_inc(s_f5, 1)
                dve.wait_ge(s_f5, i + 1)
                statistics(lambda k: ACC[:, 4 * i + k, :], i, 12)
            for i in range(4):
                dve.wait_ge(s_rs, 12 + i + 1)
                for k in range(4):
                    n = 4 * i + k
                    o = nc.vector.tensor_scalar(ACC[:, n, :], ACC[:, n, :], MV[:, n, 0:1], RS[:, n:n + 1], ALU.subtract, ALU.mult)
                o.then_inc(s_fo, 1)


def host_consts():
    mask = np.zeros((P, Q4, QW), np.float32)
    for i in range(P):
        q = i // QW
        a = (i % QW) // HD * HD
        mask[i, q, a:a + HD] = SCALE
    return {"avg": np.full((P, P), 1.0 / T, np.float32), "ident": np.eye(P, dtype=np.float32), "mask": mask,
            "diag": (np.eye(B) * T).astype(np.float32),
            "alf": np.array([[0, 0], [-1, 0], [-1, -1]], np.float32),
            "em": np.kron(np.eye(H), np.ones((HD, HD))).astype(np.float32)}


def layer_pack(Wqkv, bqkv, Wproj, bproj):
    t = lambda a: np.swapaxes(a, 1, 2)
    Wq, Wk, Wv = Wqkv[:, :C], Wqkv[:, C:2 * C], Wqkv[:, 2 * C:]
    lw = np.ascontiguousarray(np.concatenate([bqkv[:, :C, None], bproj[:, :, None], t(Wk), t(Wv), t(Wq), t(Wproj), Wq], axis=2))
    return lw, np.ascontiguousarray(bqkv[:, C:])


def kernel(**inputs):
    import concourse.bacc as bacc
    from concourse.bass_utils import run_bass_kernel_spmd

    a = {k.replace("L0_", ""): np.asarray(v) for k, v in inputs.items()}
    lw, lb = layer_pack(a["attn_Wqkv"], a["attn_bqkv"], a["attn_Wproj"], a["attn_bproj"])
    order = list(range(1, E)) + [0]
    col = lambda v: np.ascontiguousarray(v.reshape(-1, 1))
    by_unit = lambda v: v[order].reshape(E, FC, P).transpose(2, 1, 0)
    index = np.arange(E, 0, -1).astype(np.float32)
    arrays = {
        "x": a["attn_inputs_embeds"], "lw": lw, "lb": lb,
        "qw": a["ffn_q_w"], "kw": a["ffn_k_w"], "vw": a["ffn_v_w"], "ow": a["ffn_out_w"], "gw": a["ffn_gate_w"],
        "swc": col(a["ffn_scale_w"]), "gb": col(a["ffn_gate_b"]), "mg": a["ffn_moe_gate_w"],
        "rows": np.concatenate([a["ffn_n1_g"], a["ffn_n1_b"], a["ffn_n2_g"], a["ffn_n2_b"]])[None],
        "er": np.concatenate([a["ffn_moe_gate_b"], a["ffn_res_scale"], index])[None],
        "w1": a["ffn_w1"][order].transpose(1, 0, 2), "b1": a["ffn_b1"][order].reshape(1, -1),
        "w2": a["ffn_w2"][order].reshape(E, FC, P, C).transpose(2, 0, 1, 3), "b2": a["ffn_b2"][order].reshape(1, -1),
        "lnw": np.stack([by_unit(a["ffn_ln_g"]), by_unit(a["ffn_ln_b"])], axis=1),
        **host_consts(),
    }
    arrays = {f"in_{k}": np.ascontiguousarray(v) for k, v in arrays.items()}
    nc = bacc.Bacc("TRN2", target_bir_lowering=False, num_devices=1)
    aps = {k[3:]: nc.dram_tensor(k, v.shape, mybir.dt.from_np(v.dtype), kind="ExternalInput").ap() for k, v in arrays.items()}
    out = nc.dram_tensor("out", (B, T, C), fp32, kind="ExternalOutput").ap()
    build(nc, aps["x"], aps["lw"], aps["lb"], aps, aps, out)
    r = run_bass_kernel_spmd(nc, [arrays], core_ids=[0])
    return r.results[0]["out"]
```

```python
import numpy as np
import concourse.bass as bass
from concourse import mybir
from concourse.alu_op_type import AluOpType as ALU
from contextlib import ExitStack

fp32 = mybir.dt.float32
bf16 = mybir.dt.bfloat16
u32 = mybir.dt.uint32
ACT = mybir.ActivationFunctionType
AX = mybir.AxisListType

P = 128
B, T, C = 8, 256, 128
TT = T // P
NT = B * TT
L = 12
H = 16
HD = C // H
E, F = 8, 256
FC = F // P
GB = 4
Q4 = 4
QW = P // Q4
EPS = 1e-5
SCALE = float(np.float32(1.0) / np.sqrt(np.float32(HD)))

NS = (NT * P + (E - 1) * (P - 1)) // P
NX = NS + 2
NSLOT = 3

CBQ, CBP, CKT, CVT, CQT, CPT, CQN = 0, 1, 2, 2 + C, 2 + 2 * C, 2 + 3 * C, 2 + 4 * C
CQB = CQN + C
WCOLS = CQB
BQ = C + B


def build(nc, x_d, lw_d, lb_d, fw, consts, out_d):
    ctx = ExitStack()
    with ctx:
        def sb(name, shape, dt=fp32):
            return ctx.enter_context(nc.sbuf_tensor(name, shape, dt))

        def sem(name):
            return ctx.enter_context(nc.semaphore(name))

        X = sb("X", [P, B, TT, C])
        XT = sb("XT", [P, B, T])
        IR = sb("IR", [P, B, C])
        BR = sb("BR", [B, 2, 2 * C])
        KV = sb("KV", [P, 2 * C])
        MEAN = sb("MEAN", [P, B])
        MEAN0 = sb("MEAN0", [P, B])
        MSUM = sb("MSUM", [P, B])
        IDN = sb("IDN", [P, P])
        MASK = sb("MASK", [P, Q4, QW])
        DIAG = sb("DIAG", [B, B])
        AVG = sb("AVG", [P, P])

        arena = sb("ARENA", [P, 10752])
        at = [0]

        def piece(n, *dims):
            v = arena[:, at[0]:at[0] + n]
            at[0] += n
            names = "abcd"[:len(dims)]
            return v.rearrange(f"p ({' '.join(names)}) -> p {' '.join(names)}", **dict(zip(names, dims)))

        G = piece(B * C, B, C)
        RT = piece(B * C, B, C)
        IA = piece(2 * B * C, 2, B, C)
        U = piece(B * C, B, C)
        GV = piece(B * C, B, C)
        MF = piece(B * C, B, C)
        BT = piece(B * BQ, B, BQ)
        V8 = piece(B * C, B, C)
        WL = piece(2 * (WCOLS + B), 2, WCOLS + B)

        at[0] = 0
        HT = piece(NT * P, NT, P)
        QF = piece(NT * P, NT, P)
        QP = piece(3 * NT * P // 2, 3 * NT * P // 2).bitcast(bf16).rearrange("p (s t) -> p s t", s=3)
        KP = piece(3 * NT * P // 2, 3 * NT * P // 2).bitcast(bf16).rearrange("p (s t) -> p s t", s=3)
        KF = HT
        ON = HT
        OTS = sb("OTS", [P, 3, Q4, T])
        VT = sb("VT", [P, NT + TT, H, HD])
        VS = sb("VS", [P, NSLOT, TT, H, QW])
        PT = sb("PT", [P, 4, 2, T])
        STK = sb("STK", [P, 2, NSLOT, H, T], bf16)
        QS, KS = STK[:, 0], STK[:, 1]
        TH = sb("TH", [P, NT, P])
        X2 = sb("X2", [P, NT, C])
        NM = sb("NM", [P, NSLOT, H, TT])
        SHF = sb("SHF", [TT * H // 2, 2, P])
        SH = sb("SH", [TT * H // 2, 2, 3, P], bf16)
        RC = sb("RC", [P, 2, H])
        QW_ = {n: sb(n, [P, C]) for n in ("qw", "kw", "vw", "ow", "gw")}
        SWB = sb("SWB", [P, P])
        SWC = sb("SWC", [P, 1])
        GBH = sb("GBH", [P, 2])
        EM = sb("EM", [P, P])
        ROWS = sb("ROWS", [P, 4, C])
        MG = sb("MG", [P, E])
        ER = sb("ER", [P, 3, E])
        NH = sb("NH", [P, NT])
        ST = sb("ST", [P, NT, 6])
        MV = sb("MV", [P, NT, 2])
        VE = sb("VE", [P, NT])
        RS = sb("RS", [P, NT])

        OT = QF
        late = STK[:].rearrange("p a b c d -> p (a b c d)").bitcast(fp32)
        la = [0]

        def late_piece(n):
            la[0] += n
            return late[:, la[0] - n:la[0]]

        X2T = late_piece(NT * P)
        ACC = late_piece(NT * C).rearrange("p (n c) -> p n c", n=NT)
        XS = late_piece(4 * C).rearrange("p (u k c) -> p u k c", u=2, k=2)
        YS = late_piece(4 * C).rearrange("p (u k c) -> p u k c", u=2, k=2)
        XST = late_piece(4 * P).rearrange("p (u t) -> p u t", u=2)
        HN = late_piece(4 * F).rearrange("p (u k f) -> p u k f", u=2, k=2)
        GT = late_piece(4 * F).rearrange("p (u c t) -> p u c t", u=2, c=FC)
        W1 = sb("W1", [P, E, F])
        W2 = sb("W2", [P, E, FC, C])
        LNW = sb("LNW", [P, 2, FC, E])
        B1F = TH[0:3].rearrange("p n c -> p (n c)")
        TAKE = PT[0:3].rearrange("p a b c -> p (a b c)")
        B2F = X2[0:3, 0:E].rearrange("p n c -> p (n c)")
        B1P = sb("B1P", [P, E * F], bf16)
        B2P = sb("B2P", [P, E * C], bf16)
        ONE3 = sb("ONE3", [P, P], bf16)
        ALF = sb("ALF", [3, 2])
        ST2 = sb("ST2", [P, 2, 2, 6])
        MV2 = sb("MV2", [P, 2, 2, 2])
        VE2 = sb("VE2", [P, 2, 2])
        RS2 = sb("RS2", [P, 2, 2])
        NB = sb("NB", [P, NT])
        vals = VT[:].rearrange("p n h d -> p (n h d)")
        va = [0]

        def value_piece(n, a, b):
            va[0] += n
            return vals[:, va[0] - n:va[0]].rearrange("p (a b) -> p a b", a=a)

        RT8 = [value_piece(NT * E, NT, E) for n in range(3)]
        OH = value_piece((NT + 1) * E, NT + 1, E)
        SUMS = [value_piece((NT // 2 + NT) * E, NT // 2 + NT, E) for _ in range(2)]
        BASE = value_piece(NT * E, NT, E)
        UNIT = value_piece(P * 2, 2, P)
        SC_ = value_piece(E * NT + E * E + NX, 1, E * NT + E * E + NX)[:, 0]
        FULL = value_piece(E * NT, E, NT)
        BEFORE = value_piece(E * E, E, E)
        LATER = value_piece(NX * (E - 2), NX, E - 2)
        TILES = SC_[:, 0:E * NT].rearrange("p (e k) -> p e k", e=E)
        LOWER = SC_[:, E * NT:E * NT + E * E].rearrange("p (e d) -> p e d", e=E)
        TILE = SC_[:, E * NT + E * E:]
        NTILE, START = sb("NTILE", [P, E]), sb("START", [P, E])
        SLOT, TEXP = sb("SLOT", [P, NT]), sb("TEXP", [P, NX])
        SLOTI = sb("SLOTI", [P, NT], u32)
        TEXPI = sb("TEXPI", [P, NX], u32)
        R1 = [sb(f"R1_{n}", [P, NT]) for n in range(6)]
        RSC = sb("RSC", [P, NT])
        WS = sb("WS", [P, NT])
        SW = sb("SW", [P, NT])
        PS = ctx.enter_context(nc.psum_tensor("PS", [P, 8, 512], fp32))
        scr = nc.dram_tensor("parts", (2, H, 3, HD, (NT + TT) * P), bf16).ap()
        xs_d = nc.dram_tensor("sorted_x2", (NS * P, C), fp32).ap()
        ys_d = nc.dram_tensor("sorted_outputs", (NS * P, C), fp32).ap()
        scm = nc.dram_tensor("shifts", (NSLOT, 3, H, T), bf16).ap()

        def bank(g, k):
            return PS[:, 4 * g + k, :]

        def batches(ap):
            return ap.rearrange("p (b c) -> p b c", b=GB)

        s_const = sem("const_loaded")
        s_x = [sem(f"x_loaded_{u}") for u in range(2)]
        s_w = [sem(f"layer_weights_loaded_{u}") for u in range(2)]
        s_zero = sem("pool_constants_set")
        s_mrow = sem("mean_rows_summed")
        s_mcol = sem("mean_columns_summed")
        s_xc = sem("x_centred")
        s_gram = sem("gram_summed")
        s_xct = sem("centred_x_transposed")
        s_xt = sem("centred_xT_copied")
        s_g = sem("gram_ready")
        s_mean = sem("mean_ready")
        s_p = sem("gv_done")
        s_pc = sem("gv_copied")
        s_row = sem("mean_keys_values_done")
        s_kv = sem("mean_keys_values_copied")
        s_v8 = sem("mean_values_spread")
        s_qbd = sem("mean_queries_done")
        s_qb = sem("mean_queries_ready")
        s_k = sem("ktv_done")
        s_m = sem("ktv_masked")
        s_r = sem("rt_done")
        s_rt = sem("rt_ready")
        s_b = sem("bt_done")
        s_bt = sem("bt_copied")
        s_a = sem("a_done")
        s_ia = sem("ia_ready")
        s_ym = sem("mean_update_done")
        s_u = sem("u_done")
        s_uc = sem("u_copied")
        s_gd = sem("gram_done")
        s_out = sem("out_stored")

        s_wf = sem("ffn_weights_loaded")
        s_stk0 = sem("stack_constants_set")
        s_ir = sem("i_plus_r_ready")
        s_ms = sem("mean_sum_ready")
        s_h = sem("residual_done")
        s_htv, s_hta = sem("residual_copied_by_dve"), sem("residual_copied_by_act")
        s_tok = sem("residual_transposed")
        s_st = sem("statistics_taken")
        s_mv = sem("mean_variance_ready")
        s_ve = sem("variance_plus_eps_ready")
        s_rs = sem("rstd_ready")
        s_x1 = sem("x1_ready")
        s_x1t = sem("x1_transposed")
        s_xtc = sem("x1t_copied")
        s_q = sem("queries_done")
        s_qf = sem("queries_copied")
        s_kd = sem("keys_done")
        s_kf = sem("keys_scaled")
        s_z = sem("query_scale_done")
        s_th = sem("query_scale_tanh")
        s_v = sem("values_done")
        s_vt = sem("values_copied")
        s_qs = sem("queries_scaled")
        s_swb = sem("scale_weights_spread")
        s_q1, s_q1r, s_q2, s_q3 = (sem(f"query_{n}") for n in ("part_1", "rest_1", "part_2", "part_3"))
        s_k1, s_k1r, s_k2, s_k3 = (sem(f"key_{n}") for n in ("part_1", "rest_1", "part_2", "part_3"))
        s_scr = [sem(f"parts_stored_{u}") for u in range(2)]
        s_stk = [sem(f"stack_loaded_{u}") for u in range(NSLOT)]
        s_mxd = sem("max_scores_done")
        s_max = sem("maxima_taken")
        s_mt = sem("maxima_transposed")
        s_sha = sem("shift_part_1")
        s_shb = sem("shift_rest_1")
        s_shc = sem("shift_part_2")
        s_shd = sem("shift_part_3")
        s_shs = [sem(f"shifts_stored_{u}") for u in range(2)]
        s_shl = [sem(f"shifts_loaded_{u}") for u in range(2)]
        s_qk = sem("scores_done")
        s_exp = sem("exponentials_ready")
        s_vs = sem("batch_values_ready")
        s_pv = sem("pv_done")
        s_ot = sem("outputs_copied")
        s_tr = sem("outputs_transposed")
        s_rc = sem("sums_inverted")
        s_on = sem("outputs_normalised")
        s_we = sem("expert_weights_loaded")
        s_eb = sem("expert_biases_loaded")
        s_zb = sem("expert_bias_steps")
        s_gbh = sem("half_gate_bias_ready")
        s_ott = sem("normalised_outputs_transposed")
        s_otc = sem("transposed_outputs_copied")
        s_gt = sem("gate_done")
        s_tg = sem("gate_tanh")
        s_og = sem("gated_outputs_ready")
        s_at = sem("out_projection_done")
        s_xp = sem("attention_residual_ready")
        s_xn = sem("x2_normalised")
        s_xg = sem("x2_scaled")
        s_x2 = sem("x2_ready")
        s_x2t = sem("x2_transposed")
        s_x2c = sem("x2t_copied")
        s_lg = sem("logits_done")
        s_rch = sem("routing_steps")
        s_ed = sem("second_weight_exponential")
        s_oh = sem("routing_ready")
        s_zf = sem("sorted_rows_cleared")
        s_vsz = sem("values_cleared")
        s_sc = sem("slot_constants_loaded")
        s_pre0 = sem("tile_choices_copied")
        s_pre = sem("tile_sums_doubled")
        s_rk = sem("ranks_done")
        s_slot = sem("slots_ready")
        s_te = sem("tile_experts_ready")
        s_sct = sem("x2_scattered")
        s_xs = [sem(f"sorted_x2_loaded_{u}") for u in range(2)]
        s_xst = sem("sorted_x2_transposed")
        s_xsc = sem("sorted_x2t_copied")
        s_h1 = sem("hidden_done")
        s_st2 = sem("hidden_statistics_taken")
        s_mv2 = sem("hidden_mean_variance")
        s_ve2 = sem("hidden_variance_plus_eps")
        s_rs2 = sem("hidden_rstd")
        s_nrm = sem("hidden_normalised")
        s_td = sem("hidden_transposed")
        s_gl = sem("gelu_ready")
        s_y = sem("expert_output_done")
        s_yc = sem("expert_output_copied")
        s_ys = [sem(f"sorted_outputs_stored_{u}") for u in range(2)]
        s_got = [sem(f"outputs_gathered_{u}") for u in range(4)]
        s_nb = sem("shift_ready")
        s_wx = sem("weighted_x2_ready")
        s_xb = sem("x1_plus_bias_ready")
        s_f1, s_f2, s_f3 = (sem(f"final_{n}") for n in ("weighted", "centred", "summed"))
        s_fo = sem("output_rows_ready")
        block = ctx.enter_context(nc.Block())

        NPAIR = NS // 2
        assert NS % 2 == 0 and NPAIR % 2 == 1

        FINAL = [("expert", 0), ("expert", 1), ("block", 0), ("expert", 2), ("block", 1), ("expert", 3), ("block", 2), ("block", 3)]

        def tile_experts(engine, first, n):
            return nc.values_load_multi_w_load_instructions(
                TEXPI[0:1, bass.ds(first, n)], engines=(engine,), min_val=0, max_val=E - 2,
                skip_runtime_bounds_check_because="it counts E - 2 comparisons")[1]

        def alone(engine, semaphore, value):
            engine.wait_ge(semaphore, value)
            engine.nop(nofuse=True)

        XN = X[:].rearrange("p b t c -> p (b t) c")
        cols = lambda i: slice(4 * P * i, 4 * P * (i + 1))
        flat = lambda ap: ap.rearrange("p a c -> p (a c)")
        XTF = XT[:].rearrange("p b t -> p (b t)")
        SROW = 3 * QW
        KEXP, KMAX = SROW + 3, 2 * QW + HD

        @block.sync
        def _(sp):
            sp.dma_start(AVG[:], consts["avg"]).then_inc(s_const, 16)
            for i in range(4):
                sp.dma_start(X[:, 2 * i:2 * i + 2], x_d[2 * i:2 * i + 2].rearrange("b (p t) c -> p b t c", t=TT)).then_inc(s_x[i // 2], 16)
            sp.dma_start(IDN[:], consts["ident"]).then_inc(s_const, 16)
            sp.dma_start(MASK[:], consts["mask"]).then_inc(s_const, 16)
            sp.dma_start(DIAG[:], consts["diag"]).then_inc(s_const, 16)
            sp.dma_start(B1F, fw["b1"].broadcast_to([3, E * F])).then_inc(s_eb, 16)
            sp.dma_start(ALF[:], consts["alf"]).then_inc(s_eb, 16)
            sp.dma_start(B2F, fw["b2"].broadcast_to([3, E * C])).then_inc(s_eb, 16)
            for u in range(2):
                sp.dma_start(WL[:, u, 0:WCOLS], lw_d[u]).then_inc(s_w[u], 16)
                sp.dma_start(BR[:, u, :], lb_d[u:u + 1, :].broadcast_to([B, 2 * C])).then_inc(s_w[u], 16)
            sp.wait_ge(s_vsz, 1)
            sp.dma_start(xs_d.rearrange("(p n) c -> p (n c)", p=P), VS[:].rearrange("p a b c d -> p (a b c d)")[:, 0:NS * C]).then_inc(s_zf, 16)
            for n in range(2):
                sp.dma_start(scr[n, :, :, :, B * T:].rearrange("h s d t -> (h s d) t").rearrange("(p r) t -> p r t", r=3),
                             VS[:].rearrange("p a b c d -> p (a b c d)").bitcast(bf16)[:, 0:3 * T].rearrange("p (r t) -> p r t", r=3)).then_inc(s_zf, 16)
            with sp.Fori(0, L // 2 - 1) as i:
                for u in range(2):
                    sp.wait_ge(s_mean, 2 * i + u + 2)
                    sp.dma_start(WL[:, u, 0:WCOLS], lw_d[bass.ds(2 * i + u + 2, 1)].rearrange("l p c -> p (l c)")).then_inc(s_w[u], 16)
                    sp.dma_start(BR[:, u, :], lb_d[bass.ds(2 * i + u + 2, 1), :].broadcast_to([B, 2 * C])).then_inc(s_w[u], 16)
            for n, w in QW_.items():
                sp.dma_start(w[:], fw[n]).then_inc(s_wf, 16)
            sp.dma_start(SWC[:], fw["swc"]).then_inc(s_wf, 16)
            sp.dma_start(EM[:], consts["em"]).then_inc(s_wf, 16)
            sp.dma_start(GBH[:, 0:1], fw["gb"]).then_inc(s_we, 16)
            sp.dma_start(ROWS[:], fw["rows"].broadcast_to([P, 4 * C]).rearrange("p (r c) -> p r c", r=4)).then_inc(s_we, 16)
            sp.dma_start(ER[:], fw["er"].broadcast_to([P, 3 * E]).rearrange("p (r c) -> p r c", r=3)).then_inc(s_we, 16)
            sp.dma_start(MG[:], fw["mg"]).then_inc(s_we, 16)
            sp.dma_start(W1[:], fw["w1"]).then_inc(s_we, 16)
            sp.dma_start(W2[:], fw["w2"]).then_inc(s_we, 16)
            sp.dma_start(LNW[:], fw["lnw"]).then_inc(s_we, 16)
            def store_parts(half):
                sp.wait_ge(s_q3, 2 * half + 2)
                sp.wait_ge(s_k3, 2 * half + 2)
                t = slice(half * B // 2 * T, (half + 1) * B // 2 * T)
                for n, part in enumerate((QP, KP)):
                    for r in range(3):
                        sp.dma_start(scr[n, :, r, :, t], part[:, r, t]).then_inc(s_scr[half], 16)

            def load_queries(n, slot):
                q = scr[0, :, :, :, bass.ds(n * T, T)].rearrange("h s d t -> s d h t")
                row = 0
                for part, times in ((0, 3), (1, 2), (2, 1)):
                    for _ in range(times):
                        sp.dma_start(QS[HD * row:HD * (row + 1), slot], q[part]).then_inc(s_stk[slot], 16)
                        row += 1

            def load_keys(n, slot):
                k = scr[1, :, :, :, bass.ds(n * T, T)].rearrange("h s d t -> (s d) h t")
                row = 0
                for parts in (3, 2, 1):
                    sp.dma_start(KS[HD * row:HD * (row + parts), slot], k[0:HD * parts]).then_inc(s_stk[slot], 16)
                    row += parts

            def store_shift(n, slot, half):
                heads = slice(half * H // 2, (half + 1) * H // 2)
                sp.wait_ge(s_shd, 2 * n + half + 1)
                sp.dma_start(scm[slot, :, heads, :].rearrange("s h (q t) -> (h q) s t", q=TT), SH[:, half]).then_inc(s_shs[half], 16)

            def load_shift(n, slot, half):
                heads = slice(half * H // 2, (half + 1) * H // 2)
                sp.wait_ge(s_shs[half], 16 * (n + 1))
                sp.dma_start(QS[SROW:SROW + 3, slot, heads, :], scm[slot, :, heads, :]).then_inc(s_shl[half], 16)

            store_parts(0)
            sp.wait_ge(s_stk0, 5)
            sp.wait_ge(s_scr[0], 16 * 6)
            load_queries(0, 0)
            load_keys(0, 0)
            store_parts(1)
            load_queries(1, 1)
            load_keys(1, 1)
            store_shift(0, 0, 0)
            load_shift(0, 0, 0)
            store_shift(0, 0, 1)

            def sp_step(i, c):
                b = NSLOT * i + c
                if c > 0:
                    sp.wait_ge(s_qk, 16 * b)
                load_keys(b + 2, (c + 2) % NSLOT)
                load_shift(b, c % NSLOT, 1)
                load_queries(b + 2, (c + 2) % NSLOT)
                store_shift(b + 1, (c + 1) % NSLOT, 0)
                load_shift(b + 1, (c + 1) % NSLOT, 0)
                store_shift(b + 1, (c + 1) % NSLOT, 1)

            sp_step(0, 0)
            sp.wait_ge(s_scr[1], 16 * 6)
            with sp.Fori(0, 2) as i:
                for u in range(3):
                    sp_step(i, 1 + u)
            load_shift(7, 7 % NSLOT, 1)
            sp.wait_ge(s_vs, NSLOT + 6)
            sp.dma_start(UNIT, consts["unit"].rearrange("p (a b) -> p a b", a=2)).then_inc(s_sc, 16)
            sp.dma_start(SC_, consts["slots"].broadcast_to([P, E * NT + E * E + NX])).then_inc(s_sc, 16)
            sp.wait_ge(s_sct, 16 * NT)

            def load_sorted(m, u):
                if not isinstance(m, int) or m > 1:
                    sp.wait_ge(s_xst, m + 1 - 2)
                sp.dma_start(XS[:, u], xs_d[bass.ds(2 * m * P, 2 * P)].rearrange("(k p) c -> p k c", k=2)).then_inc(s_xs[u], 16)

            def store_outputs(m, u):
                sp.wait_ge(s_yc, m + 1)
                sp.dma_start(ys_d[bass.ds(2 * m * P, 2 * P)].rearrange("(k p) c -> p k c", k=2), YS[:, u]).then_inc(s_ys[u], 16)

            for m in range(5):
                load_sorted(m, m % 2)
            with sp.Fori(0, (NPAIR - 5) // 2) as i:
                for u in range(2):
                    load_sorted(2 * i + u + 5, 1 - u)
                    store_outputs(2 * i + u, u)
            for m in range(NPAIR - 5, NPAIR):
                store_outputs(m, m % 2)
            for i in range(4):
                sp.wait_ge(s_fo, i + 1)
                sp.dma_start(out_d[2 * i:2 * i + 2].rearrange("b (p t) c -> p b t c", t=TT),
                             ACC[:, 4 * i:4 * i + 4].rearrange("p (b t) c -> p b t c", t=TT)).then_inc(s_out, 16)
            sp.wait_ge(s_out, 64)

        @block.gpsimd
        def _(pool):
            nc.gpsimd.memset(VS[:], 0.0).then_inc(s_vsz, 1)
            nc.gpsimd.memset(KV[:], 0.0).then_inc(s_zero, 1)
            nc.gpsimd.memset(V8[:], 0.0).then_inc(s_zero, 1)
            pool.wait_ge(s_const, 64)
            nc.gpsimd.tensor_copy(RT[:], IDN[:].unsqueeze(1).broadcast_to([P, B, C])).then_inc(s_zero, 1)
            nc.gpsimd.tensor_copy(IA[:, 1], IDN[:].unsqueeze(1).broadcast_to([P, B, C])).then_inc(s_zero, 1)
            for a in (ONE3, B1P, B2P):
                nc.gpsimd.memset(a[:], 0.0).then_inc(s_zb, 1)
            pool.wait_ge(s_zb, 3)
            nc.gpsimd.memset(ONE3[0:3, :], 1.0).then_inc(s_zb, 1)
            pool.wait_ge(s_eb, 48)
            done = 4
            for full, parts in ((B1F, B1P), (B2F, B2P)):
                for r in range(3):
                    nc.gpsimd.tensor_copy(parts[0:3], full).then_inc(s_zb, 1)
                    done += 1
                    if r < 2:
                        pool.wait_ge(s_zb, done)
                        nc.gpsimd.tensor_scalar(TAKE[:, 0:full.shape[1]], parts[0:3], ALF[:, r:r + 1], None, ALU.mult).then_inc(s_zb, 1)
                        pool.wait_ge(s_zb, done + 1)
                        nc.gpsimd.tensor_tensor(full, full, TAKE[:, 0:full.shape[1]], ALU.add).then_inc(s_zb, 1)
                        pool.wait_ge(s_zb, done + 2)
                        done += 2
            nc.gpsimd.memset(NH[:], -0.5).then_inc(s_stk0, 1)
            nc.gpsimd.memset(VT[:, NT:], 0.0).then_inc(s_stk0, 1)
            nc.gpsimd.memset(STK[:].bitcast(u32), 0).then_inc(s_stk0, 1)
            pool.wait_ge(s_zf, 48)
            nc.gpsimd.memset(VS[:, :, :, :, HD:HD + 1], 1.0).then_inc(s_stk0, 1)
            pool.wait_ge(s_stk0, 4)
            nc.gpsimd.memset(KS[SROW:SROW + 3], 1.0).then_inc(s_stk0, 1)
            pool.wait_ge(s_stk0, 5)
            def rstd(i):
                t = slice(4 * i, 4 * i + 4)
                pool.wait_ge(s_mv, i + 1)
                nc.gpsimd.tensor_scalar(VE[:, t], MV[:, t, 1], EPS, None, ALU.add).then_inc(s_ve, 1)
                pool.wait_ge(s_ve, i + 1)
                nc.gpsimd.tensor_tensor(RS[:, t], VE[:, t], NH[:, t], ALU.pow).then_inc(s_rs, 1)

            for i in range(4):
                rstd(i)
            for half in range(2):
                for i in (2 * half, 2 * half + 1):
                    k, c = flat(KF)[:, cols(i)], cols(i)
                    pool.wait_ge(s_k1, i + 1)
                    nc.gpsimd.tensor_tensor(k, k, KP[:, 0, c], ALU.subtract).then_inc(s_k1r, 1)
                for i in (2 * half, 2 * half + 1):
                    k, c = flat(KF)[:, cols(i)], cols(i)
                    pool.wait_ge(s_k2, i + 1)
                    nc.gpsimd.tensor_tensor(KP[:, 2, c], k, KP[:, 1, c], ALU.subtract).then_inc(s_k3, 1)

            def batch_values(b, slot):
                nc.gpsimd.tensor_copy(VS[:, slot, :, :, 0:HD], VT[:, bass.ds(b * TT, TT)]).then_inc(s_vs, 1)

            def shift_parts(n, half, first=False):
                m = 2 * n + half
                pool.wait_ge(s_shb, m + 1)
                if not first:
                    alone(pool, s_shs[half], 16 * n)
                else:
                    pool.wait_ge(s_vs, NSLOT)
                nc.gpsimd.tensor_copy(SH[:, half, 1], SHF[:, half]).then_inc(s_shc, 1)
                pool.wait_ge(s_shc, m + 1)
                nc.gpsimd.tensor_tensor(SH[:, half, 2], SHF[:, half], SH[:, half, 1], ALU.subtract).then_inc(s_shd, 1)

            pool.wait_ge(s_vt, 4)
            for b in range(NSLOT):
                batch_values(b, b)
            for half in range(2):
                shift_parts(0, half, True)

            def pool_step(i, c):
                b = NSLOT * i + c
                if c > 0:
                    pool.wait_ge(s_pv, 8 * b)
                    alone(pool, s_shd, 2 * b + 2)
                    batch_values(b + 2, (c + 2) % NSLOT)
                    pool.wait_ge(s_vs, b + 3)
                for half in range(2):
                    shift_parts(b + 1, half)

            pool_step(0, 0)
            with pool.Fori(0, 2) as i:
                for u in range(3):
                    pool_step(i, 1 + u)

            for i in range(4):
                pool.wait_ge(s_shd, 16)
                t = slice(4 * i, 4 * i + 4)
                pool.wait_ge(s_mv, i + 5)
                nc.gpsimd.tensor_scalar(VE[:, t], MV[:, t, 1], EPS, None, ALU.add).then_inc(s_ve, 1)
                pool.wait_ge(s_ve, i + 5)
                nc.gpsimd.tensor_tensor(RS[:, t], VE[:, t], NH[:, t], ALU.pow).then_inc(s_rs, 1)
            nc.gpsimd.tensor_tensor(XN, XN, ROWS[:, 3, :].unsqueeze(1).broadcast_to([P, NT, C]), ALU.add).then_inc(s_xb, 1)
            pool.wait_ge(s_slot, 1)
            for n in range(NT):
                nc.gpsimd.indirect_dma_start(xs_d, bass.IndirectOffsetOnAxis(SLOTI[:, n:n + 1], 0), X2[:, n, :], None).then_inc(s_sct, 16)

            def hidden_rstd(m, u):
                alone(pool, s_mv2, m + 1)
                nc.gpsimd.tensor_scalar(VE2[:, u], MV2[:, u, :, 1], EPS, None, ALU.add).then_inc(s_ve2, 1)
                alone(pool, s_ve2, m + 1)
                nc.gpsimd.tensor_tensor(RS2[:, u], VE2[:, u], NH[:, 0:2], ALU.pow).then_inc(s_rs2, 1)

            with pool.Fori(0, NPAIR // 2) as i:
                for u in range(2):
                    hidden_rstd(2 * i + u, u)
            hidden_rstd(NPAIR - 1, 0)

            def gather(i):
                for n in range(4 * i, 4 * i + 4):
                    nc.gpsimd.indirect_dma_start(ACC[:, n, :], None, ys_d, bass.IndirectOffsetOnAxis(SLOTI[:, n:n + 1], 0)).then_inc(s_got[i], 16)

            def late_rstd(k):
                part, i = FINAL[k]
                t = slice(4 * i, 4 * i + 4)
                pool.wait_ge(s_mv, 8 + k + 1)
                nc.gpsimd.tensor_scalar(VE[:, t], MV[:, t, 1], EPS, None, ALU.add).then_inc(s_ve, 1)
                pool.wait_ge(s_ve, 8 + k + 1)
                nc.gpsimd.tensor_tensor(RS[:, t], VE[:, t], NH[:, t], ALU.pow).then_inc(s_rs, 1)
                if part == "block":
                    pool.wait_ge(s_rs, 8 + k + 1)
                    nc.gpsimd.tensor_tensor(VE[:, t], MV[:, t, 0], RS[:, t], ALU.mult).then_inc(s_nb, 1)
                    pool.wait_ge(s_nb, 2 * i + 1)
                    nc.gpsimd.tensor_scalar(NB[:, t], VE[:, t], -1.0, None, ALU.mult).then_inc(s_nb, 1)

            for u in range(2):
                pool.wait_ge(s_ys[u], 16 + 16 * ((NPAIR + 1 - u) // 2))
            gather(0)
            gather(1)
            late_rstd(0)
            gather(2)
            late_rstd(1)
            gather(3)
            for k in range(2, 8):
                late_rstd(k)

        @block.tensor
        def _(pe):
            mm = nc.tensor.matmul
            pe.wait_ge(s_const, 64)
            for g in range(2):
                pe.wait_ge(s_x[g], 32)
                for t in range(TT):
                    last = mm(batches(bank(g, 0)), AVG[:], X[:, GB * g:GB * (g + 1), t, :], start=t == 0, stop=t == TT - 1)
                last.then_inc(s_mrow, 1)
                for b in range(GB):
                    for t in range(TT):
                        last = mm(bank(g, 1)[:, b:b + 1], X[:, GB * g + b, t, :], AVG[:, 0:1], start=t == 0, stop=t == TT - 1)
                last.then_inc(s_mcol, 1)
            for g in range(2):
                pe.wait_ge(s_xc, 2 * g + 2)
                for b in range(GB):
                    xb = X[:, GB * g + b]
                    for t in range(TT):
                        last = mm(bank(g, 2)[:, b * C:(b + 1) * C], xb[:, t, :], xb[:, t, :], start=t == 0, stop=t == TT - 1)
                last.then_inc(s_gram, 1)
            for i, (g, k) in enumerate(((0, 3), (1, 3), (0, 0), (1, 0))):
                for j in range(2 * TT):
                    last = nc.tensor.transpose(bank(g, k)[:, j * P:(j + 1) * P], X[:, 2 * i + j // TT, j % TT, :], IDN[:])
                last.then_inc(s_xct, 1)
            pe.wait_ge(s_xt, 4)
            pe.wait_ge(s_zero, 5)
            def rt_product(l, u, g):
                if g == 0:
                    pe.wait_ge(s_kv, l + 1)
                else:
                    pe.wait_ge(s_qb, l + 1)
                pe.wait_ge(s_rt, 2 * l + g + 1)
                for n in range(GB * g, GB * (g + 1)):
                    last = mm(bank(g, 3)[:, (n % GB) * C:(n % GB + 1) * C], IA[:, 1 - u, n, :], RT[:, n, :], start=True, stop=True)
                last.then_inc(s_r, 1)

            with pe.Fori(0, L // 2) as i:
                for u in range(2):
                    l = 2 * i + u
                    W = WL[:, u]
                    pe.wait_ge(s_w[u], 32 * i + 32)
                    pe.wait_ge(s_mean, l + 1)
                    mm(bank(0, 3)[0:B, 0:2 * C], MEAN[:], W[:, CKT:CKT + 2 * C], start=True, stop=True).then_inc(s_row, 1)
                    mm(bank(1, 3)[:, 0:B], W[:, CQT:CQT + C], MEAN[:], start=True, stop=True).then_inc(s_qbd, 1)
                    for g in range(2):
                        pe.wait_ge(s_g, 2 * l + g + 1)
                        for b in range(GB):
                            last = mm(bank(g, 0)[:, b * C:(b + 1) * C], G[:, GB * g + b, :], W[:, CVT:CVT + C], start=True, stop=True)
                        last.then_inc(s_p, 1)
                    rt_product(l, u, 0)
                    for g in range(2):
                        pe.wait_ge(s_pc, 2 * l + g + 1)
                        pe.wait_ge(s_v8, 2 * l + g + 1)
                        for q in range(Q4):
                            quad = slice(QW * q, QW * (q + 1))
                            out = bank(g, 2)[quad, 0:GB * QW].rearrange("p (b j) -> p b j", b=GB)
                            mm(out, W[:, CKT + QW * q:CKT + QW * (q + 1)], GV[:, GB * g:GB * (g + 1), quad], start=True, stop=False)
                            last = mm(out, KV[:, quad], V8[:, GB * g:GB * (g + 1), quad], start=False, stop=True)
                        last.then_inc(s_k, 1)
                    rt_product(l, u, 1)
                    for g in range(2):
                        pe.wait_ge(s_m, 2 * l + g + 1)
                        for b in range(GB):
                            o = (b % 2) * BQ
                            last = mm(bank(g, b // 2)[:, o:o + BQ], MF[:, GB * g + b, :], W[:, CQN:CQN + BQ], start=True, stop=True)
                        last.then_inc(s_b, 1)
                    for g in range(2):
                        pe.wait_ge(s_bt, 2 * l + g + 1)
                        for b in range(GB):
                            last = mm(bank(g, 2)[:, b * C:(b + 1) * C], BT[:, GB * g + b, 0:C], W[:, CPT:CPT + C], start=True, stop=True)
                        last.then_inc(s_a, 1)
                    for g in range(2):
                        n = GB * g
                        own = BT[:].rearrange("p b c -> p (b c)")[:, n * BQ + C + n::BQ + 1][:, 0:GB]
                        mm(bank(g, 0)[:, 0:GB], W[:, CPT:CPT + C], own, start=True, stop=True).then_inc(s_ym, 1)
                    for g in range(2):
                        pe.wait_ge(s_ia, 2 * l + g + 1)
                        pe.wait_ge(s_rt, 2 * l + g + 3)
                        for b in range(GB):
                            n = GB * g + b
                            last = mm(bank(g, 3)[:, b * C:(b + 1) * C], G[:, n, :], IA[:, u, n, :], start=True, stop=True)
                        last.then_inc(s_u, 1)
                    for g in range(2):
                        pe.wait_ge(s_uc, 2 * l + g + 1)
                        for b in range(GB):
                            n = GB * g + b
                            last = mm(bank(g, 1)[:, b * C:(b + 1) * C], IA[:, u, n, :], U[:, n, :], start=True, stop=True)
                        last.then_inc(s_gd, 1)
            for g in range(2):
                for b in range(GB):
                    n = GB * g + b
                    last = mm(bank(g, 3)[:, b * C:(b + 1) * C], RT[:, n, :], IA[:, 1, n, :], start=True, stop=True)
                last.then_inc(s_r, 1)

            pe.wait_ge(s_ir, 2)
            for i in range(4):
                for b in (2 * i, 2 * i + 1):
                    last = mm(PS[:, i, (b % 2) * T:(b % 2 + 1) * T], IR[:, b, :], XT[:, b, :], start=True, stop=True)
                last.then_inc(s_h, 1)
            for i in range(4):
                pe.wait_ge((s_htv, s_hta)[i % 2], i // 2 + 1)
                for k in range(4):
                    last = nc.tensor.transpose(PS[:, 4 + i, k * P:(k + 1) * P], HT[:, 4 * i + k, :], IDN[:])
                last.then_inc(s_tok, 1)
            for i in range(4):
                pe.wait_ge(s_x1, i + 1)
                for k in range(4):
                    last = nc.tensor.transpose(PS[:, i, k * P:(k + 1) * P], XN[:, 4 * i + k, :], IDN[:])
                last.then_inc(s_x1t, 1)
            pe.wait_ge(s_wf, 16 * 7)
            for half in range(2):
                for i in (2 * half, 2 * half + 1):
                    pe.wait_ge(s_xtc, i + 1)
                    mm(PS[:, 4 + i, :], QW_["qw"][:], XTF[:, cols(i)], start=True, stop=True).then_inc(s_q, 1)
                    mm(PS[:, i, :], QW_["kw"][:], XTF[:, cols(i)], start=True, stop=True).then_inc(s_kd, 1)
                if half == 0:
                    pe.wait_ge(s_swb, 1)
                for i in (2 * half, 2 * half + 1):
                    pe.wait_ge(s_qf, i + 1)
                    mm(PS[:, 4 + i, :], SWB[:], flat(QF)[:, cols(i)], start=True, stop=True).then_inc(s_z, 1)
            for i in range(4):
                pe.wait_ge(s_kf, i + 1)
                for k in range(4):
                    last = mm(PS[:, i, k * P:(k + 1) * P], XTF[:, (4 * i + k) * P:(4 * i + k + 1) * P], QW_["vw"][:], start=True, stop=True)
                last.then_inc(s_v, 1)

            def max_scores(M, j, slot, loaded):
                pe.wait_ge(s_stk[slot], 144 * loaded)
                if M is not None:
                    pe.wait_ge(s_max, M - 1)
                for k in range(4):
                    h = 4 * (j // 2) + k
                    last = mm(PS[:, 2 * (j % 2) + k // 2, (k % 2) * T:(k % 2 + 1) * T],
                              QS[0:KMAX, slot, h, (j % 2) * P:(j % 2 + 1) * P], KS[0:KMAX, slot, h, :], start=True, stop=True)
                last.then_inc(s_mxd, 1)

            def shift_rows(n, half, slot):
                pe.wait_ge(s_max, 8 * n + 4 * half + 4)
                nm = NM[:, slot, half * H // 2:(half + 1) * H // 2, :].rearrange("p h q -> p (h q)")
                nc.tensor.transpose(PS[0:H, 7, 0:P], nm, IDN[:]).then_inc(s_mt, 1)

            def pv(b, j, slot, first):
                if j == 0:
                    pe.wait_ge(s_vs, b + 1)
                pe.wait_ge(s_exp, 16 * b + 2 * j + 2)
                if j % 2 == 0 and not (first and j == 0):
                    pe.wait_ge(s_ot, 4 * b + j // 2)
                for k in range(4):
                    last = mm(PS[QW * k:QW * (k + 1), 6, 0:T], VS[:, slot, j % 2, 4 * (j // 2) + k, :],
                              PT[:, (2 * j + k // 2) % 4, k % 2, :], start=j % 2 == 0, stop=j % 2 == 1)
                last.then_inc(s_pv, 1)

            def out_tokens(b, qt, slot):
                pe.wait_ge(s_ot, 4 * b + 4)
                for g in range(Q4):
                    last = nc.tensor.transpose(PS[:, 7, g * P:(g + 1) * P], OTS[:, slot, g, qt * P:(qt + 1) * P], IDN[:])
                last.then_inc(s_tr, 1)

            pe.wait_ge(s_vt, 4)
            for j in range(8):
                max_scores(j if j > 1 else None, j, 0, 1)
                if j == 5:
                    shift_rows(0, 0, 0)
            pe.wait_ge(s_shb, 1)
            shift_rows(0, 1, 0)
            for j in range(2):
                max_scores(8 + j, j, 1, 1)

            def pe_step(i, c, first=False, last=False):
                b, r = NSLOT * i + c, c % NSLOT
                for j in range(8):
                    if not last:
                        a = c + (1 if j < 6 else 2)
                        max_scores(8 * b + j + 10, (j + 2) % 8, a % NSLOT, i + a // NSLOT + 1)
                    if j % 4 == 0:
                        pe.wait_ge(s_shl[j // 4], 16 * b + 16)
                    for k in (0, 1):
                        if not (first and j == 0):
                            pe.wait_ge(s_exp, 16 * b + 2 * j + k - 1)
                        for hh in (0, 1):
                            h = 4 * (j // 2) + 2 * k + hh
                            o = mm(PS[:, 4 + k, hh * T:(hh + 1) * T], KS[0:KEXP, r, h, (j % 2) * P:(j % 2 + 1) * P],
                                   QS[0:KEXP, r, h, :], start=True, stop=True)
                        o.then_inc(s_qk, 1)
                    if j > 0:
                        pv(b, j - 1, r, first)
                    elif not first:
                        pv(b - 1, 7, (c - 1) % NSLOT, False)
                    if j == 2 and not last:
                        pe.wait_ge(s_shb, 2 * b + 2)
                        shift_rows(b + 1, 0, (c + 1) % NSLOT)
                    if j == 3 and not first:
                        pe.wait_ge(s_shb, 16 if last else 2 * b + 3)
                        out_tokens(b - 1, 0, (c - 1) % NSLOT)
                    if j == 5 and not first:
                        pe.wait_ge(s_on, 2 * b - 1)
                        out_tokens(b - 1, 1, (c - 1) % NSLOT)
                    if j == 6 and not last:
                        if first:
                            pe.wait_ge(s_shb, 3)
                        else:
                            pe.wait_ge(s_on, 2 * b)
                        shift_rows(b + 1, 1, (c + 1) % NSLOT)

            pe_step(0, 0, first=True)
            with pe.Fori(0, 2) as i:
                for u in range(3):
                    pe_step(i, 1 + u)
            pe_step(0, 7, last=True)
            pv(7, 7, 7 % NSLOT, False)
            for qt in range(TT):
                pe.wait_ge(s_on, 14 + qt)
                out_tokens(7, qt, 7 % NSLOT)

            pe.wait_ge(s_on, 16)
            pe.wait_ge(s_max, 66)
            for i in range(4):
                for k in range(4):
                    last = nc.tensor.transpose(PS[:, i, k * P:(k + 1) * P], ON[:, 4 * i + k, :], IDN[:])
                last.then_inc(s_ott, 1)
            for i in range(4):
                pe.wait_ge(s_otc, i + 1)
                mm(PS[:, 4 + i, :], QW_["gw"][:], flat(OT)[:, cols(i)], start=True, stop=True).then_inc(s_gt, 1)
            for i in range(4):
                pe.wait_ge(s_og, i + 1)
                for k in range(4):
                    last = mm(PS[:, i, k * P:(k + 1) * P], OT[:, 4 * i + k, :], QW_["ow"][:], start=True, stop=True)
                last.then_inc(s_at, 1)
            pe.wait_ge(s_we, 16 * 7)
            for i in range(5):
                if i < 4:
                    pe.wait_ge(s_x2, i + 1)
                    for k in range(4):
                        last = nc.tensor.transpose(PS[:, 4 + i, k * P:(k + 1) * P], X2[:, 4 * i + k, :], IDN[:])
                    last.then_inc(s_x2t, 1)
                if i > 0:
                    pe.wait_ge(s_x2c, i)
                    for n in range(4 * i - 4, 4 * i):
                        last = mm(PS[:, 0, n * E:(n + 1) * E], X2T[:, n * P:(n + 1) * P], MG[:], start=True, stop=True)
            last.then_inc(s_lg, 1)

            pe.wait_ge(s_sc, 32)
            pe.wait_ge(s_oh, 1)
            rank = PS[:, 1, 0:(NT + 1) * E].rearrange("p (n e) -> p n e", e=E)
            mm(rank, UNIT[:, 0], OH, start=True, stop=False)
            pe.wait_ge(s_pre, 4)
            mm(rank, UNIT[:, 1], SUMS[1][:, NT // 2 - 1:], start=False, stop=True).then_inc(s_rk, 1)

            def turn_x(h, u):
                pe.wait_ge(s_xs[u], 16 * h + 16)
                for k in range(2):
                    last = nc.tensor.transpose(PS[:, 4 + u, k * P:(k + 1) * P], XS[:, u, k], IDN[:])
                last.then_inc(s_xst, 1)

            def hidden(m, u, x):
                pe.wait_ge(s_xsc, m + 1)
                for k in range(2):
                    out = PS[:, u, k * F:(k + 1) * F]
                    mm(out, ONE3[:], B1P[:, bass.ds(x[k] * F, F)], start=True, stop=False)
                    last = mm(out, XST[:, u, k * P:(k + 1) * P], W1[:, bass.ds(x[k], 1), :].rearrange("p o f -> p (o f)"),
                              start=False, stop=True)
                last.then_inc(s_h1, 1)

            def turn_hidden(m, u):
                pe.wait_ge(s_nrm, m + 1)
                for c in range(FC):
                    for k in range(2):
                        last = nc.tensor.transpose(PS[:, 2 + u, (2 * c + k) * P:(2 * c + k + 1) * P], HN[:, u, k, c * P:(c + 1) * P], IDN[:])
                last.then_inc(s_td, 1)

            def output(m, u, x):
                pe.wait_ge(s_gl, m + 1)
                for k in range(2):
                    out = PS[:, 6 + u, k * C:(k + 1) * C]
                    mm(out, ONE3[:], B2P[:, bass.ds(x[k] * C, C)], start=True, stop=False)
                    for c in range(FC):
                        last = mm(out, GT[:, u, c, k * P:(k + 1) * P], W2[:, bass.ds(x[k], 1), c, :].rearrange("p o c -> p (o c)"),
                                  start=False, stop=c == FC - 1)
                last.then_inc(s_y, 1)

            pe.wait_ge(s_zb, 18)
            pe.wait_ge(s_te, 1)
            x = tile_experts(mybir.EngineType.PE, 0, 4)
            turn_x(0, 0)
            turn_x(0, 1)
            hidden(0, 0, x[0:2])
            turn_x(1, 0)
            hidden(1, 1, x[2:4])
            turn_hidden(0, 0)
            with pe.Fori(0, NPAIR // 2 - 1) as i:
                x = tile_experts(mybir.EngineType.PE, 4 * i, 8)
                for u in range(2):
                    m = 2 * i + u
                    turn_x(i + 1 + u, 1 - u)
                    hidden(m + 2, u, x[4 + 2 * u:6 + 2 * u])
                    turn_hidden(m + 1, 1 - u)
                    output(m, u, x[2 * u:2 * u + 2])
            m = NPAIR - 3
            x = tile_experts(mybir.EngineType.PE, 2 * m, 6)
            hidden(m + 2, 0, x[4:6])
            turn_hidden(m + 1, 1)
            output(m, 0, x[0:2])
            turn_hidden(m + 2, 0)
            output(m + 1, 1, x[2:4])
            output(m + 2, 0, x[4:6])

        @block.scalar
        def _(act):
            copy = lambda out, in_: nc.scalar.activation(out, in_, ACT.Copy)
            for i, (g, k) in enumerate(((0, 3), (1, 3), (0, 0), (1, 0))):
                act.wait_ge(s_xct, i + 1)
                copy(XT[:, 2 * i:2 * i + 2, :], bank(g, k).rearrange("p (b t) -> p b t", b=2)).then_inc(s_xt, 1)
            act.wait_ge(s_zero, 5)
            nc.scalar.copy(MSUM[:, 0:1], IDN[:, 0:1]).then_inc(s_rt, 1)
            nc.scalar.copy(MSUM[:, 1:2], IDN[:, 0:1]).then_inc(s_rt, 1)
            with act.Fori(0, L) as l:
                for g in range(2):
                    act.wait_ge(s_p, 2 * l + g + 1)
                    copy(GV[:, GB * g:GB * (g + 1), :], batches(bank(g, 0))).then_inc(s_pc, 1)
                for g in range(2):
                    act.wait_ge(s_r, 2 * l + g + 1)
                    copy(RT[:, GB * g:GB * (g + 1), :], batches(bank(g, 3))).then_inc(s_rt, 1)
                for g in range(2):
                    act.wait_ge(s_b, 2 * l + g + 1)
                    copy(BT[:, GB * g:GB * (g + 1), :].rearrange("p (k b) c -> p k (b c)", k=2),
                         PS[:, 4 * g:4 * g + 2, 0:2 * BQ]).then_inc(s_bt, 1)
                for g in range(2):
                    act.wait_ge(s_u, 2 * l + g + 1)
                    copy(U[:, GB * g:GB * (g + 1), :], batches(bank(g, 3))).then_inc(s_uc, 1)

            pe_bias = lambda i: MSUM[:, 2 * i:2 * i + 1]
            act.wait_ge(s_ms, 1)
            for i in (1, 3):
                act.wait_ge(s_h, i + 1)
                for b in (2 * i, 2 * i + 1):
                    o = nc.scalar.activation(flat(HT)[:, b * T:(b + 1) * T], PS[:, i, (b % 2) * T:(b % 2 + 1) * T],
                                             ACT.Identity, bias=MSUM[:, b:b + 1])
                o.then_inc(s_hta, 1)
            for i in range(4):
                act.wait_ge(s_x1t, i + 1)
                copy(XTF[:, cols(i)], PS[:, i, :]).then_inc(s_xtc, 1)
            for half in range(2):
                two = (2 * half, 2 * half + 1)
                for i in two:
                    act.wait_ge(s_kd, i + 1)
                    nc.scalar.activation(flat(KF)[:, cols(i)], PS[:, i, :], ACT.Copy, scale=SCALE).then_inc(s_kf, 1)
                for i in two:
                    act.wait_ge(s_kf, i + 1)
                    copy(KP[:, 0, cols(i)], flat(KF)[:, cols(i)]).then_inc(s_k1, 1)
                for i in two:
                    act.wait_ge(s_z, i + 1)
                    nc.scalar.activation(flat(TH[:])[:, cols(i)], PS[:, 4 + i, :], ACT.Tanh, scale=0.5).then_inc(s_th, 1)
                for i in two:
                    act.wait_ge(s_k1r, i + 1)
                    copy(KP[:, 1, cols(i)], flat(KF)[:, cols(i)]).then_inc(s_k2, 1)
                    act.wait_ge(s_qs, i + 1)
                    copy(QP[:, 0, cols(i)], flat(QF)[:, cols(i)]).then_inc(s_q1, 1)
                for i in two:
                    act.wait_ge(s_q1r, i + 1)
                    copy(QP[:, 1, cols(i)], flat(QF)[:, cols(i)]).then_inc(s_q2, 1)

            def copy_out(b, g, slot):
                act.wait_ge(s_pv, 8 * b + 2 * g + 2)
                copy(OTS[:, slot, g, :], PS[:, 6, 0:T]).then_inc(s_ot, 1)

            def act_step(i, c, first=False):
                b, r = NSLOT * i + c, c % NSLOT
                for j in range(8):
                    for k in (0, 1):
                        act.wait_ge(s_qk, 16 * b + 2 * j + k + 1)
                        if not (first and j < 2):
                            act.wait_ge(s_pv, 8 * b + j - 1)
                        nc.scalar.activation(PT[:, (2 * j + k) % 4], PS[:, 4 + k, :].rearrange("p (h t) -> p h t", h=2),
                                             ACT.Exp).then_inc(s_exp, 1)
                    if j % 2 == 0 and j > 0:
                        copy_out(b, j // 2 - 1, r)
                    elif j == 0 and not first:
                        copy_out(b - 1, 3, (c - 1) % NSLOT)

            act_step(0, 0, first=True)
            with act.Fori(0, 2) as i:
                for u in range(3):
                    act_step(i, 1 + u)
            act_step(0, 7)
            copy_out(7, 3, 7 % NSLOT)

            for i in range(4):
                act.wait_ge(s_ott, i + 1)
                copy(flat(OT)[:, cols(i)], PS[:, i, :]).then_inc(s_otc, 1)
            act.wait_ge(s_gbh, 1)
            for i in range(4):
                act.wait_ge(s_gt, i + 1)
                nc.scalar.activation(flat(TH[:])[:, cols(i)], PS[:, 4 + i, :], ACT.Tanh, scale=0.5, bias=GBH[:, 1:2]).then_inc(s_tg, 1)
            for i in range(4):
                act.wait_ge(s_x2t, i + 1)
                copy(X2T[:, cols(i)], PS[:, 4 + i, :]).then_inc(s_x2c, 1)
            act.wait_ge(s_rch, 12)
            nc.scalar.activation(R1[5][:], R1[4][:], ACT.Exp).then_inc(s_ed, 1)

            def gelu(m, u, x):
                alone(act, s_td, m + 1)
                for k in range(2):
                    for c in range(FC):
                        o = nc.scalar.activation(GT[:, u, c, k * P:(k + 1) * P], PS[:, 2 + u, (2 * c + k) * P:(2 * c + k + 1) * P], ACT.Gelu,
                                                 scale=LNW[:, 0, c, bass.ds(x[k], 1)], bias=LNW[:, 1, c, bass.ds(x[k], 1)])
                o.then_inc(s_gl, 1)

            def copy_output(h, u, m):
                act.wait_ge(s_ys[u], 16 * h + 16)
                act.wait_ge(s_y, m + 1)
                copy(YS[:, u].rearrange("p k c -> p (k c)"), PS[:, 6 + u, 0:2 * C]).then_inc(s_yc, 1)

            for u in range(2):
                nc.scalar.copy(RC[:, u, 0:1], IDN[:, 0:1]).then_inc(s_ys[u], 16)
            nc.scalar.activation(RC[:, 1, 1:2], IDN[:, 0:1], ACT.Gelu)
            act.wait_ge(s_te, 1)
            gelu(0, 0, tile_experts(mybir.EngineType.Activation, 0, 2))
            with act.Fori(0, NPAIR // 2) as i:
                x = tile_experts(mybir.EngineType.Activation, 4 * i, 8)
                for u in range(2):
                    m = 2 * i + 1 + u
                    gelu(m, 1 - u, x[2 + 2 * u:4 + 2 * u])
                    copy_output(i, u, m - 1)
            copy_output(NPAIR // 2, 0, NPAIR - 1)
            for i in range(4):
                act.wait_ge(s_nb, 2 * i + 2)
                for n in range(4 * i, 4 * i + 4):
                    o = nc.scalar.activation(ACC[:, n, :], ACC[:, n, :], ACT.Identity, scale=RS[:, n:n + 1], bias=NB[:, n:n + 1])
                o.then_inc(s_fo, 1)

        @block.vector
        def _(dve):
            tt = nc.vector.tensor_tensor
            for g in range(2):
                dve.wait_ge(s_mrow, g + 1)
                for t in range(TT):
                    xg = X[:, GB * g:GB * (g + 1), t, :]
                    if t == 0:
                        dve.wait_ge(s_mcol, g + 1)
                    tt(xg, xg, batches(bank(g, 0)), ALU.subtract).then_inc(s_xc, 1)
            for M, done in ((MEAN0, s_zero), (MEAN, s_mean)):
                for g in range(2):
                    o = nc.vector.tensor_copy(M[:, GB * g:GB * (g + 1)], bank(g, 1)[:, 0:GB])
                o.then_inc(done, 1)
            for g in range(2):
                dve.wait_ge(s_gram, g + 1)
                nc.vector.tensor_copy(G[:, GB * g:GB * (g + 1), :], batches(bank(g, 2))).then_inc(s_g, 1)
            dve.wait_ge(s_zero, 5)
            with dve.Fori(0, L // 2) as i:
                for u in range(2):
                    l = 2 * i + u
                    dve.wait_ge(s_row, l + 1)
                    tt(KV[0:B, :], bank(0, 3)[0:B, 0:2 * C], BR[:, u, :], ALU.add).then_inc(s_kv, 1)
                    dve.wait_ge(s_qbd, l + 1)
                    nc.vector.tensor_scalar(WL[:, u, CQB:CQB + B], bank(1, 3)[:, 0:B], WL[:, u, CBQ:CBQ + 1], None, ALU.add).then_inc(s_qb, 1)
                    dve.wait_ge(s_kv, l + 1)
                    for g in range(2):
                        tt(V8[0:B, GB * g:GB * (g + 1)], KV[0:B, C:].unsqueeze(1).broadcast_to([B, GB, C]),
                           DIAG[:, GB * g:GB * (g + 1)].unsqueeze(2).broadcast_to([B, GB, C]), ALU.mult).then_inc(s_v8, 1)
                    for g in range(2):
                        dve.wait_ge(s_k, 2 * l + g + 1)
                        tt(MF[:, GB * g:GB * (g + 1), :].rearrange("p b (q j) -> p b q j", q=Q4),
                           bank(g, 2)[:, 0:GB * QW].rearrange("p (b j) -> p b j", b=GB).unsqueeze(2).broadcast_to([P, GB, Q4, QW]),
                           MASK[:].unsqueeze(1).broadcast_to([P, GB, Q4, QW]), ALU.mult).then_inc(s_m, 1)
                    for g in range(2):
                        dve.wait_ge(s_a, 2 * l + g + 1)
                        tt(IA[:, u, GB * g:GB * (g + 1), :], batches(bank(g, 2)),
                           IDN[:].unsqueeze(1).broadcast_to([P, GB, C]), ALU.add).then_inc(s_ia, 1)
                    for g in range(2):
                        dve.wait_ge(s_ym, 2 * l + g + 1)
                        m = MEAN[:, GB * g:GB * (g + 1)]
                        o = nc.vector.scalar_tensor_tensor(m, bank(g, 0)[:, 0:GB], WL[:, u, CBP:CBP + 1], m, ALU.add, ALU.add)
                    o.then_inc(s_mean, 1)
                    for g in range(2):
                        dve.wait_ge(s_gd, 2 * l + g + 1)
                        nc.vector.tensor_copy(G[:, GB * g:GB * (g + 1), :], batches(bank(g, 1))).then_inc(s_g, 1)
            for g in range(2):
                dve.wait_ge(s_r, 2 * L + g + 1)
                tt(IR[:, GB * g:GB * (g + 1), :], batches(bank(g, 3)),
                   IDN[:].unsqueeze(1).broadcast_to([P, GB, C]), ALU.add).then_inc(s_ir, 1)
            dve.wait_ge(s_mean, L + 1)
            tt(MSUM[:], MEAN[:], MEAN0[:], ALU.add).then_inc(s_ms, 1)
            dve.wait_ge(s_ms, 1)
            for i in (0, 2):
                dve.wait_ge(s_h, i + 1)
                for b in (2 * i, 2 * i + 1):
                    o = nc.vector.tensor_scalar(flat(HT)[:, b * T:(b + 1) * T], PS[:, i, (b % 2) * T:(b % 2 + 1) * T],
                                                MSUM[:, b:b + 1], None, ALU.add)
                o.then_inc(s_htv, 1)
            dve.wait_ge(s_wf, 16 * 7)
            nc.vector.tensor_scalar(SWB[:], EM[:], SWC[:, 0:1], None, ALU.mult).then_inc(s_swb, 1)

            def statistics(src, i, k0):
                for k in range(4):
                    o = nc.vector.bn_stats(ST[:, 4 * i + k, :], src(k))
                o.then_inc(s_st, 1)
                dve.wait_ge(s_st, k0 + i + 1)
                for k in range(4):
                    o = nc.vector.bn_aggr(MV[:, 4 * i + k, :], ST[:, 4 * i + k, :])
                o.then_inc(s_mv, 1)

            for i in range(4):
                dve.wait_ge(s_tok, i + 1)
                statistics(lambda k: PS[:, 4 + i, k * P:(k + 1) * P], i, 0)
            for i in range(4):
                dve.wait_ge(s_rs, i + 1)
                for k in range(4):
                    n = 4 * i + k
                    o = nc.vector.tensor_scalar(XN[:, n, :], PS[:, 4 + i, k * P:(k + 1) * P], MV[:, n, 0:1], RS[:, n:n + 1],
                                                ALU.subtract, ALU.mult)
                o.then_inc(s_x1, 1)
            for half in range(2):
                two = (2 * half, 2 * half + 1)
                for i in two:
                    dve.wait_ge(s_q, i + 1)
                    nc.vector.tensor_copy(flat(QF)[:, cols(i)], PS[:, 4 + i, :]).then_inc(s_qf, 1)
                for i in two:
                    q = flat(QF)[:, cols(i)]
                    dve.wait_ge(s_th, i + 1)
                    nc.vector.scalar_tensor_tensor(q, flat(TH[:])[:, cols(i)], 1.0, q, ALU.add, ALU.mult).then_inc(s_qs, 1)
                for i in two:
                    q = flat(QF)[:, cols(i)]
                    dve.wait_ge(s_q1, i + 1)
                    tt(q, q, QP[:, 0, cols(i)], ALU.subtract).then_inc(s_q1r, 1)
                for i in two:
                    dve.wait_ge(s_q2, i + 1)
                    tt(QP[:, 2, cols(i)], flat(QF)[:, cols(i)], QP[:, 1, cols(i)], ALU.subtract).then_inc(s_q3, 1)
            for i in range(4):
                dve.wait_ge(s_v, i + 1)
                nc.vector.tensor_copy(VT[:, 4 * i:4 * i + 4].rearrange("p n h d -> p (n h d)"), PS[:, i, :]).then_inc(s_vt, 1)

            def take_max(M, j, slot):
                dve.wait_ge(s_mxd, M + 1)
                g = 4 * (j // 2)
                nc.vector.tensor_reduce(NM[:, slot, g:g + 4, j % 2],
                                        PS[:, 2 * (j % 2):2 * (j % 2) + 2, :].rearrange("p k (h t) -> p (k h) t", h=2),
                                        AX.X, ALU.max, negate=True).then_inc(s_max, 1)

            def shift_part(n, half, first=False):
                m = 2 * n + half
                dve.wait_ge(s_mt, m + 1)
                if not first:
                    dve.wait_ge(s_shs[half], 16 * n)
                nc.vector.tensor_copy(SH[:, half, 0], PS[0:H, 7, 0:P]).then_inc(s_sha, 1)
                dve.wait_ge(s_sha, m + 1)
                tt(SHF[:, half], PS[0:H, 7, 0:P], SH[:, half, 0], ALU.subtract).then_inc(s_shb, 1)

            def normalise(b, qt):
                dve.wait_ge(s_tr, 2 * b + qt + 1)
                o = PS[:, 7, :].rearrange("p (h d) -> p h d", d=QW)
                nc.vector.reciprocal(RC[:, qt, :], o[:, :, HD]).then_inc(s_rc, 1)
                dve.wait_ge(s_rc, 2 * b + qt + 1)
                tt(ON[:, bass.ds(2 * b + qt, 1), :].rearrange("p o (h d) -> p (o h) d", d=HD), o[:, :, 0:HD],
                   RC[:, qt, :].unsqueeze(2).broadcast_to([P, H, HD]), ALU.mult).then_inc(s_on, 1)

            for j in range(8):
                take_max(j, j, 0)
                if j == 5:
                    shift_part(0, 0, True)
            shift_part(0, 1, True)
            for j in range(2):
                take_max(8 + j, j, 1)

            def dve_step(i, c, first=False, last=False):
                b = NSLOT * i + c
                for j in range(8):
                    if not last:
                        take_max(8 * b + j + 10, (j + 2) % 8, (c + (1 if j < 6 else 2)) % NSLOT)
                    if j == 2 and not last:
                        shift_part(b + 1, 0)
                    if j == 3 and not first:
                        normalise(b - 1, 0)
                    if j == 5 and not first:
                        normalise(b - 1, 1)
                    if j == 6 and not last:
                        shift_part(b + 1, 1)

            dve_step(0, 0, first=True)
            with dve.Fori(0, 2) as i:
                for u in range(3):
                    dve_step(i, 1 + u)
            dve_step(0, 7, last=True)
            for qt in range(TT):
                normalise(7, qt)
            dve.wait_ge(s_we, 16 * 7)
            nc.vector.tensor_scalar(GBH[:, 1:2], GBH[:, 0:1], 0.5, None, ALU.mult).then_inc(s_gbh, 1)
            for i in range(4):
                dve.wait_ge(s_tg, i + 1)
                o = flat(OT)[:, cols(i)]
                nc.vector.scalar_tensor_tensor(o, flat(TH[:])[:, cols(i)], 1.0, o, ALU.add, ALU.mult).then_inc(s_og, 1)
            quad = lambda ap, i: ap[:, 4 * i:4 * i + 4, :]
            row = lambda r: ROWS[:, r, :].unsqueeze(1).broadcast_to([P, 4, C])
            for i in range(4):
                dve.wait_ge(s_at, i + 1)
                nc.vector.scalar_tensor_tensor(quad(X2, i), PS[:, i, :].rearrange("p (k c) -> p k c", k=4), 0.5, quad(XN, i),
                                               ALU.mult, ALU.add).then_inc(s_xp, 1)
                dve.wait_ge(s_xp, i + 1)
                statistics(lambda k: X2[:, 4 * i + k, :], i, 4)
            stt = nc.vector.scalar_tensor_tensor
            for i in range(4):
                dve.wait_ge(s_mv, 4 + i + 1)
                for n in range(4 * i, 4 * i + 4):
                    o = stt(X2[:, n, :], X2[:, n, :], MV[:, n, 0:1], ROWS[:, 0, :], ALU.subtract, ALU.mult)
                o.then_inc(s_xn, 1)
                dve.wait_ge(s_xn, i + 1)
                dve.wait_ge(s_rs, 4 + i + 1)
                for n in range(4 * i, 4 * i + 4):
                    o = stt(X2[:, n, :], X2[:, n, :], RS[:, n:n + 1], ROWS[:, 1, :], ALU.mult, ALU.add)
                o.then_inc(s_x2, 1)

            dve.wait_ge(s_vs, NSLOT + 6)
            chain = [0]

            def link(ins):
                chain[0] += 1
                ins.then_inc(s_rch, 1)
                dve.wait_ge(s_rch, chain[0])

            per = lambda a: a[:].unsqueeze(2).broadcast_to([P, NT, E])
            each = lambda r: ER[:, r, :].unsqueeze(1).broadcast_to([P, NT, E])
            lg, t8, l2 = (a[:] for a in RT8)
            top1, key1, top2, key2, diff, expd = R1
            red = lambda out, in_, op=ALU.max: nc.vector.tensor_reduce(out[:], in_, AX.X, op)
            dve.wait_ge(s_lg, 1)
            link(tt(lg, PS[:, 0, 0:NT * E].rearrange("p (n e) -> p n e", n=NT), each(0), ALU.add))
            link(red(top1, lg))
            link(tt(t8, lg, per(top1), ALU.is_equal))
            link(tt(t8, t8, each(2), ALU.mult))
            link(red(key1, t8))
            link(tt(t8, each(2), per(key1), ALU.is_equal))
            link(nc.vector.scalar_tensor_tensor(l2, t8, -3.0e38, lg, ALU.mult, ALU.add))
            link(red(top2, l2))
            link(tt(t8, l2, per(top2), ALU.is_equal))
            link(tt(t8, t8, each(2), ALU.mult))
            link(red(key2, t8))
            link(tt(diff[:], top2[:], top1[:], ALU.subtract))
            link(tt(key1[:], key1[:], key2[:], ALU.min))
            link(tt(OH[:, 0:NT], each(2), per(key1), ALU.is_equal))
            for S in SUMS:
                nc.vector.memset(S[:, 0:NT // 2], 0.0)
            nc.vector.memset(OH[:, NT:], 0.0).then_inc(s_oh, 1)
            nc.vector.tensor_copy(SUMS[1][:, NT // 2:], OH[:, 0:NT]).then_inc(s_pre0, 1)
            dve.wait_ge(s_pre0, 1)
            for r in range(4):
                a, b, back = SUMS[1 - r % 2], SUMS[r % 2], 1 << r
                tt(b[:, NT // 2:], a[:, NT // 2:], a[:, NT // 2 - back:NT // 2 + NT - back], ALU.add).then_inc(s_pre, 1)
                if r < 3:
                    dve.wait_ge(s_pre, r + 1)
            link(tt(t8, OH[:, 0:NT], each(1), ALU.mult))
            link(red(RSC, t8, ALU.add))
            dve.wait_ge(s_ed, 1)
            link(nc.vector.tensor_scalar(key1[:], expd[:], 1.0, None, ALU.add))
            link(nc.vector.reciprocal(key2[:], key1[:]))
            link(tt(top1[:], expd[:], key2[:], ALU.mult))
            link(tt(WS[:], top1[:], key2[:], ALU.add))

            rank = PS[:, 1, 0:(NT + 1) * E].rearrange("p (n e) -> p n e", e=E)
            dve.wait_ge(s_rk, 1)
            link(tt(FULL, rank[:, NT, :].unsqueeze(2).broadcast_to([P, E, NT]), TILES, ALU.is_gt))
            link(red(NTILE, FULL, ALU.add))
            link(tt(BEFORE, LOWER, NTILE[:].unsqueeze(1).broadcast_to([P, E, E]), ALU.mult))
            link(red(START, BEFORE, ALU.add))
            link(stt(BASE, START[:].unsqueeze(1).broadcast_to([P, NT, E]), float(P), rank[:, 0:NT, :], ALU.mult, ALU.add))
            link(tt(BASE, BASE, OH[:, 0:NT], ALU.mult))
            link(red(SLOT, BASE, ALU.add))
            nc.vector.tensor_copy(SLOTI[:], SLOT[:]).then_inc(s_slot, 1)
            link(tt(LATER, TILE.unsqueeze(2).broadcast_to([P, NX, E - 2]), START[:, 2:E].unsqueeze(1).broadcast_to([P, NX, E - 2]), ALU.is_ge))
            link(red(TEXP, LATER, ALU.add))
            nc.vector.tensor_copy(TEXPI[:], TEXP[:]).then_inc(s_te, 1)
            link(tt(SW[:], RSC[:], WS[:], ALU.mult))
            link(nc.vector.tensor_scalar(diff[:], WS[:], 1.0, None, ALU.add))
            for n in range(NT):
                o = nc.vector.tensor_scalar(TH[:, n, :], X2[:, n, :], diff[:, n:n + 1], None, ALU.mult)
            o.then_inc(s_wx, 1)

            def copy_x(m, u):
                dve.wait_ge(s_xst, m + 1)
                if not isinstance(m, int) or m > 1:
                    dve.wait_ge(s_h1, m + 1 - 2)
                nc.vector.tensor_copy(XST[:, u], PS[:, 4 + u, 0:2 * P]).then_inc(s_xsc, 1)

            def hidden_statistics(m, u):
                dve.wait_ge(s_h1, m + 1)
                for k in range(2):
                    o = nc.vector.bn_stats(ST2[:, u, k, :], PS[:, u, k * F:(k + 1) * F])
                o.then_inc(s_st2, 1)
                alone(dve, s_st2, m + 1)
                for k in range(2):
                    o = nc.vector.bn_aggr(MV2[:, u, k, :], ST2[:, u, k, :])
                o.then_inc(s_mv2, 1)

            def hidden_normalise(m, u):
                dve.wait_ge(s_rs2, m + 1)
                for k in range(2):
                    o = nc.vector.tensor_scalar(HN[:, u, k, :], PS[:, u, k * F:(k + 1) * F], MV2[:, u, k, 0:1], RS2[:, u, k:k + 1],
                                                ALU.subtract, ALU.mult)
                o.then_inc(s_nrm, 1)

            copy_x(0, 0)
            copy_x(1, 1)
            hidden_statistics(0, 0)
            copy_x(2, 0)
            hidden_normalise(0, 0)
            with dve.Fori(0, NPAIR // 2 - 1) as i:
                for u in range(2):
                    m = 2 * i + u
                    hidden_statistics(m + 1, 1 - u)
                    copy_x(m + 3, 1 - u)
                    hidden_normalise(m + 1, 1 - u)
            for m in (NPAIR - 2, NPAIR - 1):
                hidden_statistics(m, m % 2)
                hidden_normalise(m, m % 2)

            dve.wait_ge(s_xb, 1)
            for k, (part, i) in enumerate(FINAL):
                four = range(4 * i, 4 * i + 4)
                if part == "expert":
                    dve.wait_ge(s_got[i], 64)
                    for n in four:
                        o = stt(ACC[:, n, :], ACC[:, n, :], SW[:, n:n + 1], TH[:, n, :], ALU.mult, ALU.add)
                    o.then_inc(s_f1, 1)
                    dve.wait_ge(s_f1, i + 1)
                    statistics(lambda t: ACC[:, 4 * i + t, :], i, 8 + k - i)
                    dve.wait_ge(s_mv, 8 + k + 1)
                    for n in four:
                        o = stt(ACC[:, n, :], ACC[:, n, :], MV[:, n, 0:1], ROWS[:, 2, :], ALU.subtract, ALU.mult)
                    o.then_inc(s_f2, 1)
                else:
                    dve.wait_ge(s_f2, i + 1)
                    dve.wait_ge(s_rs, 8 + FINAL.index(("expert", i)) + 1)
                    for n in four:
                        o = stt(ACC[:, n, :], ACC[:, n, :], RS[:, n:n + 1], XN[:, n, :], ALU.mult, ALU.add)
                    o.then_inc(s_f3, 1)
                    dve.wait_ge(s_f3, i + 1)
                    statistics(lambda t: ACC[:, 4 * i + t, :], i, 8 + k - i)


def host_consts():
    mask = np.zeros((P, Q4, QW), np.float32)
    for i in range(P):
        q = i // QW
        a = (i % QW) // HD * HD
        mask[i, q, a:a + HD] = SCALE
    return {"avg": np.full((P, P), 1.0 / T, np.float32), "ident": np.eye(P, dtype=np.float32), "mask": mask,
            "diag": (np.eye(B) * T).astype(np.float32),
            "alf": np.array([[0, 0], [-1, 0], [-1, -1]], np.float32),
            "unit": np.concatenate([np.triu(np.ones((P, P)), 1), np.ones((P, P))], axis=1).astype(np.float32),
            "slots": np.concatenate([np.tile(P * np.arange(NT), E), np.tril(np.ones((E, E)), -1).reshape(-1), np.arange(NX)])[None].astype(np.float32),
            "em": np.kron(np.eye(H), np.ones((HD, HD))).astype(np.float32)}


def layer_pack(Wqkv, bqkv, Wproj, bproj):
    t = lambda a: np.swapaxes(a, 1, 2)
    Wq, Wk, Wv = Wqkv[:, :C], Wqkv[:, C:2 * C], Wqkv[:, 2 * C:]
    lw = np.ascontiguousarray(np.concatenate([bqkv[:, :C, None], bproj[:, :, None], t(Wk), t(Wv), t(Wq), t(Wproj), Wq], axis=2))
    return lw, np.ascontiguousarray(bqkv[:, C:])


def kernel(**inputs):
    import concourse.bacc as bacc
    from concourse.bass_utils import run_bass_kernel_spmd

    a = {k.replace("L0_", ""): np.asarray(v) for k, v in inputs.items()}
    lw, lb = layer_pack(a["attn_Wqkv"], a["attn_bqkv"], a["attn_Wproj"], a["attn_bproj"])
    order = list(range(1, E)) + [0]
    col = lambda v: np.ascontiguousarray(v.reshape(-1, 1))
    by_unit = lambda v: v[order].reshape(E, FC, P).transpose(2, 1, 0)
    index = np.arange(E, 0, -1).astype(np.float32)
    arrays = {
        "x": a["attn_inputs_embeds"], "lw": lw, "lb": lb,
        "qw": a["ffn_q_w"], "kw": a["ffn_k_w"], "vw": a["ffn_v_w"], "ow": a["ffn_out_w"], "gw": a["ffn_gate_w"],
        "swc": col(a["ffn_scale_w"]), "gb": col(a["ffn_gate_b"]), "mg": a["ffn_moe_gate_w"],
        "rows": np.concatenate([a["ffn_n1_g"], a["ffn_n1_b"], a["ffn_n2_g"], a["ffn_n2_b"]])[None],
        "er": np.concatenate([a["ffn_moe_gate_b"], a["ffn_res_scale"], index])[None],
        "w1": a["ffn_w1"][order].transpose(1, 0, 2), "b1": a["ffn_b1"][order].reshape(1, -1),
        "w2": a["ffn_w2"][order].reshape(E, FC, P, C).transpose(2, 0, 1, 3), "b2": a["ffn_b2"][order].reshape(1, -1),
        "lnw": np.stack([by_unit(a["ffn_ln_g"]), by_unit(a["ffn_ln_b"])], axis=1),
        **host_consts(),
    }
    arrays = {f"in_{k}": np.ascontiguousarray(v) for k, v in arrays.items()}
    nc = bacc.Bacc("TRN2", target_bir_lowering=False, num_devices=1)
    aps = {k[3:]: nc.dram_tensor(k, v.shape, mybir.dt.from_np(v.dtype), kind="ExternalInput").ap() for k, v in arrays.items()}
    out = nc.dram_tensor("out", (B, T, C), fp32, kind="ExternalOutput").ap()
    build(nc, aps["x"], aps["lw"], aps["lb"], aps, aps, out)
    r = run_bass_kernel_spmd(nc, [arrays], core_ids=[0])
    return r.results[0]["out"]
```

```python
import numpy as np
import concourse.bass as bass
from concourse import mybir
from concourse.alu_op_type import AluOpType as ALU
from contextlib import ExitStack

fp32 = mybir.dt.float32
bf16 = mybir.dt.bfloat16
u32 = mybir.dt.uint32
ACT = mybir.ActivationFunctionType
AX = mybir.AxisListType

P = 128
B, T, C = 8, 256, 128
TT = T // P
NT = B * TT
L = 12
H = 16
HD = C // H
E, F = 8, 256
FC = F // P
GB = 4
Q4 = 4
QW = P // Q4
EPS = 1e-5
SCALE = float(np.float32(1.0) / np.sqrt(np.float32(HD)))

NS = (NT * P + (E - 1) * (P - 1)) // P
NX = NS + 2
NSLOT = 3

CBQ, CBP, CKT, CVT, CQT, CPT, CQN = 0, 1, 2, 2 + C, 2 + 2 * C, 2 + 3 * C, 2 + 4 * C
CQB = CQN + C
WCOLS = CQB
BQ = C + B


def build(nc, x_d, lw_d, lb_d, fw, consts, out_d):
    ctx = ExitStack()
    with ctx:
        def sb(name, shape, dt=fp32):
            return ctx.enter_context(nc.sbuf_tensor(name, shape, dt))

        def sem(name):
            return ctx.enter_context(nc.semaphore(name))

        X = sb("X", [P, B, TT, C])
        XT = sb("XT", [P, B, T])
        IR = sb("IR", [P, B, C])
        BR = sb("BR", [B, 2, 2 * C])
        KV = sb("KV", [P, 2 * C])
        MEAN = sb("MEAN", [P, B])
        MEAN0 = sb("MEAN0", [P, B])
        MSUM = sb("MSUM", [P, B])
        IDN = sb("IDN", [P, P])
        MASK = sb("MASK", [P, Q4, QW])
        DIAG = sb("DIAG", [B, B])
        AVG = sb("AVG", [P, P])

        arena = sb("ARENA", [P, 10752])
        at = [0]

        def piece(n, *dims):
            v = arena[:, at[0]:at[0] + n]
            at[0] += n
            names = "abcd"[:len(dims)]
            return v.rearrange(f"p ({' '.join(names)}) -> p {' '.join(names)}", **dict(zip(names, dims)))

        G = piece(B * C, B, C)
        RT = piece(B * C, B, C)
        IA = piece(2 * B * C, 2, B, C)
        U = piece(B * C, B, C)
        GV = piece(B * C, B, C)
        MF = piece(B * C, B, C)
        BT = piece(B * BQ, B, BQ)
        V8 = piece(B * C, B, C)
        WL = piece(2 * (WCOLS + B), 2, WCOLS + B)

        at[0] = 0
        HT = piece(NT * P, NT, P)
        QF = piece(NT * P, NT, P)
        QP = piece(3 * NT * P // 2, 3 * NT * P // 2).bitcast(bf16).rearrange("p (s t) -> p s t", s=3)
        KP = piece(3 * NT * P // 2, 3 * NT * P // 2).bitcast(bf16).rearrange("p (s t) -> p s t", s=3)
        KF = HT
        ON = HT
        OTS = sb("OTS", [P, 3, Q4, T])
        VT = sb("VT", [P, NT + TT, H, HD])
        VS = sb("VS", [P, NSLOT, TT, H, QW])
        PT = sb("PT", [P, 4, 2, T])
        STK = sb("STK", [P, 2, NSLOT, H, T], bf16)
        QS, KS = STK[:, 0], STK[:, 1]
        TH = sb("TH", [P, NT, P])
        X2 = sb("X2", [P, NT, C])
        NM = sb("NM", [P, NSLOT, H, TT])
        SHF = sb("SHF", [TT * H // 2, 2, P])
        SH = sb("SH", [TT * H // 2, 2, 3, P], bf16)
        RC = sb("RC", [P, 2, H])
        WEIGHT = {n: sb(n, [P, C]) for n in ("qw", "kw", "vw", "ow", "gw")}
        SWB = sb("SWB", [P, P])
        SWC = sb("SWC", [P, 1])
        GBH = sb("GBH", [P, 2])
        EM = sb("EM", [P, P])
        ROWS = sb("ROWS", [P, 4, C])
        MG = sb("MG", [P, E])
        ER = sb("ER", [P, 3, E])
        NH = sb("NH", [P, NT])
        ST, MV, VE, RS = sb("ST", [P, NT, 6]), sb("MV", [P, NT, 2]), sb("VE", [P, NT]), sb("RS", [P, NT])

        OT = QF
        late = STK[:].rearrange("p a b c d -> p (a b c d)").bitcast(fp32)
        la = [0]

        def late_piece(n):
            la[0] += n
            return late[:, la[0] - n:la[0]]

        X2T = late_piece(NT * P)
        ACC = late_piece(NT * C).rearrange("p (n c) -> p n c", n=NT)
        XS = late_piece(4 * C).rearrange("p (u k c) -> p u k c", u=2, k=2)
        YS = late_piece(4 * C).rearrange("p (u k c) -> p u k c", u=2, k=2)
        XST = late_piece(4 * P).rearrange("p (u t) -> p u t", u=2)
        HN = late_piece(4 * F).rearrange("p (u k f) -> p u k f", u=2, k=2)
        GT = late_piece(4 * F).rearrange("p (u c t) -> p u c t", u=2, c=FC)
        W1 = sb("W1", [P, E, F])
        W2 = sb("W2", [P, E, FC, C])
        LNW = sb("LNW", [P, 2, FC, E])
        B1F = TH[0:3].rearrange("p n c -> p (n c)")
        TAKE = PT[0:3].rearrange("p a b c -> p (a b c)")
        B2F = X2[0:3, 0:E].rearrange("p n c -> p (n c)")
        B1P = sb("B1P", [P, E * F], bf16)
        B2P = sb("B2P", [P, E * C], bf16)
        ONE3 = sb("ONE3", [P, P], bf16)
        ALF = sb("ALF", [3, 2])
        ST2, MV2, VE2, RS2 = sb("ST2", [P, 2, 2, 6]), sb("MV2", [P, 2, 2, 2]), sb("VE2", [P, 2, 2]), sb("RS2", [P, 2, 2])
        NB = sb("NB", [P, NT])
        vals = VT[:].rearrange("p n h d -> p (n h d)")
        va = [0]

        def value_piece(n, a, b):
            va[0] += n
            return vals[:, va[0] - n:va[0]].rearrange("p (a b) -> p a b", a=a)

        RT8 = [value_piece(NT * E, NT, E) for n in range(3)]
        OH = value_piece((NT + 1) * E, NT + 1, E)
        SUMS = [value_piece((NT // 2 + NT) * E, NT // 2 + NT, E) for _ in range(2)]
        BASE = value_piece(NT * E, NT, E)
        UNIT = value_piece(P * 2, 2, P)
        SLOT_CONSTS = value_piece(E * NT + E * E + NX, 1, E * NT + E * E + NX)[:, 0]
        FULL = value_piece(E * NT, E, NT)
        BEFORE = value_piece(E * E, E, E)
        LATER = value_piece(NX * (E - 2), NX, E - 2)
        TILES = SLOT_CONSTS[:, 0:E * NT].rearrange("p (e k) -> p e k", e=E)
        LOWER = SLOT_CONSTS[:, E * NT:E * NT + E * E].rearrange("p (e d) -> p e d", e=E)
        TILE = SLOT_CONSTS[:, E * NT + E * E:]
        NTILE, START = sb("NTILE", [P, E]), sb("START", [P, E])
        SLOT, TEXP = sb("SLOT", [P, NT]), sb("TEXP", [P, NX])
        SLOTI = sb("SLOTI", [P, NT], u32)
        TEXPI = sb("TEXPI", [P, NX], u32)
        R1 = [sb(f"R1_{n}", [P, NT]) for n in range(6)]
        RSC = sb("RSC", [P, NT])
        WS = sb("WS", [P, NT])
        SW = sb("SW", [P, NT])
        PS = ctx.enter_context(nc.psum_tensor("PS", [P, 8, 512], fp32))
        scq = nc.dram_tensor("query_parts", (3, H, HD, (NT + TT) * P), bf16).ap()
        sck = nc.dram_tensor("key_parts", (H, 3, HD, (NT + TT) * P), bf16).ap()
        xs_d = nc.dram_tensor("sorted_x2", (NS * P, C), fp32).ap()
        ys_d = nc.dram_tensor("sorted_outputs", (NS * P, C), fp32).ap()
        scm = nc.dram_tensor("shifts", (NSLOT, 3, H, T), bf16).ap()

        def bank(g, k):
            return PS[:, 4 * g + k, :]

        def batches(ap):
            return ap.rearrange("p (b c) -> p b c", b=GB)

        s_const = sem("const_loaded")
        s_x = [sem(f"x_loaded_{u}") for u in range(2)]
        s_w = [sem(f"layer_weights_loaded_{u}") for u in range(2)]
        s_zero = sem("pool_constants_set")
        s_mrow = sem("mean_rows_summed")
        s_mcol = sem("mean_columns_summed")
        s_xc = sem("x_centred")
        s_gram = sem("gram_summed")
        s_xct = sem("centred_x_transposed")
        s_xt = sem("centred_xT_copied")
        s_g = sem("gram_ready")
        s_mean = sem("mean_ready")
        s_p = sem("gv_done")
        s_pc = sem("gv_copied")
        s_row = sem("mean_keys_values_done")
        s_kv = sem("mean_keys_values_copied")
        s_v8 = sem("mean_values_spread")
        s_qbd = sem("mean_queries_done")
        s_qb = sem("mean_queries_ready")
        s_k = sem("ktv_done")
        s_m = sem("ktv_masked")
        s_r = sem("rt_done")
        s_rt = sem("rt_ready")
        s_b = sem("bt_done")
        s_bt = sem("bt_copied")
        s_a = sem("a_done")
        s_ia = sem("ia_ready")
        s_ym = sem("mean_update_done")
        s_u = sem("u_done")
        s_uc = sem("u_copied")
        s_gd = sem("gram_done")
        s_out = sem("out_stored")

        s_wf = sem("ffn_weights_loaded")
        s_stk0 = sem("stack_constants_set")
        s_ir = sem("i_plus_r_ready")
        s_ms = sem("mean_sum_ready")
        s_h = sem("residual_done")
        s_htv, s_hta = sem("residual_copied_by_dve"), sem("residual_copied_by_act")
        s_tok = sem("residual_transposed")
        s_st = sem("statistics_taken")
        s_mv = sem("mean_variance_ready")
        s_ve = sem("variance_plus_eps_ready")
        s_rs = sem("rstd_ready")
        s_x1 = [sem(f"x1_ready_{u}") for u in ("dve", "act")]
        s_x1t = sem("x1_transposed")
        s_xtc = sem("x1t_copied")
        s_q = sem("queries_done")
        s_qf = sem("queries_copied")
        s_kd = sem("keys_done")
        s_kf = sem("keys_scaled")
        s_z = sem("query_scale_done")
        s_th = sem("query_scale_tanh")
        s_v = sem("values_done")
        s_vt = sem("values_copied")
        s_qs = sem("queries_scaled")
        s_swb = sem("scale_weights_spread")
        s_q1, s_q1r, s_q2, s_q3 = (sem(f"query_{n}") for n in ("part_1", "rest_1", "part_2", "part_3"))
        s_k1, s_k1r, s_k2, s_k3 = (sem(f"key_{n}") for n in ("part_1", "rest_1", "part_2", "part_3"))
        s_scr = [sem(f"parts_stored_{u}") for u in range(2)]
        s_stk = [sem(f"stack_loaded_{u}") for u in range(NSLOT)]
        s_mxd = sem("max_scores_done")
        s_max = sem("maxima_taken")
        s_mt = sem("maxima_transposed")
        s_sha = sem("shift_part_1")
        s_shb = sem("shift_rest_1")
        s_shc = sem("shift_part_2")
        s_shd = sem("shift_part_3")
        s_shs = [sem(f"shifts_stored_{u}") for u in range(2)]
        s_shl = [sem(f"shifts_loaded_{u}") for u in range(2)]
        s_qk = sem("scores_done")
        s_exp = sem("exponentials_ready")
        s_vs = sem("batch_values_ready")
        s_pv = sem("pv_done")
        s_ot = sem("outputs_copied")
        s_tr = sem("outputs_transposed")
        s_rc = sem("sums_inverted")
        s_on = sem("outputs_normalised")
        s_we = sem("expert_weights_loaded")
        s_eb = sem("expert_biases_loaded")
        s_zb = sem("expert_bias_steps")
        s_gbh = sem("half_gate_bias_ready")
        s_ott = sem("normalised_outputs_transposed")
        s_otc = sem("transposed_outputs_copied")
        s_gt = sem("gate_done")
        s_tg = sem("gate_tanh")
        s_og = sem("gated_outputs_ready")
        s_at = sem("out_projection_done")
        s_xp = sem("attention_residual_ready")
        s_xn = sem("x2_normalised")
        s_x2 = sem("x2_ready")
        s_x2t = sem("x2_transposed")
        s_x2c = sem("x2t_copied")
        s_lg = sem("logits_done")
        s_rch = sem("routing_steps")
        s_ed = sem("second_weight_exponential")
        s_oh = sem("routing_ready")
        s_zf = sem("sorted_rows_cleared")
        s_vsz = sem("values_cleared")
        s_sc = sem("slot_constants_loaded")
        s_pre = sem("tile_sums_doubled")
        s_rk = sem("ranks_done")
        s_slot = sem("slots_ready")
        s_te = sem("tile_experts_ready")
        s_sct = sem("x2_scattered")
        s_xs = [sem(f"sorted_x2_loaded_{u}") for u in range(2)]
        s_xst = sem("sorted_x2_transposed")
        s_xsc = sem("sorted_x2t_copied")
        s_h1 = sem("hidden_done")
        s_st2 = sem("hidden_statistics_taken")
        s_mv2 = sem("hidden_mean_variance")
        s_ve2 = sem("hidden_variance_plus_eps")
        s_rs2 = sem("hidden_rstd")
        s_nrm = sem("hidden_normalised")
        s_td = sem("hidden_transposed")
        s_gl = sem("gelu_ready")
        s_y = sem("expert_output_done")
        s_yc = sem("expert_output_copied")
        s_ys = [sem(f"sorted_outputs_stored_{u}") for u in range(2)]
        s_got = [sem(f"outputs_gathered_{u}") for u in range(4)]
        s_nb0 = sem("mean_times_rstd")
        s_nb = sem("shift_ready")
        s_wx = sem("weighted_x2_ready")
        s_xb = sem("x1_plus_bias_ready")
        s_f1, s_f2, s_f3 = (sem(f"final_{n}") for n in ("weighted", "centred", "summed"))
        s_fo = sem("output_rows_ready")
        block = ctx.enter_context(nc.Block())

        NPAIR = NS // 2
        assert NS % 2 == 0 and NPAIR % 2 == 1

        FINAL = [("expert", 0), ("expert", 1), ("block", 0), ("expert", 2), ("block", 1), ("expert", 3), ("block", 2), ("block", 3)]

        def tile_experts(engine, first, n):
            return nc.values_load_multi_w_load_instructions(
                TEXPI[0:1, bass.ds(first, n)], engines=(engine,), min_val=0, max_val=E - 2,
                skip_runtime_bounds_check_because="it counts E - 2 comparisons")[1]

        def alone(engine, semaphore, value):
            engine.wait_ge(semaphore, value)
            engine.nop(nofuse=True)

        XN = X[:].rearrange("p b t c -> p (b t) c")
        cols = lambda i: slice(4 * P * i, 4 * P * (i + 1))
        flat = lambda ap: ap.rearrange("p a c -> p (a c)")
        XTF = XT[:].rearrange("p b t -> p (b t)")
        SROW = 3 * QW
        KEXP, KMAX = SROW + 3, 2 * QW + HD

        @block.sync
        def _(sp):
            sp.dma_start(AVG[:], consts["avg"]).then_inc(s_const, 16)
            for i in range(4):
                sp.dma_start(X[:, 2 * i:2 * i + 2], x_d[2 * i:2 * i + 2].rearrange("b (p t) c -> p b t c", t=TT)).then_inc(s_x[i // 2], 16)
            sp.dma_start(IDN[:], consts["ident"]).then_inc(s_const, 16)
            sp.dma_start(MASK[:], consts["mask"]).then_inc(s_const, 16)
            sp.dma_start(DIAG[:], consts["diag"]).then_inc(s_const, 16)
            sp.dma_start(B1F, fw["b1"].broadcast_to([3, E * F])).then_inc(s_eb, 16)
            sp.dma_start(ALF[:], consts["alf"]).then_inc(s_eb, 16)
            sp.dma_start(B2F, fw["b2"].broadcast_to([3, E * C])).then_inc(s_eb, 16)
            for u in range(2):
                sp.dma_start(WL[:, u, 0:WCOLS], lw_d[u]).then_inc(s_w[u], 16)
                sp.dma_start(BR[:, u, :], lb_d[u:u + 1, :].broadcast_to([B, 2 * C])).then_inc(s_w[u], 16)
            sp.wait_ge(s_vsz, 1)
            sp.dma_start(xs_d.rearrange("(p n) c -> p (n c)", p=P), VS[:].rearrange("p a b c d -> p (a b c d)")[:, 0:NS * C]).then_inc(s_zf, 16)
            for d in (scq, sck):
                sp.dma_start(d[:, :, :, B * T:].rearrange("a b d t -> (a b d) t").rearrange("(p r) t -> p r t", r=3),
                             VS[:].rearrange("p a b c d -> p (a b c d)").bitcast(bf16)[:, 0:3 * T].rearrange("p (r t) -> p r t", r=3)).then_inc(s_zf, 16)
            with sp.Fori(0, L // 2 - 1) as i:
                for u in range(2):
                    sp.wait_ge(s_mean, 2 * i + u + 2)
                    sp.dma_start(WL[:, u, 0:WCOLS], lw_d[bass.ds(2 * i + u + 2, 1)].rearrange("l p c -> p (l c)")).then_inc(s_w[u], 16)
                    sp.dma_start(BR[:, u, :], lb_d[bass.ds(2 * i + u + 2, 1), :].broadcast_to([B, 2 * C])).then_inc(s_w[u], 16)
            for n, w in WEIGHT.items():
                sp.dma_start(w[:], fw[n]).then_inc(s_wf, 16)
            sp.dma_start(SWC[:], fw["swc"]).then_inc(s_wf, 16)
            sp.dma_start(EM[:], consts["em"]).then_inc(s_wf, 16)
            sp.dma_start(GBH[:, 0:1], fw["gb"]).then_inc(s_we, 16)
            sp.dma_start(ROWS[:], fw["rows"].broadcast_to([P, 4 * C]).rearrange("p (r c) -> p r c", r=4)).then_inc(s_we, 16)
            sp.dma_start(ER[:], fw["er"].broadcast_to([P, 3 * E]).rearrange("p (r c) -> p r c", r=3)).then_inc(s_we, 16)
            sp.dma_start(MG[:], fw["mg"]).then_inc(s_we, 16)
            sp.dma_start(W1[:], fw["w1"]).then_inc(s_we, 16)
            sp.dma_start(W2[:], fw["w2"]).then_inc(s_we, 16)
            sp.dma_start(LNW[:], fw["lnw"]).then_inc(s_we, 16)
            def store_parts(half):
                sp.wait_ge(s_k3, (1, 4)[half])
                t = (slice(0, 2 * T), slice(2 * T, B * T))[half]
                for r in range(3):
                    sp.dma_start(sck[:, r, :, t], KP[:, r, t]).then_inc(s_scr[half], 16)
                sp.wait_ge(s_q3, (1, 4)[half])
                sp.dma_start(scq[:, :, :, t].rearrange("s h d t -> (h d) s t"), QP[:, :, t]).then_inc(s_scr[half], 16)

            def load_queries(n, slot):
                q = scq[:, :, :, bass.ds(n * T, T)].rearrange("s h d t -> s d h t")
                row = 0
                for part, times in ((0, 3), (1, 2), (2, 1)):
                    for _ in range(times):
                        sp.dma_start(QS[HD * row:HD * (row + 1), slot], q[part]).then_inc(s_stk[slot], 16)
                        row += 1

            def load_keys(n, slot):
                k = sck[:, :, :, bass.ds(n * T, T)].rearrange("h s d t -> (s d) h t")
                row = 0
                for parts in (3, 2, 1):
                    sp.dma_start(KS[HD * row:HD * (row + parts), slot], k[0:HD * parts]).then_inc(s_stk[slot], 16)
                    row += parts

            def store_shift(n, slot, half):
                heads = slice(half * H // 2, (half + 1) * H // 2)
                sp.wait_ge(s_shd, 2 * n + half + 1)
                sp.dma_start(scm[slot, :, heads, :].rearrange("s h (q t) -> (h q) s t", q=TT), SH[:, half]).then_inc(s_shs[half], 16)

            def load_shift(n, slot, half):
                heads = slice(half * H // 2, (half + 1) * H // 2)
                sp.wait_ge(s_shs[half], 16 * (n + 1))
                sp.dma_start(QS[SROW:SROW + 3, slot, heads, :], scm[slot, :, heads, :]).then_inc(s_shl[half], 16)

            store_parts(0)
            sp.wait_ge(s_stk0, 5)
            sp.wait_ge(s_scr[0], 16 * 4)
            load_keys(0, 0)
            load_queries(0, 0)
            load_queries(1, 1)
            load_keys(1, 1)
            store_parts(1)
            store_shift(0, 0, 0)
            load_shift(0, 0, 0)
            store_shift(0, 0, 1)

            def sp_step(i, c):
                b = NSLOT * i + c
                if c > 0:
                    sp.wait_ge(s_qk, 16 * b)
                load_keys(b + 2, (c + 2) % NSLOT)
                load_shift(b, c % NSLOT, 1)
                load_queries(b + 2, (c + 2) % NSLOT)
                store_shift(b + 1, (c + 1) % NSLOT, 0)
                load_shift(b + 1, (c + 1) % NSLOT, 0)
                store_shift(b + 1, (c + 1) % NSLOT, 1)

            sp.wait_ge(s_scr[1], 16 * 4)
            sp_step(0, 0)
            with sp.Fori(0, 2) as i:
                for u in range(3):
                    sp_step(i, 1 + u)
            load_shift(7, 7 % NSLOT, 1)
            sp.wait_ge(s_vs, NSLOT + 6)
            sp.dma_start(UNIT, consts["unit"].rearrange("p (a b) -> p a b", a=2)).then_inc(s_sc, 16)
            sp.dma_start(SLOT_CONSTS, consts["slots"].broadcast_to([P, E * NT + E * E + NX])).then_inc(s_sc, 16)
            sp.wait_ge(s_sct, 16 * NT)

            def load_sorted(m, u):
                if not isinstance(m, int) or m > 1:
                    sp.wait_ge(s_xst, m + 1 - 2)
                sp.dma_start(XS[:, u], xs_d[bass.ds(2 * m * P, 2 * P)].rearrange("(k p) c -> p k c", k=2)).then_inc(s_xs[u], 16)

            def store_outputs(m, u):
                sp.wait_ge(s_yc, m + 1)
                sp.dma_start(ys_d[bass.ds(2 * m * P, 2 * P)].rearrange("(k p) c -> p k c", k=2), YS[:, u]).then_inc(s_ys[u], 16)

            for m in range(5):
                load_sorted(m, m % 2)
            with sp.Fori(0, (NPAIR - 5) // 2) as i:
                for u in range(2):
                    load_sorted(2 * i + u + 5, 1 - u)
                    store_outputs(2 * i + u, u)
            for m in range(NPAIR - 5, NPAIR):
                store_outputs(m, m % 2)
            for i in range(4):
                sp.wait_ge(s_fo, i + 1)
                sp.dma_start(out_d[2 * i:2 * i + 2].rearrange("b (p t) c -> p b t c", t=TT),
                             ACC[:, 4 * i:4 * i + 4].rearrange("p (b t) c -> p b t c", t=TT)).then_inc(s_out, 16)
            sp.wait_ge(s_out, 64)

        @block.gpsimd
        def _(pool):
            nc.gpsimd.memset(VS[:], 0.0).then_inc(s_vsz, 1)
            nc.gpsimd.memset(KV[:], 0.0).then_inc(s_zero, 1)
            nc.gpsimd.memset(V8[:], 0.0).then_inc(s_zero, 1)
            pool.wait_ge(s_const, 64)
            nc.gpsimd.tensor_copy(RT[:], IDN[:].unsqueeze(1).broadcast_to([P, B, C])).then_inc(s_zero, 1)
            nc.gpsimd.tensor_copy(IA[:, 1], IDN[:].unsqueeze(1).broadcast_to([P, B, C])).then_inc(s_zero, 1)
            for a in (ONE3, B1P, B2P):
                nc.gpsimd.memset(a[:], 0.0).then_inc(s_zb, 1)
            pool.wait_ge(s_zb, 3)
            nc.gpsimd.memset(ONE3[0:3, :], 1.0).then_inc(s_zb, 1)
            pool.wait_ge(s_eb, 48)
            done = 4
            for full, parts in ((B1F, B1P), (B2F, B2P)):
                for r in range(3):
                    nc.gpsimd.tensor_copy(parts[0:3], full).then_inc(s_zb, 1)
                    done += 1
                    if r < 2:
                        pool.wait_ge(s_zb, done)
                        nc.gpsimd.tensor_scalar(TAKE[:, 0:full.shape[1]], parts[0:3], ALF[:, r:r + 1], None, ALU.mult).then_inc(s_zb, 1)
                        pool.wait_ge(s_zb, done + 1)
                        nc.gpsimd.tensor_tensor(full, full, TAKE[:, 0:full.shape[1]], ALU.add).then_inc(s_zb, 1)
                        pool.wait_ge(s_zb, done + 2)
                        done += 2
            nc.gpsimd.memset(NH[:], -0.5).then_inc(s_stk0, 1)
            nc.gpsimd.memset(VT[:, NT:], 0.0).then_inc(s_stk0, 1)
            nc.gpsimd.memset(STK[:].bitcast(u32), 0).then_inc(s_stk0, 1)
            pool.wait_ge(s_zf, 48)
            nc.gpsimd.memset(VS[:, :, :, :, HD:HD + 1], 1.0).then_inc(s_stk0, 1)
            pool.wait_ge(s_stk0, 4)
            nc.gpsimd.memset(KS[SROW:SROW + 3], 1.0).then_inc(s_stk0, 1)
            pool.wait_ge(s_stk0, 5)
            def rstd(i):
                t = slice(4 * i, 4 * i + 4)
                pool.wait_ge(s_mv, i + 1)
                nc.gpsimd.tensor_scalar(VE[:, t], MV[:, t, 1], EPS, None, ALU.add).then_inc(s_ve, 1)
                pool.wait_ge(s_ve, i + 1)
                nc.gpsimd.tensor_tensor(RS[:, t], VE[:, t], NH[:, t], ALU.pow).then_inc(s_rs, 1)

            for i in range(4):
                rstd(i)
                if i % 2:
                    t = slice(4 * i, 4 * i + 4)
                    pool.wait_ge(s_rs, i + 1)
                    nc.gpsimd.tensor_tensor(VE[:, t], MV[:, t, 0], RS[:, t], ALU.mult).then_inc(s_nb0, 1)
                    pool.wait_ge(s_nb0, i // 2 + 1)
                    nc.gpsimd.tensor_scalar(NB[:, t], VE[:, t], -1.0, None, ALU.mult).then_inc(s_nb, 1)
            for i in range(4):
                k, c = flat(KF)[:, cols(i)], cols(i)
                pool.wait_ge(s_k1, i + 1)
                nc.gpsimd.tensor_tensor(k, k, KP[:, 0, c], ALU.subtract).then_inc(s_k1r, 1)
                pool.wait_ge(s_k2, i + 1)
                nc.gpsimd.tensor_tensor(KP[:, 2, c], k, KP[:, 1, c], ALU.subtract).then_inc(s_k3, 1)

            def batch_values(b, slot):
                nc.gpsimd.tensor_copy(VS[:, slot, :, :, 0:HD], VT[:, bass.ds(b * TT, TT)]).then_inc(s_vs, 1)

            def shift_parts(n, half, first=False):
                m = 2 * n + half
                pool.wait_ge(s_shb, m + 1)
                if not first:
                    alone(pool, s_shs[half], 16 * n)
                else:
                    pool.wait_ge(s_vs, NSLOT)
                nc.gpsimd.tensor_copy(SH[:, half, 1], SHF[:, half]).then_inc(s_shc, 1)
                pool.wait_ge(s_shc, m + 1)
                nc.gpsimd.tensor_tensor(SH[:, half, 2], SHF[:, half], SH[:, half, 1], ALU.subtract).then_inc(s_shd, 1)

            pool.wait_ge(s_vt, 4)
            for b in range(NSLOT):
                batch_values(b, b)
            for half in range(2):
                shift_parts(0, half, True)

            def pool_step(i, c):
                b = NSLOT * i + c
                if c > 0:
                    pool.wait_ge(s_pv, 8 * b)
                    alone(pool, s_shd, 2 * b + 2)
                    batch_values(b + 2, (c + 2) % NSLOT)
                    pool.wait_ge(s_vs, b + 3)
                for half in range(2):
                    shift_parts(b + 1, half)

            pool_step(0, 0)
            with pool.Fori(0, 2) as i:
                for u in range(3):
                    pool_step(i, 1 + u)

            for i in range(4):
                pool.wait_ge(s_shd, 16)
                t = slice(4 * i, 4 * i + 4)
                pool.wait_ge(s_mv, i + 5)
                nc.gpsimd.tensor_scalar(VE[:, t], MV[:, t, 1], EPS, None, ALU.add).then_inc(s_ve, 1)
                pool.wait_ge(s_ve, i + 5)
                nc.gpsimd.tensor_tensor(RS[:, t], VE[:, t], NH[:, t], ALU.pow).then_inc(s_rs, 1)
            nc.gpsimd.tensor_tensor(XN, XN, ROWS[:, 3, :].unsqueeze(1).broadcast_to([P, NT, C]), ALU.add).then_inc(s_xb, 1)
            pool.wait_ge(s_slot, 1)
            for n in range(NT):
                nc.gpsimd.indirect_dma_start(xs_d, bass.IndirectOffsetOnAxis(SLOTI[:, n:n + 1], 0), X2[:, n, :], None).then_inc(s_sct, 16)

            def hidden_rstd(m, u):
                alone(pool, s_mv2, m + 1)
                nc.gpsimd.tensor_scalar(VE2[:, u], MV2[:, u, :, 1], EPS, None, ALU.add).then_inc(s_ve2, 1)
                alone(pool, s_ve2, m + 1)
                nc.gpsimd.tensor_tensor(RS2[:, u], VE2[:, u], NH[:, 0:2], ALU.pow).then_inc(s_rs2, 1)

            with pool.Fori(0, NPAIR // 2) as i:
                for u in range(2):
                    hidden_rstd(2 * i + u, u)
            hidden_rstd(NPAIR - 1, 0)

            def gather(i):
                for n in range(4 * i, 4 * i + 4):
                    nc.gpsimd.indirect_dma_start(ACC[:, n, :], None, ys_d, bass.IndirectOffsetOnAxis(SLOTI[:, n:n + 1], 0)).then_inc(s_got[i], 16)

            def late_rstd(k):
                part, i = FINAL[k]
                t = slice(4 * i, 4 * i + 4)
                pool.wait_ge(s_mv, 8 + k + 1)
                nc.gpsimd.tensor_scalar(VE[:, t], MV[:, t, 1], EPS, None, ALU.add).then_inc(s_ve, 1)
                pool.wait_ge(s_ve, 8 + k + 1)
                nc.gpsimd.tensor_tensor(RS[:, t], VE[:, t], NH[:, t], ALU.pow).then_inc(s_rs, 1)
                if part == "block":
                    pool.wait_ge(s_rs, 8 + k + 1)
                    nc.gpsimd.tensor_tensor(VE[:, t], MV[:, t, 0], RS[:, t], ALU.mult).then_inc(s_nb0, 1)
                    pool.wait_ge(s_nb0, 2 + i + 1)
                    nc.gpsimd.tensor_scalar(NB[:, t], VE[:, t], -1.0, None, ALU.mult).then_inc(s_nb, 1)

            for u in range(2):
                pool.wait_ge(s_ys[u], 16 + 16 * ((NPAIR + 1 - u) // 2))
            gather(0)
            gather(1)
            late_rstd(0)
            gather(2)
            late_rstd(1)
            gather(3)
            for k in range(2, 8):
                late_rstd(k)

        @block.tensor
        def _(pe):
            mm = nc.tensor.matmul
            pe.wait_ge(s_const, 64)
            for g in range(2):
                pe.wait_ge(s_x[g], 32)
                for t in range(TT):
                    last = mm(batches(bank(g, 0)), AVG[:], X[:, GB * g:GB * (g + 1), t, :], start=t == 0, stop=t == TT - 1)
                last.then_inc(s_mrow, 1)
                for b in range(GB):
                    for t in range(TT):
                        last = mm(bank(g, 1)[:, b:b + 1], X[:, GB * g + b, t, :], AVG[:, 0:1], start=t == 0, stop=t == TT - 1)
                last.then_inc(s_mcol, 1)
            for g in range(2):
                pe.wait_ge(s_xc, 2 * g + 2)
                for b in range(GB):
                    xb = X[:, GB * g + b]
                    for t in range(TT):
                        last = mm(bank(g, 2)[:, b * C:(b + 1) * C], xb[:, t, :], xb[:, t, :], start=t == 0, stop=t == TT - 1)
                last.then_inc(s_gram, 1)
            for i, (g, k) in enumerate(((0, 3), (1, 3), (0, 0), (1, 0))):
                for j in range(2 * TT):
                    last = nc.tensor.transpose(bank(g, k)[:, j * P:(j + 1) * P], X[:, 2 * i + j // TT, j % TT, :], IDN[:])
                last.then_inc(s_xct, 1)
            pe.wait_ge(s_xt, 4)
            pe.wait_ge(s_zero, 5)
            def rt_product(l, u, g):
                if g == 0:
                    pe.wait_ge(s_kv, l + 1)
                else:
                    pe.wait_ge(s_qb, l + 1)
                pe.wait_ge(s_rt, 2 * l + g - 1)
                for n in range(GB * g, GB * (g + 1)):
                    last = mm(bank(g, 3)[:, (n % GB) * C:(n % GB + 1) * C], IA[:, 1 - u, n, :], RT[:, n, :], start=True, stop=True)
                last.then_inc(s_r, 1)

            def pe_layer(i, u, first=False, final=False):
                l = 2 * i + u
                W = WL[:, u]
                pe.wait_ge(s_w[u], 32 * i + 32)
                pe.wait_ge(s_mean, l + 1)
                mm(bank(0, 3)[0:B, 0:2 * C], MEAN[:], W[:, CKT:CKT + 2 * C], start=True, stop=True).then_inc(s_row, 1)
                mm(bank(1, 3)[:, 0:B], W[:, CQT:CQT + C], MEAN[:], start=True, stop=True).then_inc(s_qbd, 1)
                for g in range(2):
                    pe.wait_ge(s_g, 2 * l + g + 1)
                    for b in range(GB):
                        last = mm(bank(g, 0)[:, b * C:(b + 1) * C], G[:, GB * g + b, :], W[:, CVT:CVT + C], start=True, stop=True)
                    last.then_inc(s_p, 1)
                if not first:
                    rt_product(l, u, 0)
                for g in range(2):
                    pe.wait_ge(s_pc, 2 * l + g + 1)
                    pe.wait_ge(s_v8, 2 * l + g + 1)
                    for q in range(Q4):
                        quad = slice(QW * q, QW * (q + 1))
                        out = bank(g, 2)[quad, 0:GB * QW].rearrange("p (b j) -> p b j", b=GB)
                        mm(out, W[:, CKT + QW * q:CKT + QW * (q + 1)], GV[:, GB * g:GB * (g + 1), quad], start=True, stop=False)
                        last = mm(out, KV[:, quad], V8[:, GB * g:GB * (g + 1), quad], start=False, stop=True)
                    last.then_inc(s_k, 1)
                if not first:
                    rt_product(l, u, 1)
                for g in range(2):
                    pe.wait_ge(s_m, 2 * l + g + 1)
                    for b in range(GB):
                        o = (b % 2) * BQ
                        last = mm(bank(g, b // 2)[:, o:o + BQ], MF[:, GB * g + b, :], W[:, CQN:CQN + BQ], start=True, stop=True)
                    last.then_inc(s_b, 1)
                for g in range(2):
                    pe.wait_ge(s_bt, 2 * l + g + 1)
                    for b in range(GB):
                        last = mm(bank(g, 2)[:, b * C:(b + 1) * C], BT[:, GB * g + b, 0:C], W[:, CPT:CPT + C], start=True, stop=True)
                    last.then_inc(s_a, 1)
                for g in range(2):
                    n = GB * g
                    own = BT[:].rearrange("p b c -> p (b c)")[:, n * BQ + C + n::BQ + 1][:, 0:GB]
                    mm(bank(g, 0)[:, 0:GB], W[:, CPT:CPT + C], own, start=True, stop=True).then_inc(s_ym, 1)
                if final:
                    return
                for g in range(2):
                    pe.wait_ge(s_ia, 2 * l + g + 1)
                    pe.wait_ge(s_rt, 2 * l + g + 1)
                    for b in range(GB):
                        n = GB * g + b
                        last = mm(bank(g, 3)[:, b * C:(b + 1) * C], G[:, n, :], IA[:, u, n, :], start=True, stop=True)
                    last.then_inc(s_u, 1)
                for g in range(2):
                    pe.wait_ge(s_uc, 2 * l + g + 1)
                    for b in range(GB):
                        n = GB * g + b
                        last = mm(bank(g, 1)[:, b * C:(b + 1) * C], IA[:, u, n, :], U[:, n, :], start=True, stop=True)
                    last.then_inc(s_gd, 1)

            pe_layer(0, 0, first=True)
            pe_layer(0, 1)
            with pe.Fori(0, L // 2 - 2) as i:
                for u in range(2):
                    pe_layer(i + 1, u)
            pe_layer(L // 2 - 1, 0)
            pe_layer(L // 2 - 1, 1, final=True)
            for g in range(2):
                pe.wait_ge(s_rt, 2 * (L - 1) + g + 1)
                pe.wait_ge(s_ia, 2 * (L - 1) + g + 1)
                for b in range(GB):
                    n = GB * g + b
                    last = mm(bank(g, 3)[:, b * C:(b + 1) * C], RT[:, n, :], IA[:, 1, n, :], start=True, stop=True)
                last.then_inc(s_r, 1)

            pe.wait_ge(s_ir, 2)
            def residual_done(i):
                for b in (2 * i, 2 * i + 1):
                    last = mm(PS[:, i, (b % 2) * T:(b % 2 + 1) * T], IR[:, b, :], XT[:, b, :], start=True, stop=True)
                last.then_inc(s_h, 1)

            def residual_turned(i):
                pe.wait_ge((s_htv, s_hta)[i % 2], i // 2 + 1)
                for k in range(4):
                    last = nc.tensor.transpose(PS[:, 4 + i, k * P:(k + 1) * P], HT[:, 4 * i + k, :], IDN[:])
                last.then_inc(s_tok, 1)

            residual_done(0)
            residual_done(1)
            residual_turned(0)
            residual_done(2)
            residual_turned(1)
            residual_done(3)
            residual_turned(2)
            residual_turned(3)

            def turn_x1(i):
                pe.wait_ge(s_x1[i % 2], i // 2 + 1)
                for k in range(4):
                    last = nc.tensor.transpose(PS[:, i, k * P:(k + 1) * P], XN[:, 4 * i + k, :], IDN[:])
                last.then_inc(s_x1t, 1)

            pe.wait_ge(s_wf, 16 * 7)
            turn_x1(0)
            def project(w, bank_, i, done):
                pe.wait_ge(s_xtc, i + 1)
                mm(PS[:, bank_ + i, :], WEIGHT[w][:], XTF[:, cols(i)], start=True, stop=True).then_inc(done, 1)

            queries = lambda i: project("qw", 4, i, s_q)
            keys = lambda i: project("kw", 0, i, s_kd)

            def query_scale(i):
                pe.wait_ge(s_qf, i + 1)
                mm(PS[:, 4 + i, :], SWB[:], flat(QF)[:, cols(i)], start=True, stop=True).then_inc(s_z, 1)

            queries(0)
            turn_x1(1)
            keys(0)
            turn_x1(2)
            queries(1)
            turn_x1(3)
            pe.wait_ge(s_swb, 1)
            query_scale(0)
            keys(1)
            query_scale(1)
            queries(2)
            keys(2)
            queries(3)
            query_scale(2)
            keys(3)
            query_scale(3)
            for i in range(4):
                pe.wait_ge(s_kf, i + 1)
                for k in range(4):
                    last = mm(PS[:, i, k * P:(k + 1) * P], XTF[:, (4 * i + k) * P:(4 * i + k + 1) * P], WEIGHT["vw"][:], start=True, stop=True)
                last.then_inc(s_v, 1)

            def max_scores(M, j, slot, loaded):
                pe.wait_ge(s_stk[slot], 144 * loaded)
                if M is not None:
                    pe.wait_ge(s_max, M - 1)
                for k in range(4):
                    h = 4 * (j // 2) + k
                    last = mm(PS[:, 2 * (j % 2) + k // 2, (k % 2) * T:(k % 2 + 1) * T],
                              QS[0:KMAX, slot, h, (j % 2) * P:(j % 2 + 1) * P], KS[0:KMAX, slot, h, :], start=True, stop=True)
                last.then_inc(s_mxd, 1)

            def shift_rows(n, half, slot):
                pe.wait_ge(s_max, 8 * n + 4 * half + 4)
                nm = NM[:, slot, half * H // 2:(half + 1) * H // 2, :].rearrange("p h q -> p (h q)")
                nc.tensor.transpose(PS[0:H, 7, 0:P], nm, IDN[:]).then_inc(s_mt, 1)

            def pv(b, j, slot, first):
                if j == 0:
                    pe.wait_ge(s_vs, b + 1)
                pe.wait_ge(s_exp, 16 * b + 2 * j + 2)
                if j % 2 == 0 and not (first and j == 0):
                    pe.wait_ge(s_ot, 4 * b + j // 2)
                for k in range(4):
                    last = mm(PS[QW * k:QW * (k + 1), 6, 0:T], VS[:, slot, j % 2, 4 * (j // 2) + k, :],
                              PT[:, (2 * j + k // 2) % 4, k % 2, :], start=j % 2 == 0, stop=j % 2 == 1)
                last.then_inc(s_pv, 1)

            def out_tokens(b, qt, slot):
                pe.wait_ge(s_ot, 4 * b + 4)
                for g in range(Q4):
                    last = nc.tensor.transpose(PS[:, 7, g * P:(g + 1) * P], OTS[:, slot, g, qt * P:(qt + 1) * P], IDN[:])
                last.then_inc(s_tr, 1)

            pe.wait_ge(s_vt, 4)
            for j in range(8):
                max_scores(j if j > 1 else None, j, 0, 1)
                if j == 4:
                    shift_rows(0, 0, 0)
            pe.wait_ge(s_shb, 1)
            shift_rows(0, 1, 0)
            for j in range(2):
                max_scores(8 + j, j, 1, 1)

            def outputs_turned(i):
                pe.wait_ge(s_max, 66)
                pe.wait_ge(s_on, 4 * i + 4)
                for k in range(4):
                    last = nc.tensor.transpose(PS[:, i, k * P:(k + 1) * P], ON[:, 4 * i + k, :], IDN[:])
                last.then_inc(s_ott, 1)

            def gate(i):
                pe.wait_ge(s_otc, i + 1)
                mm(PS[:, i, :], WEIGHT["gw"][:], flat(OT)[:, cols(i)], start=True, stop=True).then_inc(s_gt, 1)

            def out_projection(i):
                pe.wait_ge(s_og, i + 1)
                for k in range(4):
                    last = mm(PS[:, i, k * P:(k + 1) * P], OT[:, 4 * i + k, :], WEIGHT["ow"][:], start=True, stop=True)
                last.then_inc(s_at, 1)

            def x2_turned(i):
                pe.wait_ge(s_x2, i + 1)
                for k in range(4):
                    last = nc.tensor.transpose(PS[:, i, k * P:(k + 1) * P], X2[:, 4 * i + k, :], IDN[:])
                last.then_inc(s_x2t, 1)

            def logits(i):
                pe.wait_ge(s_x2c, i + 1)
                for n in range(4 * i, 4 * i + 4):
                    last = mm(PS[:, 5, n * E:(n + 1) * E], X2T[:, n * P:(n + 1) * P], MG[:], start=True, stop=True)
                last.then_inc(s_lg, 1)

            def pe_step(i, c, first=False, last=False):
                b, r = NSLOT * i + c, c % NSLOT
                for j in range(8):
                    if not last:
                        a = c + (1 if j < 6 else 2)
                        max_scores(8 * b + j + 10, (j + 2) % 8, a % NSLOT, i + a // NSLOT + 1)
                    if j % 4 == 0:
                        pe.wait_ge(s_shl[j // 4], 16 * b + 16)
                    for k in (0, 1):
                        if not (first and j == 0):
                            pe.wait_ge(s_exp, 16 * b + 2 * j + k - 1)
                        for hh in (0, 1):
                            h = 4 * (j // 2) + 2 * k + hh
                            o = mm(PS[:, 4 + k, hh * T:(hh + 1) * T], KS[0:KEXP, r, h, (j % 2) * P:(j % 2 + 1) * P],
                                   QS[0:KEXP, r, h, :], start=True, stop=True)
                        o.then_inc(s_qk, 1)
                    if j > 0:
                        pv(b, j - 1, r, first)
                    elif not first:
                        pv(b - 1, 7, (c - 1) % NSLOT, False)
                    if j == 2 and not last:
                        pe.wait_ge(s_shb, 2 * b + 2)
                        shift_rows(b + 1, 0, (c + 1) % NSLOT)
                    if j == 3 and not first:
                        pe.wait_ge(s_shb, 16 if last else 2 * b + 3)
                        out_tokens(b - 1, 0, (c - 1) % NSLOT)
                    if j == 5 and not first:
                        pe.wait_ge(s_on, 2 * b - 1)
                        out_tokens(b - 1, 1, (c - 1) % NSLOT)
                    if j == 6 and not last:
                        if first:
                            pe.wait_ge(s_shb, 3)
                        else:
                            pe.wait_ge(s_on, 2 * b)
                        shift_rows(b + 1, 1, (c + 1) % NSLOT)
                    if last:
                        if j < 3:
                            outputs_turned(j)
                        if 2 <= j < 5:
                            gate(j - 2)
                        if j > 5:
                            out_projection(j - 6)

            pe_step(0, 0, first=True)
            with pe.Fori(0, 2) as i:
                for u in range(3):
                    pe_step(i, 1 + u)
            pe_step(0, 7, last=True)
            pv(7, 7, 7 % NSLOT, False)
            out_projection(2)
            for qt in range(TT):
                pe.wait_ge(s_on, 14 + qt)
                out_tokens(7, qt, 7 % NSLOT)
            outputs_turned(3)
            pe.wait_ge(s_we, 16 * 7)
            x2_turned(0)
            gate(3)
            x2_turned(1)
            out_projection(3)
            logits(0)
            logits(1)
            x2_turned(2)
            logits(2)
            x2_turned(3)
            logits(3)

            pe.wait_ge(s_sc, 32)
            pe.wait_ge(s_oh, 1)
            rank = PS[:, 1, 0:(NT + 1) * E].rearrange("p (n e) -> p n e", e=E)
            mm(rank, UNIT[:, 0], OH, start=True, stop=False)
            pe.wait_ge(s_pre, 4)
            mm(rank, UNIT[:, 1], SUMS[1][:, NT // 2 - 1:], start=False, stop=True).then_inc(s_rk, 1)

            def turn_x(h, u):
                pe.wait_ge(s_xs[u], 16 * h + 16)
                for k in range(2):
                    last = nc.tensor.transpose(PS[:, 4 + u, k * P:(k + 1) * P], XS[:, u, k], IDN[:])
                last.then_inc(s_xst, 1)

            def hidden(m, u, x):
                pe.wait_ge(s_xsc, m + 1)
                for k in range(2):
                    out = PS[:, u, k * F:(k + 1) * F]
                    mm(out, ONE3[:], B1P[:, bass.ds(x[k] * F, F)], start=True, stop=False)
                    last = mm(out, XST[:, u, k * P:(k + 1) * P], W1[:, bass.ds(x[k], 1), :].rearrange("p o f -> p (o f)"),
                              start=False, stop=True)
                last.then_inc(s_h1, 1)

            def turn_hidden(m, u):
                pe.wait_ge(s_nrm, m + 1)
                for c in range(FC):
                    for k in range(2):
                        last = nc.tensor.transpose(PS[:, 2 + u, (2 * c + k) * P:(2 * c + k + 1) * P], HN[:, u, k, c * P:(c + 1) * P], IDN[:])
                last.then_inc(s_td, 1)

            def output(m, u, x):
                pe.wait_ge(s_gl, m + 1)
                for k in range(2):
                    out = PS[:, 6 + u, k * C:(k + 1) * C]
                    mm(out, ONE3[:], B2P[:, bass.ds(x[k] * C, C)], start=True, stop=False)
                    for c in range(FC):
                        last = mm(out, GT[:, u, c, k * P:(k + 1) * P], W2[:, bass.ds(x[k], 1), c, :].rearrange("p o c -> p (o c)"),
                                  start=False, stop=c == FC - 1)
                last.then_inc(s_y, 1)

            pe.wait_ge(s_zb, 18)
            pe.wait_ge(s_te, 1)
            x = tile_experts(mybir.EngineType.PE, 0, 4)
            turn_x(0, 0)
            turn_x(0, 1)
            hidden(0, 0, x[0:2])
            turn_x(1, 0)
            hidden(1, 1, x[2:4])
            turn_hidden(0, 0)
            with pe.Fori(0, NPAIR // 2 - 1) as i:
                x = tile_experts(mybir.EngineType.PE, 4 * i, 8)
                for u in range(2):
                    m = 2 * i + u
                    turn_x(i + 1 + u, 1 - u)
                    hidden(m + 2, u, x[4 + 2 * u:6 + 2 * u])
                    turn_hidden(m + 1, 1 - u)
                    output(m, u, x[2 * u:2 * u + 2])
            m = NPAIR - 3
            x = tile_experts(mybir.EngineType.PE, 2 * m, 6)
            hidden(m + 2, 0, x[4:6])
            turn_hidden(m + 1, 1)
            output(m, 0, x[0:2])
            turn_hidden(m + 2, 0)
            output(m + 1, 1, x[2:4])
            output(m + 2, 0, x[4:6])

        @block.scalar
        def _(act):
            copy = lambda out, in_: nc.scalar.activation(out, in_, ACT.Copy)
            for i, (g, k) in enumerate(((0, 3), (1, 3), (0, 0), (1, 0))):
                act.wait_ge(s_xct, i + 1)
                copy(XT[:, 2 * i:2 * i + 2, :], bank(g, k).rearrange("p (b t) -> p b t", b=2)).then_inc(s_xt, 1)
            act.wait_ge(s_zero, 5)
            nc.scalar.copy(MSUM[:, 0:1], IDN[:, 0:1]).then_inc(s_rt, 1)
            nc.scalar.copy(MSUM[:, 1:2], IDN[:, 0:1]).then_inc(s_rt, 1)
            def act_layer(i, u, first=False, final=False):
                l = 2 * i + u
                for g in range(2):
                    act.wait_ge(s_p, 2 * l + g + 1)
                    copy(GV[:, GB * g:GB * (g + 1), :], batches(bank(g, 0))).then_inc(s_pc, 1)
                for g in range(0 if first else 2):
                    act.wait_ge(s_r, 2 * l + g - 1)
                    copy(RT[:, GB * g:GB * (g + 1), :], batches(bank(g, 3))).then_inc(s_rt, 1)
                for g in range(2):
                    act.wait_ge(s_b, 2 * l + g + 1)
                    copy(BT[:, GB * g:GB * (g + 1), :].rearrange("p (k b) c -> p k (b c)", k=2),
                         PS[:, 4 * g:4 * g + 2, 0:2 * BQ]).then_inc(s_bt, 1)
                for g in range(0 if final else 2):
                    act.wait_ge(s_u, 2 * l + g + 1)
                    copy(U[:, GB * g:GB * (g + 1), :], batches(bank(g, 3))).then_inc(s_uc, 1)

            act_layer(0, 0, first=True)
            act_layer(0, 1)
            with act.Fori(0, L // 2 - 2) as i:
                for u in range(2):
                    act_layer(i + 1, u)
            act_layer(L // 2 - 1, 0)
            act_layer(L // 2 - 1, 1, final=True)
            act.wait_ge(s_ms, 1)
            for i in (1, 3):
                act.wait_ge(s_h, i + 1)
                for b in (2 * i, 2 * i + 1):
                    o = nc.scalar.activation(flat(HT)[:, b * T:(b + 1) * T], PS[:, i, (b % 2) * T:(b % 2 + 1) * T],
                                             ACT.Identity, bias=MSUM[:, b:b + 1])
                o.then_inc(s_hta, 1)
            for i in (1, 3):
                act.wait_ge(s_x1t, i)
                copy(XTF[:, cols(i - 1)], PS[:, i - 1, :]).then_inc(s_xtc, 1)
                act.wait_ge(s_nb, i // 2 + 1)
                for k in range(4):
                    n = 4 * i + k
                    o = nc.scalar.activation(XN[:, n, :], PS[:, 4 + i, k * P:(k + 1) * P], ACT.Identity,
                                             scale=RS[:, n:n + 1], bias=NB[:, n:n + 1])
                o.then_inc(s_x1[1], 1)
                act.wait_ge(s_x1t, i + 1)
                copy(XTF[:, cols(i)], PS[:, i, :]).then_inc(s_xtc, 1)
            def keys_scaled(i):
                act.wait_ge(s_kd, i + 1)
                nc.scalar.activation(flat(KF)[:, cols(i)], PS[:, i, :], ACT.Copy, scale=SCALE).then_inc(s_kf, 1)
                act.wait_ge(s_kf, i + 1)
                copy(KP[:, 0, cols(i)], flat(KF)[:, cols(i)]).then_inc(s_k1, 1)

            def tanh_scale(i):
                act.wait_ge(s_z, i + 1)
                nc.scalar.activation(flat(TH[:])[:, cols(i)], PS[:, 4 + i, :], ACT.Tanh, scale=0.5).then_inc(s_th, 1)

            def key_part_2(i):
                act.wait_ge(s_k1r, i + 1)
                copy(KP[:, 1, cols(i)], flat(KF)[:, cols(i)]).then_inc(s_k2, 1)

            def query_part_1(i):
                act.wait_ge(s_qs, i + 1)
                copy(QP[:, 0, cols(i)], flat(QF)[:, cols(i)]).then_inc(s_q1, 1)

            def query_part_2(i):
                act.wait_ge(s_q1r, i + 1)
                copy(QP[:, 1, cols(i)], flat(QF)[:, cols(i)]).then_inc(s_q2, 1)

            keys_scaled(0)
            tanh_scale(0)
            key_part_2(0)
            query_part_1(0)
            keys_scaled(1)
            query_part_2(0)
            tanh_scale(1)
            keys_scaled(2)
            for i in range(1, 4):
                key_part_2(i)
                query_part_1(i)
                if i < 3:
                    tanh_scale(i + 1)
                query_part_2(i)
                if i == 1:
                    keys_scaled(3)

            def copy_out(b, g, slot):
                act.wait_ge(s_pv, 8 * b + 2 * g + 2)
                copy(OTS[:, slot, g, :], PS[:, 6, 0:T]).then_inc(s_ot, 1)

            def gate_tanh(i):
                if i == 0:
                    act.wait_ge(s_gbh, 1)
                act.wait_ge(s_gt, i + 1)
                nc.scalar.activation(flat(TH[:])[:, cols(i)], PS[:, i, :], ACT.Tanh, scale=0.5, bias=GBH[:, 1:2]).then_inc(s_tg, 1)

            def x2t_copied(i):
                act.wait_ge(s_x2t, i + 1)
                copy(X2T[:, cols(i)], PS[:, i, :]).then_inc(s_x2c, 1)

            def act_step(i, c, first=False, last=False):
                b, r = NSLOT * i + c, c % NSLOT
                for j in range(8):
                    for k in (0, 1):
                        act.wait_ge(s_qk, 16 * b + 2 * j + k + 1)
                        if not (first and j < 2):
                            act.wait_ge(s_pv, 8 * b + j - 1)
                        nc.scalar.activation(PT[:, (2 * j + k) % 4], PS[:, 4 + k, :].rearrange("p (h t) -> p h t", h=2),
                                             ACT.Exp).then_inc(s_exp, 1)
                    if j % 2 == 0 and j > 0:
                        copy_out(b, j // 2 - 1, r)
                    elif j == 0 and not first:
                        copy_out(b - 1, 3, (c - 1) % NSLOT)
                    if last and 3 <= j < 6:
                        gate_tanh(j - 3)

            act_step(0, 0, first=True)
            with act.Fori(0, 2) as i:
                for u in range(3):
                    act_step(i, 1 + u)
            act_step(0, 7, last=True)
            copy_out(7, 3, 7 % NSLOT)
            x2t_copied(0)
            gate_tanh(3)
            for i in range(1, 4):
                x2t_copied(i)
            act.wait_ge(s_rch, 14)
            nc.scalar.activation(R1[5][:], R1[4][:], ACT.Exp).then_inc(s_ed, 1)

            def gelu(m, u, x):
                alone(act, s_td, m + 1)
                for k in range(2):
                    for c in range(FC):
                        o = nc.scalar.activation(GT[:, u, c, k * P:(k + 1) * P], PS[:, 2 + u, (2 * c + k) * P:(2 * c + k + 1) * P], ACT.Gelu,
                                                 scale=LNW[:, 0, c, bass.ds(x[k], 1)], bias=LNW[:, 1, c, bass.ds(x[k], 1)])
                o.then_inc(s_gl, 1)

            def copy_output(h, u, m):
                act.wait_ge(s_ys[u], 16 * h + 16)
                act.wait_ge(s_y, m + 1)
                copy(YS[:, u].rearrange("p k c -> p (k c)"), PS[:, 6 + u, 0:2 * C]).then_inc(s_yc, 1)

            for u in range(2):
                nc.scalar.copy(RC[:, u, 0:1], IDN[:, 0:1]).then_inc(s_ys[u], 16)
            nc.scalar.activation(RC[:, 1, 1:2], IDN[:, 0:1], ACT.Gelu)
            act.wait_ge(s_te, 1)
            gelu(0, 0, tile_experts(mybir.EngineType.Activation, 0, 2))
            with act.Fori(0, NPAIR // 2) as i:
                x = tile_experts(mybir.EngineType.Activation, 4 * i, 8)
                for u in range(2):
                    m = 2 * i + 1 + u
                    gelu(m, 1 - u, x[2 + 2 * u:4 + 2 * u])
                    copy_output(i, u, m - 1)
            copy_output(NPAIR // 2, 0, NPAIR - 1)
            for i in range(4):
                act.wait_ge(s_nb, 2 + i + 1)
                for n in range(4 * i, 4 * i + 4):
                    o = nc.scalar.activation(ACC[:, n, :], ACC[:, n, :], ACT.Identity, scale=RS[:, n:n + 1], bias=NB[:, n:n + 1])
                o.then_inc(s_fo, 1)

        @block.vector
        def _(dve):
            tt = nc.vector.tensor_tensor
            for g in range(2):
                dve.wait_ge(s_mrow, g + 1)
                for t in range(TT):
                    xg = X[:, GB * g:GB * (g + 1), t, :]
                    if t == 0:
                        dve.wait_ge(s_mcol, g + 1)
                    tt(xg, xg, batches(bank(g, 0)), ALU.subtract).then_inc(s_xc, 1)
            for M, done in ((MEAN0, s_zero), (MEAN, s_mean)):
                for g in range(2):
                    o = nc.vector.tensor_copy(M[:, GB * g:GB * (g + 1)], bank(g, 1)[:, 0:GB])
                o.then_inc(done, 1)
            for g in range(2):
                dve.wait_ge(s_gram, g + 1)
                nc.vector.tensor_copy(G[:, GB * g:GB * (g + 1), :], batches(bank(g, 2))).then_inc(s_g, 1)
            dve.wait_ge(s_zero, 5)

            def dve_layer(i, u, first=False, final=False):
                l = 2 * i + u
                dve.wait_ge(s_row, l + 1)
                tt(KV[0:B, :], bank(0, 3)[0:B, 0:2 * C], BR[:, u, :], ALU.add).then_inc(s_kv, 1)
                dve.wait_ge(s_qbd, l + 1)
                nc.vector.tensor_scalar(WL[:, u, CQB:CQB + B], bank(1, 3)[:, 0:B], WL[:, u, CBQ:CBQ + 1], None, ALU.add).then_inc(s_qb, 1)
                dve.wait_ge(s_kv, l + 1)
                for g in range(2):
                    tt(V8[0:B, GB * g:GB * (g + 1)], KV[0:B, C:].unsqueeze(1).broadcast_to([B, GB, C]),
                       DIAG[:, GB * g:GB * (g + 1)].unsqueeze(2).broadcast_to([B, GB, C]), ALU.mult).then_inc(s_v8, 1)
                for g in range(2):
                    dve.wait_ge(s_k, 2 * l + g + 1)
                    tt(MF[:, GB * g:GB * (g + 1), :].rearrange("p b (q j) -> p b q j", q=Q4),
                       bank(g, 2)[:, 0:GB * QW].rearrange("p (b j) -> p b j", b=GB).unsqueeze(2).broadcast_to([P, GB, Q4, QW]),
                       MASK[:].unsqueeze(1).broadcast_to([P, GB, Q4, QW]), ALU.mult).then_inc(s_m, 1)
                for g in range(2):
                    dve.wait_ge(s_a, 2 * l + g + 1)
                    tt(IA[:, u, GB * g:GB * (g + 1), :], batches(bank(g, 2)),
                       IDN[:].unsqueeze(1).broadcast_to([P, GB, C]), ALU.add).then_inc(s_ia, 1)
                for g in range(2):
                    dve.wait_ge(s_ym, 2 * l + g + 1)
                    m = MEAN[:, GB * g:GB * (g + 1)]
                    o = nc.vector.scalar_tensor_tensor(m, bank(g, 0)[:, 0:GB], WL[:, u, CBP:CBP + 1], m, ALU.add, ALU.add)
                o.then_inc(s_mean, 1)
                for g in range(0 if final else 2):
                    dve.wait_ge(s_gd, 2 * l + g + 1)
                    nc.vector.tensor_copy(G[:, GB * g:GB * (g + 1), :], batches(bank(g, 1))).then_inc(s_g, 1)

            dve_layer(0, 0, first=True)
            dve_layer(0, 1)
            with dve.Fori(0, L // 2 - 2) as i:
                for u in range(2):
                    dve_layer(i + 1, u)
            dve_layer(L // 2 - 1, 0)
            dve_layer(L // 2 - 1, 1, final=True)
            for g in range(2):
                dve.wait_ge(s_r, 2 * (L - 1) + g + 1)
                tt(IR[:, GB * g:GB * (g + 1), :], batches(bank(g, 3)),
                   IDN[:].unsqueeze(1).broadcast_to([P, GB, C]), ALU.add).then_inc(s_ir, 1)
            dve.wait_ge(s_mean, L + 1)
            tt(MSUM[:], MEAN[:], MEAN0[:], ALU.add).then_inc(s_ms, 1)
            dve.wait_ge(s_ms, 1)
            def residual_copied(i):
                dve.wait_ge(s_h, i + 1)
                for b in (2 * i, 2 * i + 1):
                    o = nc.vector.tensor_scalar(flat(HT)[:, b * T:(b + 1) * T], PS[:, i, (b % 2) * T:(b % 2 + 1) * T],
                                                MSUM[:, b:b + 1], None, ALU.add)
                o.then_inc(s_htv, 1)

            residual_copied(0)
            dve.wait_ge(s_wf, 16 * 7)
            nc.vector.tensor_scalar(SWB[:], EM[:], SWC[:, 0:1], None, ALU.mult).then_inc(s_swb, 1)

            def statistics(src, i, k0):
                for k in range(4):
                    o = nc.vector.bn_stats(ST[:, 4 * i + k, :], src(k))
                o.then_inc(s_st, 1)
                dve.wait_ge(s_st, k0 + i + 1)
                for k in range(4):
                    o = nc.vector.bn_aggr(MV[:, 4 * i + k, :], ST[:, 4 * i + k, :])
                o.then_inc(s_mv, 1)

            for i in range(4):
                dve.wait_ge(s_tok, i + 1)
                statistics(lambda k: PS[:, 4 + i, k * P:(k + 1) * P], i, 0)
                if i == 0:
                    residual_copied(2)
                if i in (1, 3):
                    j = i - 1
                    dve.wait_ge(s_rs, j + 1)
                    for k in range(4):
                        n = 4 * j + k
                        o = nc.vector.tensor_scalar(XN[:, n, :], PS[:, 4 + j, k * P:(k + 1) * P], MV[:, n, 0:1], RS[:, n:n + 1],
                                                    ALU.subtract, ALU.mult)
                    o.then_inc(s_x1[0], 1)
            def queries_copied(i):
                dve.wait_ge(s_q, i + 1)
                nc.vector.tensor_copy(flat(QF)[:, cols(i)], PS[:, 4 + i, :]).then_inc(s_qf, 1)

            def queries_scaled(i):
                q = flat(QF)[:, cols(i)]
                dve.wait_ge(s_th, i + 1)
                nc.vector.scalar_tensor_tensor(q, flat(TH[:])[:, cols(i)], 1.0, q, ALU.add, ALU.mult).then_inc(s_qs, 1)

            def query_rest_1(i):
                q = flat(QF)[:, cols(i)]
                dve.wait_ge(s_q1, i + 1)
                tt(q, q, QP[:, 0, cols(i)], ALU.subtract).then_inc(s_q1r, 1)

            def query_part_3(i):
                dve.wait_ge(s_q2, i + 1)
                tt(QP[:, 2, cols(i)], flat(QF)[:, cols(i)], QP[:, 1, cols(i)], ALU.subtract).then_inc(s_q3, 1)

            queries_copied(0)
            queries_copied(1)
            queries_scaled(0)
            query_rest_1(0)
            query_part_3(0)
            queries_copied(2)
            queries_copied(3)
            def values_copied(i):
                dve.wait_ge(s_v, i + 1)
                nc.vector.tensor_copy(VT[:, 4 * i:4 * i + 4].rearrange("p n h d -> p (n h d)"), PS[:, i, :]).then_inc(s_vt, 1)

            for i in range(1, 4):
                queries_scaled(i)
                if i > 1:
                    values_copied(2 * i - 4)
                query_rest_1(i)
                if i > 1:
                    values_copied(2 * i - 3)
                query_part_3(i)

            def take_max(M, j, slot):
                dve.wait_ge(s_mxd, M + 1)
                g = 4 * (j // 2)
                nc.vector.tensor_reduce(NM[:, slot, g:g + 4, j % 2],
                                        PS[:, 2 * (j % 2):2 * (j % 2) + 2, :].rearrange("p k (h t) -> p (k h) t", h=2),
                                        AX.X, ALU.max, negate=True).then_inc(s_max, 1)

            def shift_part(n, half, first=False):
                m = 2 * n + half
                dve.wait_ge(s_mt, m + 1)
                if not first:
                    dve.wait_ge(s_shs[half], 16 * n)
                nc.vector.tensor_copy(SH[:, half, 0], PS[0:H, 7, 0:P]).then_inc(s_sha, 1)
                dve.wait_ge(s_sha, m + 1)
                tt(SHF[:, half], PS[0:H, 7, 0:P], SH[:, half, 0], ALU.subtract).then_inc(s_shb, 1)

            def normalise(b, qt):
                dve.wait_ge(s_tr, 2 * b + qt + 1)
                o = PS[:, 7, :].rearrange("p (h d) -> p h d", d=QW)
                nc.vector.reciprocal(RC[:, qt, :], o[:, :, HD]).then_inc(s_rc, 1)
                dve.wait_ge(s_rc, 2 * b + qt + 1)
                tt(ON[:, bass.ds(2 * b + qt, 1), :].rearrange("p o (h d) -> p (o h) d", d=HD), o[:, :, 0:HD],
                   RC[:, qt, :].unsqueeze(2).broadcast_to([P, H, HD]), ALU.mult).then_inc(s_on, 1)

            for j in range(8):
                take_max(j, j, 0)
                if j == 4:
                    shift_part(0, 0, True)
            shift_part(0, 1, True)
            for j in range(2):
                take_max(8 + j, j, 1)

            quad = lambda ap, i: ap[:, 4 * i:4 * i + 4, :]
            stt = nc.vector.scalar_tensor_tensor

            def outputs_copied(i):
                dve.wait_ge(s_ott, i + 1)
                nc.vector.tensor_copy(flat(OT)[:, cols(i)], PS[:, i, :]).then_inc(s_otc, 1)

            def outputs_gated(i):
                dve.wait_ge(s_tg, i + 1)
                o = flat(OT)[:, cols(i)]
                stt(o, flat(TH[:])[:, cols(i)], 1.0, o, ALU.add, ALU.mult).then_inc(s_og, 1)

            def residual(i):
                dve.wait_ge(s_at, i + 1)
                stt(quad(X2, i), PS[:, i, :].rearrange("p (k c) -> p k c", k=4), 0.5, quad(XN, i), ALU.mult, ALU.add).then_inc(s_xp, 1)
                dve.wait_ge(s_xp, i + 1)
                statistics(lambda k: X2[:, 4 * i + k, :], i, 4)

            def x2_norm(i):
                dve.wait_ge(s_mv, 4 + i + 1)
                for n in range(4 * i, 4 * i + 4):
                    o = stt(X2[:, n, :], X2[:, n, :], MV[:, n, 0:1], ROWS[:, 0, :], ALU.subtract, ALU.mult)
                o.then_inc(s_xn, 1)
                dve.wait_ge(s_xn, i + 1)
                dve.wait_ge(s_rs, 4 + i + 1)
                for n in range(4 * i, 4 * i + 4):
                    o = stt(X2[:, n, :], X2[:, n, :], RS[:, n:n + 1], ROWS[:, 1, :], ALU.mult, ALU.add)
                o.then_inc(s_x2, 1)

            def dve_step(i, c, first=False, last=False):
                b = NSLOT * i + c
                for j in range(8):
                    if not last:
                        take_max(8 * b + j + 10, (j + 2) % 8, (c + (1 if j < 6 else 2)) % NSLOT)
                    if j == 2 and not last:
                        shift_part(b + 1, 0)
                    if j == 3 and not first:
                        normalise(b - 1, 0)
                    if j == 5 and not first:
                        normalise(b - 1, 1)
                    if j == 6 and not last:
                        shift_part(b + 1, 1)
                    if last:
                        if j < 3:
                            outputs_copied(j)
                        if j > 4:
                            outputs_gated(j - 5)
                        if j == 7:
                            residual(0)

            dve_step(0, 0, first=True)
            with dve.Fori(0, 2) as i:
                for u in range(3):
                    dve_step(i, 1 + u)
            dve.wait_ge(s_we, 16 * 7)
            nc.vector.tensor_scalar(GBH[:, 1:2], GBH[:, 0:1], 0.5, None, ALU.mult).then_inc(s_gbh, 1)
            dve_step(0, 7, last=True)
            normalise(7, 0)
            residual(1)
            normalise(7, 1)
            outputs_copied(3)
            x2_norm(0)
            residual(2)
            x2_norm(1)
            outputs_gated(3)
            x2_norm(2)
            residual(3)
            x2_norm(3)

            dve.wait_ge(s_vs, NSLOT + 6)
            chain = [0]

            def link(ins):
                chain[0] += 1
                ins.then_inc(s_rch, 1)
                dve.wait_ge(s_rch, chain[0])

            per = lambda a: a[:].unsqueeze(2).broadcast_to([P, NT, E])
            each = lambda r: ER[:, r, :].unsqueeze(1).broadcast_to([P, NT, E])
            lg, t8, l2 = (a[:] for a in RT8)
            top1, key1, top2, key2, diff, expd = R1
            red = lambda out, in_, op=ALU.max: nc.vector.tensor_reduce(out[:], in_, AX.X, op)
            for zeros in (SUMS[0][:, 0:NT // 2], SUMS[1][:, 0:NT // 2], OH[:, NT:]):
                nc.vector.memset(zeros, 0.0)
            dve.wait_ge(s_lg, 4)
            link(tt(lg, PS[:, 5, 0:NT * E].rearrange("p (n e) -> p n e", n=NT), each(0), ALU.add))
            link(red(top1, lg))
            link(tt(t8, lg, per(top1), ALU.is_equal))
            link(tt(t8, t8, each(2), ALU.mult))
            link(red(key1, t8))
            link(tt(t8, each(2), per(key1), ALU.is_equal))
            link(nc.vector.scalar_tensor_tensor(l2, t8, -3.0e38, lg, ALU.mult, ALU.add))
            link(red(top2, l2))
            link(tt(t8, l2, per(top2), ALU.is_equal))
            link(tt(t8, t8, each(2), ALU.mult))
            link(red(key2, t8))
            link(tt(key1[:], key1[:], key2[:], ALU.min))
            tt(OH[:, 0:NT], each(2), per(key1), ALU.is_equal).then_inc(s_oh, 1)
            link(tt(SUMS[1][:, NT // 2:], each(2), per(key1), ALU.is_equal))
            for r in range(4):
                a, b, back = SUMS[1 - r % 2], SUMS[r % 2], 1 << r
                tt(b[:, NT // 2:], a[:, NT // 2:], a[:, NT // 2 - back:NT // 2 + NT - back], ALU.add).then_inc(s_pre, 1)
                if r < 3:
                    dve.wait_ge(s_pre, r + 1)
            link(tt(diff[:], top2[:], top1[:], ALU.subtract))

            rank = PS[:, 1, 0:(NT + 1) * E].rearrange("p (n e) -> p n e", e=E)
            dve.wait_ge(s_rk, 1)
            link(tt(FULL, rank[:, NT, :].unsqueeze(2).broadcast_to([P, E, NT]), TILES, ALU.is_gt))
            link(red(NTILE, FULL, ALU.add))
            link(tt(BEFORE, LOWER, NTILE[:].unsqueeze(1).broadcast_to([P, E, E]), ALU.mult))
            link(red(START, BEFORE, ALU.add))
            link(stt(BASE, START[:].unsqueeze(1).broadcast_to([P, NT, E]), float(P), rank[:, 0:NT, :], ALU.mult, ALU.add))
            link(tt(BASE, BASE, OH[:, 0:NT], ALU.mult))
            link(red(SLOT, BASE, ALU.add))
            nc.vector.tensor_copy(SLOTI[:], SLOT[:]).then_inc(s_slot, 1)
            link(tt(LATER, TILE.unsqueeze(2).broadcast_to([P, NX, E - 2]), START[:, 2:E].unsqueeze(1).broadcast_to([P, NX, E - 2]), ALU.is_ge))
            link(red(TEXP, LATER, ALU.add))
            nc.vector.tensor_copy(TEXPI[:], TEXP[:]).then_inc(s_te, 1)
            link(tt(t8, OH[:, 0:NT], each(1), ALU.mult))
            link(red(RSC, t8, ALU.add))
            dve.wait_ge(s_ed, 1)
            link(nc.vector.tensor_scalar(key1[:], expd[:], 1.0, None, ALU.add))
            link(nc.vector.reciprocal(key2[:], key1[:]))
            link(tt(top1[:], expd[:], key2[:], ALU.mult))
            link(tt(WS[:], top1[:], key2[:], ALU.add))
            link(tt(SW[:], RSC[:], WS[:], ALU.mult))
            link(nc.vector.tensor_scalar(diff[:], WS[:], 1.0, None, ALU.add))
            for n in range(NT):
                o = nc.vector.tensor_scalar(TH[:, n, :], X2[:, n, :], diff[:, n:n + 1], None, ALU.mult)
            o.then_inc(s_wx, 1)

            def copy_x(m, u):
                dve.wait_ge(s_xst, m + 1)
                if not isinstance(m, int) or m > 1:
                    dve.wait_ge(s_h1, m + 1 - 2)
                nc.vector.tensor_copy(XST[:, u], PS[:, 4 + u, 0:2 * P]).then_inc(s_xsc, 1)

            def hidden_statistics(m, u):
                dve.wait_ge(s_h1, m + 1)
                for k in range(2):
                    o = nc.vector.bn_stats(ST2[:, u, k, :], PS[:, u, k * F:(k + 1) * F])
                o.then_inc(s_st2, 1)
                alone(dve, s_st2, m + 1)
                for k in range(2):
                    o = nc.vector.bn_aggr(MV2[:, u, k, :], ST2[:, u, k, :])
                o.then_inc(s_mv2, 1)

            def hidden_normalise(m, u):
                dve.wait_ge(s_rs2, m + 1)
                for k in range(2):
                    o = nc.vector.tensor_scalar(HN[:, u, k, :], PS[:, u, k * F:(k + 1) * F], MV2[:, u, k, 0:1], RS2[:, u, k:k + 1],
                                                ALU.subtract, ALU.mult)
                o.then_inc(s_nrm, 1)

            copy_x(0, 0)
            copy_x(1, 1)
            hidden_statistics(0, 0)
            copy_x(2, 0)
            hidden_normalise(0, 0)
            with dve.Fori(0, NPAIR // 2 - 1) as i:
                for u in range(2):
                    m = 2 * i + u
                    hidden_statistics(m + 1, 1 - u)
                    copy_x(m + 3, 1 - u)
                    hidden_normalise(m + 1, 1 - u)
            for m in (NPAIR - 2, NPAIR - 1):
                hidden_statistics(m, m % 2)
                hidden_normalise(m, m % 2)

            dve.wait_ge(s_xb, 1)
            dve.wait_ge(s_wx, 1)
            for k, (part, i) in enumerate(FINAL):
                four = range(4 * i, 4 * i + 4)
                if part == "expert":
                    dve.wait_ge(s_got[i], 64)
                    for n in four:
                        o = stt(ACC[:, n, :], ACC[:, n, :], SW[:, n:n + 1], TH[:, n, :], ALU.mult, ALU.add)
                    o.then_inc(s_f1, 1)
                    dve.wait_ge(s_f1, i + 1)
                    statistics(lambda t: ACC[:, 4 * i + t, :], i, 8 + k - i)
                    dve.wait_ge(s_mv, 8 + k + 1)
                    for n in four:
                        o = stt(ACC[:, n, :], ACC[:, n, :], MV[:, n, 0:1], ROWS[:, 2, :], ALU.subtract, ALU.mult)
                    o.then_inc(s_f2, 1)
                else:
                    dve.wait_ge(s_f2, i + 1)
                    dve.wait_ge(s_rs, 8 + FINAL.index(("expert", i)) + 1)
                    for n in four:
                        o = stt(ACC[:, n, :], ACC[:, n, :], RS[:, n:n + 1], XN[:, n, :], ALU.mult, ALU.add)
                    o.then_inc(s_f3, 1)
                    dve.wait_ge(s_f3, i + 1)
                    statistics(lambda t: ACC[:, 4 * i + t, :], i, 8 + k - i)


def host_consts():
    mask = np.zeros((P, Q4, QW), np.float32)
    for i in range(P):
        q = i // QW
        a = (i % QW) // HD * HD
        mask[i, q, a:a + HD] = SCALE
    return {"avg": np.full((P, P), 1.0 / T, np.float32), "ident": np.eye(P, dtype=np.float32), "mask": mask,
            "diag": (np.eye(B) * T).astype(np.float32),
            "alf": np.array([[0, 0], [-1, 0], [-1, -1]], np.float32),
            "unit": np.concatenate([np.triu(np.ones((P, P)), 1), np.ones((P, P))], axis=1).astype(np.float32),
            "slots": np.concatenate([np.tile(P * np.arange(NT), E), np.tril(np.ones((E, E)), -1).reshape(-1), np.arange(NX)])[None].astype(np.float32),
            "em": np.kron(np.eye(H), np.ones((HD, HD))).astype(np.float32)}


def layer_pack(Wqkv, bqkv, Wproj, bproj):
    t = lambda a: np.swapaxes(a, 1, 2)
    Wq, Wk, Wv = Wqkv[:, :C], Wqkv[:, C:2 * C], Wqkv[:, 2 * C:]
    lw = np.ascontiguousarray(np.concatenate([bqkv[:, :C, None], bproj[:, :, None], t(Wk), t(Wv), t(Wq), t(Wproj), Wq], axis=2))
    return lw, np.ascontiguousarray(bqkv[:, C:])


def kernel(**inputs):
    import concourse.bacc as bacc
    from concourse.bass_utils import run_bass_kernel_spmd

    a = {k.replace("L0_", ""): np.asarray(v) for k, v in inputs.items()}
    lw, lb = layer_pack(a["attn_Wqkv"], a["attn_bqkv"], a["attn_Wproj"], a["attn_bproj"])
    order = list(range(1, E)) + [0]
    col = lambda v: np.ascontiguousarray(v.reshape(-1, 1))
    by_unit = lambda v: v[order].reshape(E, FC, P).transpose(2, 1, 0)
    index = np.arange(E, 0, -1).astype(np.float32)
    arrays = {
        "x": a["attn_inputs_embeds"], "lw": lw, "lb": lb,
        "qw": a["ffn_q_w"], "kw": a["ffn_k_w"], "vw": a["ffn_v_w"], "ow": a["ffn_out_w"], "gw": a["ffn_gate_w"],
        "swc": col(a["ffn_scale_w"]), "gb": col(a["ffn_gate_b"]), "mg": a["ffn_moe_gate_w"],
        "rows": np.concatenate([a["ffn_n1_g"], a["ffn_n1_b"], a["ffn_n2_g"], a["ffn_n2_b"]])[None],
        "er": np.concatenate([a["ffn_moe_gate_b"], a["ffn_res_scale"], index])[None],
        "w1": a["ffn_w1"][order].transpose(1, 0, 2), "b1": a["ffn_b1"][order].reshape(1, -1),
        "w2": a["ffn_w2"][order].reshape(E, FC, P, C).transpose(2, 0, 1, 3), "b2": a["ffn_b2"][order].reshape(1, -1),
        "lnw": np.stack([by_unit(a["ffn_ln_g"]), by_unit(a["ffn_ln_b"])], axis=1),
        **host_consts(),
    }
    arrays = {f"in_{k}": np.ascontiguousarray(v) for k, v in arrays.items()}
    nc = bacc.Bacc("TRN2", target_bir_lowering=False, num_devices=1)
    aps = {k[3:]: nc.dram_tensor(k, v.shape, mybir.dt.from_np(v.dtype), kind="ExternalInput").ap() for k, v in arrays.items()}
    out = nc.dram_tensor("out", (B, T, C), fp32, kind="ExternalOutput").ap()
    build(nc, aps["x"], aps["lw"], aps["lb"], aps, aps, out)
    r = run_bass_kernel_spmd(nc, [arrays], core_ids=[0])
    return r.results[0]["out"]
```
